# Optimizing a Trainium2 kernel written in Bass

```python
import numpy as np
import jax
import jax.numpy as jnp

def _softmax(x, axis=-1):
    return jax.nn.softmax(x, axis=axis)

def _gelu(x):
    return jax.nn.gelu(x, approximate=True)

def _silu(x):
    return jax.nn.silu(x)

def _sigmoid(x):
    return jax.nn.sigmoid(x)

def _layernorm(x, axis=-1, eps=1e-05):
    m = jnp.mean(x, axis=axis, keepdims=True)
    v = jnp.var(x, axis=axis, keepdims=True)
    return (x - m) / jnp.sqrt(v + eps)

def _scatter_add(tgt, idx, src, axis=0):
    return tgt.at[idx].add(src)

def _segment_sum(src, seg, n):
    return jax.ops.segment_sum(src, seg, n)
kernel_name = 'mk_seq_postln_d2_jaxref_r8_927d2f'

def setup_inputs(seed: int=0):
    np.random.seed(seed)
    _w = jnp.asarray

    def _L0_attn_setup():
        import jax, jax.numpy as jnp
        import numpy as np
        N_HEADS = 16
        HEAD_DIM = 128
        ROPE_BASE = 10000.0

        def _apply_rope(x, start_pos):
            B, T, H, Dh = x.shape
            half = Dh // 2
            inv_freq = 1.0 / ROPE_BASE ** (jnp.arange(0, Dh, 2, dtype=jnp.float32) / Dh)
            pos = jnp.arange(T, dtype=jnp.float32) + start_pos
            ang = pos[:, None] * inv_freq[None, :]
            cos = jnp.cos(ang)[None, :, None, :].astype(x.dtype)
            sin = jnp.sin(ang)[None, :, None, :].astype(x.dtype)
            x1 = x[..., 0::2]
            x2 = x[..., 1::2]
            r1 = x1 * cos - x2 * sin
            r2 = x1 * sin + x2 * cos
            return jnp.stack([r1, r2], axis=-1).reshape(B, T, H, Dh)
        key = jax.random.key(seed)
        k0, k1, k2, k3, k4 = jax.random.split(key, 5)
        B, T, D = (2, 256, 256)
        d_lat = 128
        x = jax.random.normal(k0, (B, T, D), dtype=jnp.float32)
        wq = jax.random.normal(k1, (D, N_HEADS * HEAD_DIM), dtype=jnp.float32) / np.sqrt(D)
        w_down = jax.random.normal(k2, (D, d_lat), dtype=jnp.float32) / np.sqrt(D)
        w_up = jax.random.normal(k3, (d_lat, 2 * N_HEADS * HEAD_DIM), dtype=jnp.float32) / np.sqrt(d_lat)
        wo = jax.random.normal(k4, (N_HEADS * HEAD_DIM, D), dtype=jnp.float32) / np.sqrt(N_HEADS * HEAD_DIM)
        return {'x': x, 'wq': wq, 'w_down': w_down, 'w_up': w_up, 'wo': wo}
    _L0_attn_in = _L0_attn_setup()

    def _L0_ffn_setup():
        import jax, jax.numpy as jnp
        import numpy as np
        B, L, D = (2, 128, 256)
        E, TOP_K, RANK, DFF = (8, 2, 8, 688)

        def _lora(x, A, Bm, scale):
            return x @ A @ Bm * scale

        def _expert_lora(x, A, Bm, w, scale):
            xA = jnp.einsum('bld,edr->bler', x, A)
            xAB = jnp.einsum('bler,erd->bled', xA, Bm) * scale
            return (xAB * w).sum(axis=2)
        key = jax.random.key(seed)
        ks = jax.random.split(key, 18)
        r = lambda k, s, sc: jax.random.normal(k, s, dtype=jnp.float32) * sc
        inv_d = 1.0 / np.sqrt(D)
        inv_f = 1.0 / np.sqrt(DFF)
        return {'x': r(ks[0], (B, L, D), 1.0), 'W_router': r(ks[1], (D, E), inv_d), 'W_gate': r(ks[2], (D, DFF), inv_d), 'W_up': r(ks[3], (D, DFF), inv_d), 'W_down': r(ks[4], (DFF, D), inv_f), 'sA_gate': r(ks[5], (D, RANK), inv_d), 'sB_gate': r(ks[6], (RANK, DFF), 0.02), 'sA_up': r(ks[7], (D, RANK), inv_d), 'sB_up': r(ks[8], (RANK, DFF), 0.02), 'sA_down': r(ks[9], (DFF, RANK), inv_f), 'sB_down': r(ks[10], (RANK, D), 0.02), 'A_gate': r(ks[11], (E, D, RANK), inv_d), 'B_gate': r(ks[12], (E, RANK, DFF), 0.02), 'A_up': r(ks[13], (E, D, RANK), inv_d), 'B_up': r(ks[14], (E, RANK, DFF), 0.02), 'A_down': r(ks[15], (E, DFF, RANK), inv_f), 'B_down': r(ks[16], (E, RANK, D), 0.02), 'expert_bias': jnp.zeros((E,), dtype=jnp.float32)}
    _L0_ffn_in = _L0_ffn_setup()

    def _L1_attn_setup():
        import jax, jax.numpy as jnp
        import numpy as np
        B, S, QD = (2, 512, 256)
        H, D = (32, 64)
        INNER = H * D
        key = jax.random.key(seed)
        ks = jax.random.split(key, 6)
        scale = 1.0 / np.sqrt(QD)
        return {'hidden_states': jax.random.normal(ks[0], (B, S, QD), dtype=jnp.float32), 'Wq': jax.random.normal(ks[1], (QD, INNER), dtype=jnp.float32) * scale, 'Wk': jax.random.normal(ks[2], (QD, INNER), dtype=jnp.float32) * scale, 'Wv': jax.random.normal(ks[3], (QD, INNER), dtype=jnp.float32) * scale, 'Wo': jax.random.normal(ks[4], (INNER, QD), dtype=jnp.float32) * (1.0 / np.sqrt(INNER)), 'bo': jax.random.normal(ks[5], (QD,), dtype=jnp.float32) * 0.01}
    _L1_attn_in = _L1_attn_setup()

    def _L1_ffn_setup():
        import jax, jax.numpy as jnp
        import numpy as np
        E, K, H, I = (64, 6, 256, 176)
        NS = 2
        IS = NS * I
        CAP = 32
        T_TOKENS = (1, 128)
        SCALE = 0.02

        def _moe_infer(x, gate_w, w_gate, w_up, w_down):
            T = x.shape[0]
            TK = T * K
            logits = x @ gate_w.T
            scores = jax.nn.softmax(logits, axis=-1)
            topk_w, topk_i = jax.lax.top_k(scores, K)
            flat_i = topk_i.reshape(-1)
            flat_w = topk_w.reshape(-1)
            token_ids = jnp.arange(TK, dtype=jnp.int32) // K
            order = jnp.argsort(flat_i)
            sorted_e = flat_i[order]
            counts = jnp.bincount(flat_i, length=E)
            starts = jnp.concatenate([jnp.zeros((1,), counts.dtype), jnp.cumsum(counts)[:-1]])
            pos_sorted = jnp.arange(TK) - starts[sorted_e]
            pos = jnp.zeros((TK,), jnp.int32).at[order].set(pos_sorted.astype(jnp.int32))
            valid = pos < CAP
            slot = jnp.where(valid, pos, CAP)
            buf = jnp.zeros((E, CAP + 1, H), x.dtype).at[flat_i, slot].set(x[token_ids])
            g = jnp.einsum('ech,ehi->eci', buf, w_gate)
            u = jnp.einsum('ech,ehi->eci', buf, w_up)
            y = jnp.einsum('eci,eih->ech', jax.nn.silu(g) * u, w_down)
            out_slots = y[flat_i, slot] * (flat_w * valid)[:, None]
            return out_slots.reshape(T, K, H).sum(axis=1)
        key = jax.random.key(seed)
        ks = jax.random.split(key, 8)
        f32 = jnp.float32
        return {'hidden_states': jax.random.normal(ks[0], (*T_TOKENS, H), f32), 'gate_w': jax.random.normal(ks[1], (E, H), f32) * SCALE, 'w_gate': jax.random.normal(ks[2], (E, H, I), f32) * SCALE, 'w_up': jax.random.normal(ks[3], (E, H, I), f32) * SCALE, 'w_down': jax.random.normal(ks[4], (E, I, H), f32) * SCALE, 'sw_gate': jax.random.normal(ks[5], (H, IS), f32) * SCALE, 'sw_up': jax.random.normal(ks[6], (H, IS), f32) * SCALE, 'sw_down': jax.random.normal(ks[7], (IS, H), f32) * SCALE}
    _L1_ffn_in = _L1_ffn_setup()
    _d = {'L0_attn_x': _L0_attn_in['x'], 'L0_attn_wq': _L0_attn_in['wq'], 'L0_attn_w_down': _L0_attn_in['w_down'], 'L0_attn_w_up': _L0_attn_in['w_up'], 'L0_attn_wo': _L0_attn_in['wo'], 'L0_ffn_W_router': _L0_ffn_in['W_router'], 'L0_ffn_W_gate': _L0_ffn_in['W_gate'], 'L0_ffn_W_up': _L0_ffn_in['W_up'], 'L0_ffn_W_down': _L0_ffn_in['W_down'], 'L0_ffn_sA_gate': _L0_ffn_in['sA_gate'], 'L0_ffn_sB_gate': _L0_ffn_in['sB_gate'], 'L0_ffn_sA_up': _L0_ffn_in['sA_up'], 'L0_ffn_sB_up': _L0_ffn_in['sB_up'], 'L0_ffn_sA_down': _L0_ffn_in['sA_down'], 'L0_ffn_sB_down': _L0_ffn_in['sB_down'], 'L0_ffn_A_gate': _L0_ffn_in['A_gate'], 'L0_ffn_B_gate': _L0_ffn_in['B_gate'], 'L0_ffn_A_up': _L0_ffn_in['A_up'], 'L0_ffn_B_up': _L0_ffn_in['B_up'], 'L0_ffn_A_down': _L0_ffn_in['A_down'], 'L0_ffn_B_down': _L0_ffn_in['B_down'], 'L0_ffn_expert_bias': _L0_ffn_in['expert_bias'], 'L1_attn_Wq': _L1_attn_in['Wq'], 'L1_attn_Wk': _L1_attn_in['Wk'], 'L1_attn_Wv': _L1_attn_in['Wv'], 'L1_attn_Wo': _L1_attn_in['Wo'], 'L1_attn_bo': _L1_attn_in['bo'], 'L1_ffn_gate_w': _L1_ffn_in['gate_w'], 'L1_ffn_w_gate': _L1_ffn_in['w_gate'], 'L1_ffn_w_up': _L1_ffn_in['w_up'], 'L1_ffn_w_down': _L1_ffn_in['w_down'], 'L1_ffn_sw_gate': _L1_ffn_in['sw_gate'], 'L1_ffn_sw_up': _L1_ffn_in['sw_up'], 'L1_ffn_sw_down': _L1_ffn_in['sw_down']}
    _x0 = _d['L0_attn_x']
    _d['L0_attn_x'] = jax.random.normal(jax.random.fold_in(jax.random.key(seed), 1), (4, 512, 256), dtype=_x0.dtype)
    del _x0
    return _d

def reference(L0_attn_x, L0_attn_wq, L0_attn_w_down, L0_attn_w_up, L0_attn_wo, L0_ffn_W_router, L0_ffn_W_gate, L0_ffn_W_up, L0_ffn_W_down, L0_ffn_sA_gate, L0_ffn_sB_gate, L0_ffn_sA_up, L0_ffn_sB_up, L0_ffn_sA_down, L0_ffn_sB_down, L0_ffn_A_gate, L0_ffn_B_gate, L0_ffn_A_up, L0_ffn_B_up, L0_ffn_A_down, L0_ffn_B_down, L0_ffn_expert_bias, L1_attn_Wq, L1_attn_Wk, L1_attn_Wv, L1_attn_Wo, L1_attn_bo, L1_ffn_gate_w, L1_ffn_w_gate, L1_ffn_w_up, L1_ffn_w_down, L1_ffn_sw_gate, L1_ffn_sw_up, L1_ffn_sw_down):

    def _L0_attn_ref(x, wq, w_down, w_up, wo):
        import jax, jax.numpy as jnp
        import numpy as np
        N_HEADS = 16
        HEAD_DIM = 128
        ROPE_BASE = 10000.0

        def _apply_rope(x, start_pos):
            B, T, H, Dh = x.shape
            half = Dh // 2
            inv_freq = 1.0 / ROPE_BASE ** (jnp.arange(0, Dh, 2, dtype=jnp.float32) / Dh)
            pos = jnp.arange(T, dtype=jnp.float32) + start_pos
            ang = pos[:, None] * inv_freq[None, :]
            cos = jnp.cos(ang)[None, :, None, :].astype(x.dtype)
            sin = jnp.sin(ang)[None, :, None, :].astype(x.dtype)
            x1 = x[..., 0::2]
            x2 = x[..., 1::2]
            r1 = x1 * cos - x2 * sin
            r2 = x1 * sin + x2 * cos
            return jnp.stack([r1, r2], axis=-1).reshape(B, T, H, Dh)
        B, T, D = x.shape
        H, Dh = (N_HEADS, HEAD_DIM)
        scale = Dh ** (-0.5)
        q = (x @ wq).reshape(B, T, H, Dh)
        c_kv = x @ w_down
        kv_up = (c_kv @ w_up).reshape(B, T, H, 2 * Dh)
        k, v = (kv_up[..., :Dh], kv_up[..., Dh:])
        q = _apply_rope(q, 0)
        k = _apply_rope(k, 0)
        scores = jnp.einsum('bqhd,bkhd->bhqk', q, k) * scale
        causal = jnp.tril(jnp.ones((T, T), dtype=bool))
        scores = jnp.where(causal[None, None, :, :], scores, jnp.float32(-jnp.inf))
        attn = jax.nn.softmax(scores, axis=-1)
        out = jnp.einsum('bhqk,bkhd->bqhd', attn, v).reshape(B, T, H * Dh)
        return out @ wo

    def _L0_ffn_ref(x, W_router, W_gate, W_up, W_down, sA_gate, sB_gate, sA_up, sB_up, sA_down, sB_down, A_gate, B_gate, A_up, B_up, A_down, B_down, expert_bias):
        import jax, jax.numpy as jnp
        import numpy as np
        B, L, D = (2, 128, 256)
        E, TOP_K, RANK, DFF = (8, 2, 8, 688)

        def _lora(x, A, Bm, scale):
            return x @ A @ Bm * scale

        def _expert_lora(x, A, Bm, w, scale):
            xA = jnp.einsum('bld,edr->bler', x, A)
            xAB = jnp.einsum('bler,erd->bled', xA, Bm) * scale
            return (xAB * w).sum(axis=2)
        scale = 1.0 / RANK
        logits = x @ W_router
        scores = jax.nn.sigmoid(logits)
        biased = scores + expert_bias
        _, topk_idx = jax.lax.top_k(biased, TOP_K)
        topk_scores = jnp.take_along_axis(scores, topk_idx, axis=-1)
        topk_w = topk_scores / (topk_scores.sum(-1, keepdims=True) + 1e-08)
        one_hot = jax.nn.one_hot(topk_idx, E, dtype=x.dtype)
        expert_weights = (one_hot * topk_w[..., None]).sum(axis=2)
        w = expert_weights[..., None]
        gate = x @ W_gate + _lora(x, sA_gate, sB_gate, scale) + _expert_lora(x, A_gate, B_gate, w, scale)
        up = x @ W_up + _lora(x, sA_up, sB_up, scale) + _expert_lora(x, A_up, B_up, w, scale)
        hidden = jax.nn.silu(gate) * up
        out = hidden @ W_down + _lora(hidden, sA_down, sB_down, scale) + _expert_lora(hidden, A_down, B_down, w, scale)
        return out

    def _L1_attn_ref(hidden_states, Wq, Wk, Wv, Wo, bo):
        import jax, jax.numpy as jnp
        import numpy as np
        B, S, QD = (2, 512, 256)
        H, D = (32, 64)
        INNER = H * D
        b, s, _ = hidden_states.shape

        def proj(W):
            return (hidden_states @ W).reshape(b, s, H, D).transpose(0, 2, 1, 3)
        q = jax.nn.relu(proj(Wq))
        k = jax.nn.relu(proj(Wk))
        v = proj(Wv)
        kv = jnp.einsum('bhsd,bhse->bhde', k, v)
        qkv = jnp.einsum('bhsd,bhde->bhse', q, kv)
        key_sum = k.sum(axis=2)
        normalizer = jnp.einsum('bhsd,bhd->bhs', q, key_sum)
        normalizer = jnp.clip(normalizer, 1e-06, None)[..., None]
        out = qkv / normalizer
        out = out.transpose(0, 2, 1, 3).reshape(b, s, INNER)
        return out @ Wo + bo

    def _L1_ffn_ref(hidden_states, gate_w, w_gate, w_up, w_down, sw_gate, sw_up, sw_down):
        import jax, jax.numpy as jnp
        import numpy as np
        E, K, H, I = (64, 6, 256, 176)
        NS = 2
        IS = NS * I
        CAP = 32
        T_TOKENS = (1, 128)
        SCALE = 0.02

        def _moe_infer(x, gate_w, w_gate, w_up, w_down):
            T = x.shape[0]
            TK = T * K
            logits = x @ gate_w.T
            scores = jax.nn.softmax(logits, axis=-1)
            topk_w, topk_i = jax.lax.top_k(scores, K)
            flat_i = topk_i.reshape(-1)
            flat_w = topk_w.reshape(-1)
            token_ids = jnp.arange(TK, dtype=jnp.int32) // K
            order = jnp.argsort(flat_i)
            sorted_e = flat_i[order]
            counts = jnp.bincount(flat_i, length=E)
            starts = jnp.concatenate([jnp.zeros((1,), counts.dtype), jnp.cumsum(counts)[:-1]])
            pos_sorted = jnp.arange(TK) - starts[sorted_e]
            pos = jnp.zeros((TK,), jnp.int32).at[order].set(pos_sorted.astype(jnp.int32))
            valid = pos < CAP
            slot = jnp.where(valid, pos, CAP)
            buf = jnp.zeros((E, CAP + 1, H), x.dtype).at[flat_i, slot].set(x[token_ids])
            g = jnp.einsum('ech,ehi->eci', buf, w_gate)
            u = jnp.einsum('ech,ehi->eci', buf, w_up)
            y = jnp.einsum('eci,eih->ech', jax.nn.silu(g) * u, w_down)
            out_slots = y[flat_i, slot] * (flat_w * valid)[:, None]
            return out_slots.reshape(T, K, H).sum(axis=1)
        orig_shape = hidden_states.shape
        x = hidden_states.reshape(-1, orig_shape[-1])
        y = _moe_infer(x, gate_w, w_gate, w_up, w_down).reshape(orig_shape)
        shared = jax.nn.silu(hidden_states @ sw_gate) * (hidden_states @ sw_up) @ sw_down
        return y + shared
    x = L0_attn_x
    x = _layernorm(x + _L0_attn_ref(x, L0_attn_wq, L0_attn_w_down, L0_attn_w_up, L0_attn_wo), axis=-1)
    x = _layernorm(x + _L0_ffn_ref(x, L0_ffn_W_router, L0_ffn_W_gate, L0_ffn_W_up, L0_ffn_W_down, L0_ffn_sA_gate, L0_ffn_sB_gate, L0_ffn_sA_up, L0_ffn_sB_up, L0_ffn_sA_down, L0_ffn_sB_down, L0_ffn_A_gate, L0_ffn_B_gate, L0_ffn_A_up, L0_ffn_B_up, L0_ffn_A_down, L0_ffn_B_down, L0_ffn_expert_bias), axis=-1)
    x = _layernorm(x + _L1_attn_ref(x, L1_attn_Wq, L1_attn_Wk, L1_attn_Wv, L1_attn_Wo, L1_attn_bo), axis=-1)
    x = _layernorm(x + _L1_ffn_ref(x, L1_ffn_gate_w, L1_ffn_w_gate, L1_ffn_w_up, L1_ffn_w_down, L1_ffn_sw_gate, L1_ffn_sw_up, L1_ffn_sw_down), axis=-1)
    return x

_drawn_inputs = setup_inputs


def setup_inputs(seed=0):
    import zlib

    import numpy as np

    out = dict(_drawn_inputs(seed))
    spreads = {'L0_ffn_expert_bias': (0.0, 0.8)}
    factors = {'L0_ffn_W_router': 8.0,
     'L0_ffn_sA_gate': 8.0,
     'L0_ffn_sB_gate': 8.0,
     'L0_ffn_sA_up': 8.0,
     'L0_ffn_sB_up': 8.0,
     'L0_ffn_sA_down': 8.0,
     'L0_ffn_sB_down': 8.0,
     'L0_ffn_A_gate': 8.0,
     'L0_ffn_B_gate': 8.0,
     'L0_ffn_A_up': 8.0,
     'L0_ffn_B_up': 8.0,
     'L0_ffn_A_down': 8.0,
     'L0_ffn_B_down': 8.0,
     'L1_attn_Wq': 2.981,
     'L1_attn_bo': 5.43,
     'L1_ffn_gate_w': 8.0,
     'L1_ffn_w_gate': 8.0,
     'L1_ffn_w_up': 8.0,
     'L1_ffn_w_down': 8.0,
     'L1_ffn_sw_gate': 2.889,
     'L1_ffn_sw_up': 2.859,
     'L1_ffn_sw_down': 2.856}
    for name, (base, spread) in spreads.items():
        noise = np.random.default_rng([zlib.crc32(name.encode()), seed]).standard_normal(out[name].shape)
        drawn = base * np.exp(spread * noise) if base else spread * noise
        out[name] = jnp.asarray(drawn.astype(out[name].dtype))
    for name, factor in factors.items():
        out[name] = (out[name] * factor).astype(out[name].dtype)
    return out
```

```python
from contextlib import ExitStack

import numpy as np

import concourse.bass as bass
from concourse import mybir

ALU = mybir.AluOpType
ACT = mybir.ActivationFunctionType
AX_X = mybir.AxisListType.X
F32 = mybir.dt.float32
F32R = mybir.dt.float32r
BF16 = mybir.dt.bfloat16
U32 = mybir.dt.uint32

P = 128
BATCH, T, D = 4, 512, 256
TOK = BATCH * T
TILES = TOK // P
TPB = T // P
KD = D // P
HEADS, DH = 16, 128
PAIRS = HEADS // 2
STEPS = 2 * BATCH
EPS = 1e-5
F0, E0, R0 = 688, 8, 8
NL = (1 + E0) * R0
NA = E0 + 2 * NL
FT0 = 6
F0S = [(i * 115, 115) for i in range(4)] + [(460, 114), (574, 114)]
M0 = 115
E1, I1, CAP, TOP1 = 64, 176, 32, 6
IH = I1 // 2
GROUPS = E1 * CAP // P
ROW = D + E1
F1S = 352
F1T = [(0, 118), (118, 117), (235, 117)]
FT1, M1 = 3, 118
LINKS4 = 46
CHUNKS = 4
PPC = 4
BLOCKS = CHUNKS * BATCH
LINKS0 = 38
SCALE = float(DH) ** -0.5
MASKED = -1.0e30
ROPE_BASE = 10000.0
HALVES = ((0, 0), (1, 0), (0, 1))


def program(nc, io, out):
    ctx = ExitStack()
    with ctx:
        def sem(name):
            return ctx.enter_context(nc.semaphore(name))

        def wait_past(engine, signal, count):
            if not (isinstance(count, int) and count <= 0):
                engine.wait_ge(signal, count)

        ps = ctx.enter_context(nc.psum_tensor("ps", [P, 8, 512], F32))
        BS, BA, BW, BO = 0, 2, 4, 7

        def place(name, kb, shape, dt=F32):
            with ExitStack() as stack:
                if kb:
                    stack.enter_context(nc.sbuf_tensor(name + "_below", [P, int(kb * 256)], F32))
                return stack.enter_context(nc.sbuf_tensor(name, shape, dt))

        acc = place("acc", 0, [P, TILES, D])
        ident = place("ident", 16, [P, P])
        identb = place("identb", 16.5, [P, P], BF16)
        maskb = place("maskb", 16.75, [P, P], BF16)
        halfp = place("halfp", 17, [P, TPB])
        iota8 = place("iota8", 17.25, [P, 64])
        ebias = place("ebias", 17.5, [P, E0])
        scratch = place("scratch", 17.75, [P, 1])

        xT = [place(f"xT{h}", 20 + 16 * h, [P, KD, TOK], F32R) for h in range(2)]
        cT = [place(f"cT{h}", 52 + 8 * h, [P, TOK], F32R) for h in range(2)]
        c_tok = place("c_tok", 68, [P, TILES, DH])
        rope = place("rope_sb", 76, [P, 2, T])
        wq_in = place("wq_in", 80, [P, KD, 2 * DH])
        wk_in = place("wk_in", 82, [P, 2 * DH])
        wq = [place(f"wq{h}", 83 + 2 * h, [P, KD, 2 * DH], F32R) for h in range(2)]
        wk = [place(f"wk{h}", 87 + h, [P, 2 * DH], F32R) for h in range(2)]
        U = place("U", 89, [P, HEADS, D])
        qT = place("qT", 105, [P, 2, BATCH, T])
        kT = place("kT", 121, [P, 2, BATCH, T])
        prod = [[place(f"prod{i}{j}", 137 + 8 * i + 4 * j, [P, 2, T]) for j in range(2)] for i in range(2)]
        mx = place("mx", 153, [P, 2, TPB])
        nm = place("nm", 153.25, [P, 2, TPB])
        rs = place("rs", 153.5, [P, 2, TPB])
        rinv = place("rinv", 153.75, [P, 2, TPB])
        wd_in = place("wd_in", 154, [P, KD, DH])
        wd = [place(f"wd{h}", 155 + h, [P, KD, DH], F32R) for h in range(2)]
        wv = place("wv", 157, [P, HEADS, DH])
        wvT = place("wvT", 165, [P, HEADS, DH])
        wo = place("wo", 173, [P, HEADS, D])
        probs = [place(f"probs{i}", 154 + 5 * i, [P, 10 * P]) for i in range(2)]
        pT = place("pT", 164, [P, TPB, T])
        oT = place("oT", 172, [P, T])

        gu_in = place("gu_in", 174, [P, KD, 2, F0])
        lb_in = place("lb_in", 185, [NL, 2, F0])
        dn = place("dn", 191, [M0, FT0, D + NL])
        la_in = place("la_in", 199, [P, KD, NA])
        ldn = place("ldn", 200.5, [NL, D])
        gu = [place(f"gu{h}", 20 + 11 * h, [P, KD, 2, F0], F32R) for h in range(2)]
        lb = [place(f"lb{h}", 42 + 5.5 * h, [NL, 2, F0], F32R) for h in range(2)]
        la = [place(f"la{h}", 53 + 1.25 * h, [P, KD, NA], F32R) for h in range(2)]
        x1T = [place(f"x1T{h}", 56 + 4 * h, [P, KD, T], F32R) for h in range(2)]
        xaT = [place(f"xaT{h}", 64 + 4 * h, [NL, 2, T], F32R) for h in range(2)]
        gated = [place(f"gated{h}", 72 + 2 * h, [M0, T]) for h in range(2)]
        hidT = place("hidT", 76, [M0, FT0, T])
        haT = place("haT", 88, [NL, T])
        xa = place("xa", 90, [P, TPB, 2 * NL])
        ha = place("ha", 92.5, [P, TPB, NL])
        x1s = place("x1s", 94, [P, TPB, D])
        stat = place("stat", 19.25, [P, TPB, 6])
        meanvar = place("meanvar", 19.375, [P, TPB, 2])
        vareps = place("vareps", 19.5, [P, TPB])
        rstd = place("rstd", 19.625, [P, TPB])
        sig = place("sig", 99, [P, TPB, E0])
        biased = place("biased", 99.25, [P, TPB, E0])
        top8 = place("top8", 99.5, [P, TPB, 8])
        topi = place("topi", 99.75, [P, TPB, 8], U32)
        topf = place("topf", 100, [P, TPB, 8])
        one0 = place("one0", 100.25, [P, TPB, E0])
        one1 = place("one1", 100.5, [P, TPB, E0])
        picked = place("picked", 100.75, [P, TPB, E0])
        den = place("den", 101, [P, TPB])
        wexp = place("wexp", 101.25, [P, TPB, 1 + E0])
        x2 = [place(f"x2{h}", 158 + 16 * h, [P, TILES, D], F32R) for h in range(2)]

        CH = 4 * P
        wq3_in = place("wq3_in", 110, [P, KD, CH])
        wv3_in = place("wv3_in", 114, [P, KD, CH])
        wo3_in = place("wo3_in", 118, [P, 4, D])
        wk3_in = place("wk3_in", 122, [P, KD, CH])
        wq3 = [place(f"wq3{h}", 126 + 4 * h, [P, KD, CH], F32R) for h in range(2)]
        wv3 = [place(f"wv3{h}", 134 + 4 * h, [P, KD, CH], F32R) for h in range(2)]
        wo3 = [place(f"wo3{h}", 142 + 4 * h, [P, 4, D], F32R) for h in range(2)]
        wk3 = [place("wk30", 190, [P, CHUNKS, KD, CH], F32R), place("wk31", 93, [P, CHUNKS, KD, CH], F32R)]
        x2T = [place(f"x2T{h}", 20 + 16 * h, [P, KD, TOK], F32R) for h in range(2)]
        k3 = [place(f"k3{h}", 52 + 8 * h, [P, TPB, CH], F32R) for h in range(2)]
        g3 = [place(f"g3{h}", 68 + 4 * h, [P, KD, CH], F32R) for h in range(2)]
        kvs = [place(f"kvs{h}", 76 + 2.25 * h, [P, 4, P + 2], F32R) for h in range(2)]
        q3 = [place(f"q3{h}", 80.5 + 2 * h, [P, T], F32R) for h in range(2)]
        y3 = place("y3", 84.5, [P, TPB, P])
        yT3 = [place(f"yT3{h}", 86.5 + 2 * h, [P, T], F32R) for h in range(2)]
        ks4 = place("ks4", 90.5, [P, CH])
        nrm = place("nrm", 92.5, [P, 2, 2, 2])
        rnm = place("rnm", 92.75, [P, TPB, 2])
        sw_in = place("sw_in", 93, [P, KD, 2, F1S])
        swd = place("swd", 98.5, [M1, FT1, D])
        gw_in = place("gw_in", 102, [E1, D])
        sw = [place(f"sw{h}", 20 + 5.5 * h, [P, KD, 2, F1S], F32R) for h in range(2)]
        gwT = [place(f"gwT{h}", 31 + 0.5 * h, [P, KD, E1], F32R) for h in range(2)]
        rows = place("rows", 32, [P, TPB, ROW])
        x3T = [place(f"x3T{h}", 37 + 4 * h, [P, KD, T], F32R) for h in range(2)]
        gated4 = [place(f"gated4{h}", 45 + 2 * h, [M1, T]) for h in range(2)]
        hid4 = place("hid4", 49, [M1, FT1, T])
        onehot = [place(f"onehot{h}", 55 + 4 * h, [P, E1, CAP], BF16) for h in range(2)]
        capi = place("capi", 63, [P, E1, CAP], BF16)
        tokv = place("tokv", 67, [P, TILES, 4], BF16)
        tri = place("tri", 67.25, [P, P], BF16)
        onesb = place("onesb", 67.5, [P, P], BF16)
        carry = place("carry", 67.75, [P, E1], BF16)
        sel = place("sel", 68, [P, TPB, E1], BF16)
        selsum = place("selsum", 68.5, [P, E1])
        e4 = place("e4", 69, [P, TPB, E1])
        posb = place("posb", 70, [P, TPB, E1], BF16)
        pm = place("pm", 70.5, [P, TPB, E1])
        mx4 = place("mx4", 71.5, [P, TPB])
        nmx4 = place("nmx4", 71.75, [P, TPB])
        sm4 = place("sm4", 72, [P, TPB])
        top4 = place("top4", 72.25, [P, TPB, 8])
        top4i = place("top4i", 72.5, [P, TPB, 8], U32)
        top4f = place("top4f", 72.75, [P, TPB, 8])
        slots = place("slots", 73, [P, GROUPS, 4])
        xg = place("xg", 20, [P, GROUPS, ROW])
        xs = place("xs", 40, [P, D])
        xsT = [place(f"xsT{h}", 41 + 22 * h, [P, KD, P]) for h in range(2)]
        actE = place("actE", 42, [P, I1])
        hE = place("hE", 43, [P, I1])
        hET = place("hET", 44, [IH, 2, P])
        pick = [place(f"pick{h}", 45 + 8 * h, [P, GROUPS, P], F32R) for h in range(2)]
        fin = place("fin", 61, [P, 2, D])
        y4 = [place("y40", 74, [P, GROUPS, D], F32R), place("y41", 104, [P, GROUPS, D], F32R)]
        iota_t = place("iota_t", 90, [P, P])
        tbase = place("tbase", 90.75, [P, TILES])
        quarter = place("quarter", 91, [P, 4])
        wslot = place("wslot", 91.25, [P, GROUPS])
        idxf = place("idxf", 91.5, [P, GROUPS])
        gidx = place("gidx", 91.75, [P, GROUPS], U32)
        wtmp = place("wtmp", 92, [P, GROUPS, 4])
        eg = [place(f"eg{i}", 131 + 19 * i, [P, 4, 2, 2, I1]) for i in range(4)]
        ed = [place(f"ed{i}", 142 + 19 * i, [IH, 4, 2, D]) for i in range(4)]
        rows_dram = nc.dram_tensor("rows_dram", [TOK, ROW], F32, kind="Internal").ap()
        bo_sb = place("bo_sb", 18, [P, D])
        ones = place("ones", 19, [P, 1])

        x_in = [sem(f"x_in{b}") for b in range(BATCH)]
        wd_loaded, wv_loaded, wo_loaded = sem("wd_loaded"), sem("wv_loaded"), sem("wo_loaded")
        wq_loaded, wk_loaded = sem("wq_loaded"), sem("wk_loaded")
        zeroed, consts_ready = sem("zeroed"), sem("consts_ready")
        x_turned, xhi_ready, xlo_ready = sem("x_turned"), sem("xhi_ready"), sem("xlo_ready")
        wd_hi, wd_lo = sem("wd_hi"), sem("wd_lo")
        c_ready, chi_ready, clo_ready, ctok_ready = sem("c_ready"), sem("chi_ready"), sem("clo_ready"), sem("ctok_ready")
        wv_turned, wvT_ready, u_ready, u_copied = sem("wv_turned"), sem("wvT_ready"), sem("u_ready"), sem("u_copied")
        wq_hi, wq_lo, wk_hi, wk_lo = sem("wq_hi"), sem("wq_lo"), sem("wk_hi"), sem("wk_lo")
        proj_ready, products_ready, roped = sem("proj_ready"), sem("products_ready"), sem("roped")
        scores_ready, max_ready, negmax_ready, probs_ready = (
            sem("scores_ready"), sem("max_ready"), sem("negmax_ready"), sem("probs_ready"))
        transposed, pt_copied, pv_done, ot_copied = sem("transposed"), sem("pt_copied"), sem("pv_done"), sem("ot_copied")
        out_ready, acc_added, rinv_ready = sem("out_ready"), sem("acc_added"), sem("rinv_ready")
        stored = sem("stored")
        sw_loaded, gw_loaded, sw_hi, sw_lo = sem("sw_loaded"), sem("gw_loaded"), sem("sw_hi"), sem("sw_lo")
        gw_turned, consts4 = sem("gw_turned"), sem("consts4")
        x3_ready, x3_turned, x3hi_ready, x3lo_ready = sem("x3_ready"), sem("x3_turned"), sem("x3hi_ready"), sem("x3lo_ready")
        logits4, nmx4_ready, exp4, scored = sem("logits4"), sem("nmx4_ready"), sem("exp4"), sem("scored")
        rows_stored, gate4_ready, gated4_ready, hid4_ready = (
            sem("rows_stored"), sem("gate4_ready"), sem("gated4_ready"), sem("hid4_ready"))
        sel_ready, carry_ready, pos_ready = sem("sel_ready"), sem("carry_ready"), sem("pos_ready")
        onehot_ready, onehot_used, down4, added4 = sem("onehot_ready"), sem("onehot_used"), sem("down4"), sem("added4")
        slots_added, gidx_ready, gathered = sem("slots_added"), sem("gidx_ready"), sem("gathered")
        wslot_ready = sem("wslot_ready")
        e_loaded = x_in
        xs_ready, xs_turned, xsT_ready = sem("xs_ready"), sem("xs_turned"), sem("xsT_ready")
        gu4_ready, actE_ready, hE_ready, hE_turned, hET_ready = (
            sem("gu4_ready"), sem("actE_ready"), sem("hE_ready"), sem("hE_turned"), sem("hET_ready"))
        y_mm, yhi_ready, ylo_ready = sem("y_mm"), sem("yhi_ready"), sem("ylo_ready")
        pick_ready, comb_ready, comb_added, fin_ready = (
            sem("pick_ready"), sem("comb_ready"), sem("comb_added"), sem("fin_ready"))
        wq3_loaded, wk3_loaded, wv3_loaded, wo3_loaded, bo_loaded = (
            sem("wq3_loaded"), sem("wk3_loaded"), sem("wv3_loaded"), sem("wo3_loaded"), sem("bo_loaded"))
        wq3_ready, wk3_ready, wo3_ready = sem("wq3_ready"), sem("wk3_ready"), sem("wo3_ready")
        pool3, wv3_hi, wv3_lo = sem("pool3"), sem("wv3_hi"), sem("wv3_lo")
        x2_turned, x2Thi_ready, x2Tlo_ready = sem("x2_turned"), sem("x2Thi_ready"), sem("x2Tlo_ready")
        q_ready, qhi_ready, qlo_ready = sem("q_ready"), sem("qhi_ready"), sem("qlo_ready")
        k_ready, khi_ready, klo_ready = sem("k_ready"), sem("khi_ready"), sem("klo_ready")
        g_ready, ghi_ready, glo_ready = sem("g_ready"), sem("ghi_ready"), sem("glo_ready")
        ksummed, kv_ready, kvhi_ready, kvlo_ready = sem("ksummed"), sem("kv_ready"), sem("kvhi_ready"), sem("kvlo_ready")
        qkv_ready, norm_ready, y_ready = sem("qkv_ready"), sem("norm_ready"), sem("y_ready")
        yt_ready, ythi_ready, ytlo_ready = sem("yt_ready"), sem("ythi_ready"), sem("ytlo_ready")
        out3_ready, added3 = sem("out3_ready"), sem("added3")
        gu_loaded, lb_loaded, la_loaded, dn_loaded = sem("gu_loaded"), sem("lb_loaded"), sem("la_loaded"), sem("dn_loaded")
        w0_hi, w0_lo = sem("w0_hi"), sem("w0_lo")
        dchain = sem("dchain")
        var_ready, rstd_ready = sem("var_ready"), sem("rstd_ready")
        x1_ready, x1_turned, x1hi_ready, x1lo_ready = sem("x1_ready"), sem("x1_turned"), sem("x1hi_ready"), sem("x1lo_ready")
        logits_ready, sig_ready, xa_ready, xa_turned = sem("logits_ready"), sem("sig_ready"), sem("xa_ready"), sem("xa_turned")
        xahi_ready, xalo_ready = sem("xahi_ready"), sem("xalo_ready")
        gate_ready, gated_ready, hid_ready = sem("gate_ready"), sem("gated_ready"), sem("hid_ready")
        down_ready, ha_ready, ha_turned, haT_ready, ffn_ready = (
            sem("down_ready"), sem("ha_ready"), sem("ha_turned"), sem("haT_ready"), sem("ffn_ready"))
        ffn_added = sem("ffn_added")
        x2_ready, x2hi_ready, x2lo_ready = sem("x2_ready"), sem("x2hi_ready"), sem("x2lo_ready")

        x_dram = io["L0_attn_x"].rearrange("b (i p) d -> b p i d", p=P)
        out_dram = out.rearrange("b (i p) d -> b p i d", p=P)
        wq_dram = io["L0_attn_wq"].rearrange("(k p) n -> p k n", p=P)
        wup_dram = io["L0_attn_w_up"].rearrange("p (h w d) -> p h w d", w=2, d=DH)
        wo_dram = io["L0_attn_wo"].rearrange("(h p) n -> p h n", p=DH)

        block = ctx.enter_context(nc.Block())

        @block.sync
        def _(sp):
            for b in range(BATCH):
                sp.dma_start(acc[:, b * TPB:(b + 1) * TPB, :], x_dram[b]).then_inc(x_in[b], 16)
            sp.dma_start(wd_in[:], io["L0_attn_w_down"].rearrange("(k p) n -> p k n", p=P)).then_inc(wd_loaded, 16)
            sp.dma_start(wv[:], wup_dram[:, :, 1, :]).then_inc(wv_loaded, 16)
            sp.dma_start(wo[:], wo_dram).then_inc(wo_loaded, 16)
            sp.dma_start(rope[:], io["rope"].rearrange("w p t -> p w t")).then_inc(wo_loaded, 16)
            def load_pair(g):
                wait_past(sp, wq_lo, g)
                sp.dma_start(wq_in[:], wq_dram[:, :, bass.ds(g * (2 * DH), 2 * DH)]).then_inc(wq_loaded, 16)
                wait_past(sp, wk_lo, g)
                sp.dma_start(wk_in[:].rearrange("p (h d) -> p h d", h=2),
                             wup_dram[:, bass.ds(g * 2, 2), 0, :]).then_inc(wk_loaded, 16)

            load_pair(0)
            with sp.Fori(1, PAIRS) as g:
                load_pair(g)
            sp.wait_ge(u_ready, 8)
            for w, name in enumerate(("gate", "up")):
                sp.dma_start(gu_in[:, :, w, :], io["L0_ffn_W_" + name].rearrange("(k p) n -> p k n", p=P)).then_inc(gu_loaded, 16)
            for w, name in enumerate(("gate", "up")):
                sp.dma_start(lb_in[0:R0, w, :], io["L0_ffn_sB_" + name]).then_inc(lb_loaded, 16)
                sp.dma_start(lb_in[R0:NL, w, :], io["L0_ffn_B_" + name].rearrange("e r n -> (e r) n")).then_inc(lb_loaded, 16)
            sp.dma_start(la_in[:, :, 0:E0], io["L0_ffn_W_router"].rearrange("(k p) n -> p k n", p=P)).then_inc(la_loaded, 16)
            for w, name in enumerate(("gate", "up")):
                at = E0 + w * NL
                sp.dma_start(la_in[:, :, at:at + R0], io["L0_ffn_sA_" + name].rearrange("(k p) n -> p k n", p=P)).then_inc(la_loaded, 16)
                for k in range(KD):
                    sp.dma_start(la_in[:, k, at + R0:at + NL].rearrange("p (e r) -> p e r", r=R0),
                                 io["L0_ffn_A_" + name].rearrange("e (k p) r -> k p e r", p=P)[k]).then_inc(la_loaded, 16)
            for lo, hi, size in ((0, 4, 115), (4, 6, 114)):
                inner = slice(F0S[lo][0], F0S[hi - 1][0] + size)
                sp.dma_start(dn[0:size, lo:hi, 0:D],
                             io["L0_ffn_W_down"][inner, :].rearrange("(i p) n -> p i n", p=size)).then_inc(dn_loaded, 16)
                sp.dma_start(dn[0:size, lo:hi, D:D + R0],
                             io["L0_ffn_sA_down"][inner, :].rearrange("(i p) n -> p i n", p=size)).then_inc(dn_loaded, 16)
                for i in range(lo, hi):
                    sp.dma_start(dn[0:size, i, D + R0:D + NL].rearrange("p (e r) -> p e r", r=R0),
                                 io["L0_ffn_A_down"][:, F0S[i][0]:F0S[i][0] + size, :].rearrange("e p r -> p e r")).then_inc(dn_loaded, 16)
            sp.dma_start(ldn[0:R0, :], io["L0_ffn_sB_down"]).then_inc(dn_loaded, 16)
            sp.dma_start(ldn[R0:NL, :], io["L0_ffn_B_down"].rearrange("e r n -> (e r) n")).then_inc(dn_loaded, 16)
            sp.dma_start(ebias[:], io["L0_ffn_expert_bias"].rearrange("(a e) -> a e", a=1).broadcast_to([P, E0])).then_inc(la_loaded, 16)
            w3 = {n: io["L1_attn_W" + n].rearrange("(k p) n -> p k n", p=P) for n in "qkv"}
            wo3_dram = io["L1_attn_Wo"].rearrange("(j p) n -> p j n", p=P)
            sp.dma_start(bo_sb[:], io["L1_attn_bo"].rearrange("(a e) -> a e", a=1).broadcast_to([P, D])).then_inc(bo_loaded, 16)
            sp.wait_ge(acc_added, 4 * STEPS * PAIRS)

            def load_chunk(c):
                cols = bass.ds(c * CH, CH)
                wait_past(sp, wq3_ready, PPC * c)
                sp.dma_start(wq3_in[:], w3["q"][:, :, cols]).then_inc(wq3_loaded, 16)
                wait_past(sp, wv3_lo, c)
                sp.dma_start(wv3_in[:], w3["v"][:, :, cols]).then_inc(wv3_loaded, 16)
                wait_past(sp, wo3_ready, PPC * c)
                sp.dma_start(wo3_in[:], wo3_dram[:, bass.ds(c * PPC, PPC), :]).then_inc(wo3_loaded, 16)
                wait_past(sp, wk3_ready, c)
                sp.dma_start(wk3_in[:], w3["k"][:, :, cols]).then_inc(wk3_loaded, 16)

            load_chunk(0)
            with sp.Fori(1, CHUNKS) as c:
                load_chunk(c)
            sp.wait_ge(k_ready, 4 * BLOCKS)
            for w, name in enumerate(("gate", "up")):
                sp.dma_start(sw_in[:, :, w, :], io["L1_ffn_sw_" + name].rearrange("(k p) n -> p k n", p=P)).then_inc(sw_loaded, 16)
            sp.dma_start(gw_in[:], io["L1_ffn_gate_w"]).then_inc(gw_loaded, 16)
            sp.dma_start(swd[:, 0, :], io["L1_ffn_sw_down"][0:118, :]).then_inc(sw_loaded, 16)
            sp.dma_start(swd[0:117, 1:3, :], io["L1_ffn_sw_down"][118:352, :].rearrange("(i p) n -> p i n", p=117)).then_inc(sw_loaded, 16)

            def load_experts(s, i):
                x = slice(4 * s, 4 * s + 4) if isinstance(s, int) else bass.ds(4 * s, 4)
                for w, name in enumerate(("gate", "up")):
                    sp.dma_start(eg[i][:, :, w, :, :].rearrange("p x k n -> p x (k n)"),
                                 io["L1_ffn_w_" + name].rearrange("x (p k) n -> p x (k n)", k=2)[:, x, :]).then_inc(e_loaded[i], 16)
                sp.dma_start(ed[i][:].rearrange("p x k n -> p x (k n)"),
                             io["L1_ffn_w_down"].rearrange("x (p k) n -> p x (k n)", k=2)[:, x, :]).then_inc(e_loaded[i], 16)

            sp.wait_ge(g_ready, 2 * BLOCKS)
            for i in (1, 2, 3):
                load_experts(i, i)
            sp.wait_ge(out3_ready, BLOCKS * PPC)
            load_experts(0, 0)
            with sp.Fori(0, BATCH) as b:
                sp.wait_ge(scored, b + 1)
                sp.dma_start(rows_dram[bass.ds(b * T, T), :].rearrange("(i p) n -> p i n", p=P), rows[:]).then_inc(rows_stored, 16)
            with sp.Fori(1, GROUPS // 4) as it:
                for i in range(4):
                    sp.wait_ge(y_mm, it * 4 + (i - 3))
                    load_experts(it * 4 + i, i)
            with sp.Fori(0, TILES // 2) as j:
                sp.wait_ge(fin_ready, 2 * j + 2)
                sp.dma_start(out.rearrange("b t d -> (b t) d")[bass.ds(j * (2 * P), 2 * P), :].rearrange("(i p) n -> p i n", p=P),
                             fin[:]).then_inc(stored, 16)
            sp.wait_ge(stored, 16 * (TILES // 2))
        @block.gpsimd
        def _(pool):
            nc.gpsimd.memset(ident[:], 0.0).then_inc(zeroed, 1)
            nc.gpsimd.memset(identb[:], 0.0).then_inc(zeroed, 1)
            nc.gpsimd.memset(maskb[:], 0.0).then_inc(zeroed, 1)
            nc.gpsimd.memset(ones[:], 1.0).then_inc(consts_ready, 1)
            nc.gpsimd.memset(halfp[:], -0.5).then_inc(consts_ready, 1)
            nc.gpsimd.iota(iota8[:], pattern=[[1, 64]], base=0, channel_multiplier=0,
                           allow_small_or_imprecise_dtypes=True).then_inc(consts_ready, 1)
            pool.wait_ge(zeroed, 3)
            for m in (ident, identb):
                nc.gpsimd.affine_select(out=m[:], in_=m[:], compare_op=ALU.not_equal, fill=1.0, base=0,
                                        pattern=[[-1, P]], channel_multiplier=1).then_inc(consts_ready, 1)
            nc.gpsimd.affine_select(out=maskb[:], in_=maskb[:], compare_op=ALU.is_ge, fill=MASKED, base=0,
                                    pattern=[[-1, P]], channel_multiplier=1).then_inc(consts_ready, 1)

            def rotate(dst, b, idx, parity, scores_before):
                pool.wait_ge(products_ready, 2 * idx + 2)
                if scores_before is not None:
                    pool.wait_ge(scores_ready, scores_before)
                byc, bys = prod[parity]
                for h in range(2):
                    r = slice(64 * h, 64 * h + 64)
                    nc.gpsimd.tensor_tensor(dst[0:64, h, b, :], byc[r, 0, :], bys[r, 1, :],
                                            ALU.subtract).then_inc(roped, 1)
                    nc.gpsimd.tensor_tensor(dst[64:128, h, b, :], bys[r, 0, :], byc[r, 1, :],
                                            ALU.add).then_inc(roped, 1)

            for b in range(BATCH - 1):
                rotate(qT, b, 2 * b, 0, None)
                rotate(kT, b, 2 * b + 1, 1, None)

            def pair(g, first, last):
                for n in range(2 if last else STEPS):
                    idx = g * STEPS + (6 + n)
                    b = (3, 0, 1, 2)[n // 2]
                    if n < 2:
                        before = None if first else g * (4 * STEPS)
                    else:
                        before = g * (4 * STEPS) + 4 * (2 * b + 2)
                    rotate((qT, kT)[n % 2], b, idx, n % 2, before)

            pair(0, True, False)
            with pool.Fori(1, PAIRS - 1) as g:
                pair(g, False, False)
            pair(PAIRS - 1, False, True)

            def root(n):
                pool.wait_ge(var_ready, n)
                nc.gpsimd.tensor_tensor(rstd[:], vareps[:], halfp[:], ALU.pow).then_inc(rstd_ready, 1)

            def x2_rest(b):
                pool.wait_ge(x2hi_ready, b + 1)
                t = bass.ds(b * TPB, TPB)
                nc.gpsimd.tensor_tensor(x2[1][:, t, :], acc[:, t, :], x2[0][:, t, :].bitcast(F32),
                                        ALU.subtract).then_inc(x2lo_ready, 1)

            root(1)
            root(2)
            root(3)
            x2_rest(0)
            pool.wait_ge(acc_added, 4 * STEPS * PAIRS)
            pool3_done = [0, 0]

            def halve(whole, hi, lo, ready):
                one = ones[0:whole.shape[0], :]
                if len(whole.shape) == 3:
                    one = one.rearrange("p (a n) -> p a n", a=1)
                nc.gpsimd.tensor_tensor(hi, whole, one.broadcast_to(list(whole.shape)), ALU.mult).then_inc(pool3, 1)
                pool3_done[1] += 1
                pool.wait_ge(pool3, pool3_done[0] + pool3_done[1])
                nc.gpsimd.tensor_tensor(lo, whole, hi.bitcast(F32), ALU.subtract).then_inc(ready, 1)

            def halve_wq3(p):
                j = slice(p * P, (p + 1) * P)
                halve(wq3_in[:, :, j], wq3[0][:, :, j], wq3[1][:, :, j], wq3_ready)

            def halve_wo3(p):
                halve(wo3_in[:, p, :], wo3[0][:, p, :], wo3[1][:, p, :], wo3_ready)

            def halve_wk3(c):
                pool.wait_ge(wk3_loaded, 16 * c + 16)
                if isinstance(c, int):
                    o = [w[:, c, :, :] for w in wk3]
                else:
                    o = [w[:, bass.ds(c, 1), :, :].rearrange("p c k n -> p (c k) n") for w in wk3]
                halve(wk3_in[:], o[0], o[1], wk3_ready)

            pool.wait_ge(consts_ready, 6)
            pool.wait_ge(wq3_loaded, 16)
            halve_wq3(0)
            halve_wq3(1)
            root(4)
            root(5)
            x2_rest(1)
            halve_wq3(2)
            halve_wq3(3)
            pool.wait_ge(wo3_loaded, 16)
            root(6)
            root(7)
            x2_rest(2)
            for p in range(PPC):
                halve_wo3(p)
            root(8)
            x2_rest(3)
            pool.wait_ge(x2_ready, TILES)
            halve_wk3(0)
            nc.gpsimd.memset(kvs[0][:].bitcast(F32), 0.0).then_inc(zeroed, 1)
            nc.gpsimd.memset(kvs[1][:].bitcast(F32), 0.0).then_inc(zeroed, 1)

            def sum_keys(n, p):
                pool.wait_ge(klo_ready, 4 * n + (p + 1))
                hi, lo = k3[0][:, p, :].bitcast(F32), k3[1][:, p, :].bitcast(F32)
                if p == 0:
                    if not (isinstance(n, int) and n == 0):
                        pool.wait_ge(kv_ready, n)
                    nc.gpsimd.tensor_tensor(ks4[:], hi, lo, ALU.add).then_inc(ksummed, 1)
                else:
                    for j, part in enumerate((hi, lo)):
                        pool.wait_ge(ksummed, 7 * n + 2 * p - 1 + j)
                        nc.gpsimd.tensor_tensor(ks4[:], ks4[:], part, ALU.add).then_inc(ksummed, 1)

            def chunk3(c, last):
                for b in range(BATCH):
                    n = c * BATCH + b
                    if b == 3 and last:
                        return
                    for p in range(PPC):
                        sum_keys(n + 1, p)
                        if b == 3:
                            pool.wait_ge(wq3_loaded, 16 * c + 32)
                            pool.wait_ge(q_ready, 4 * n + (p + 1))
                            halve_wq3(p)
                            if p >= 2:
                                pool.wait_ge(wo3_loaded, 16 * c + 32)
                                pool.wait_ge(out3_ready, 4 * n + (p - 1))
                                halve_wo3(p - 2)
                    if b == 1 and not last:
                        halve_wk3(c + 1)

            for p in range(PPC):
                sum_keys(0, p)

            def wo_tail(n):
                for p in (2, 3):
                    pool.wait_ge(out3_ready, 4 * n + (p + 1))
                    halve_wo3(p)

            pool3_done[0], pool3_done[1] = pool3_done[1], 0
            first_base = pool3_done[0]
            chunk3(0, False)
            per = pool3_done[1] + 2
            with pool.Fori(1, CHUNKS - 1) as c:
                pool3_done[0], pool3_done[1] = first_base + (c - 1) * per + (per - 2), 0
                wo_tail(c * BATCH - 1)
                chunk3(c, False)
                assert pool3_done[1] == per
            pool3_done[0], pool3_done[1] = first_base + (CHUNKS - 2) * per + (per - 2), 0
            wo_tail((CHUNKS - 1) * BATCH - 1)
            chunk3(CHUNKS - 1, True)

            pool.wait_ge(added3, 4 * BLOCKS)
            nc.gpsimd.memset(tri[:], 1.0).then_inc(zeroed, 1)
            nc.gpsimd.memset(onesb[:], 1.0).then_inc(consts4, 1)
            nc.gpsimd.memset(carry[:], 0.0).then_inc(consts4, 1)
            nc.gpsimd.memset(quarter[:], 0.0).then_inc(zeroed, 1)
            root(9)
            pool.wait_ge(zeroed, 7)
            nc.gpsimd.affine_select(out=tri[:], in_=tri[:], compare_op=ALU.is_gt, fill=0.0, base=0,
                                    pattern=[[1, P]], channel_multiplier=-1).then_inc(consts4, 1)
            for j in range(4):
                pool.wait_ge(consts4, 3 + j)
                nc.gpsimd.memset(quarter[32 * j:32 * j + 32, j:j + 1], 1.0).then_inc(consts4, 1)

            pool.wait_ge(consts4, 7)

            def iota(o, pattern, mult):
                nc.gpsimd.iota(o, pattern=pattern, base=0, channel_multiplier=mult,
                               allow_small_or_imprecise_dtypes=True).then_inc(consts4, 1)

            iota(tokv[:, :, 0], [[0, TILES]], 1)
            iota(tokv[:, :, 1], [[P, TILES]], 0)
            nc.gpsimd.memset(tokv[:, :, 2:3], 1.0).then_inc(consts4, 1)
            nc.gpsimd.memset(tokv[:, :, 3:4], 0.0).then_inc(consts4, 1)
            iota(iota_t[:], [[1, P]], 0)
            iota(tbase[:], [[P, TILES]], 0)
            iota(capi[:], [[0, E1], [1, CAP]], 0)
            with pool.Fori(1, BATCH) as b:
                root(b + 9)
            pool.wait_ge(gidx_ready, 1)
            pool.wait_ge(rows_stored, 16 * BATCH)
            pool.wait_ge(down4, TILES)
            for s in range(GROUPS):
                nc.gpsimd.indirect_dma_start(out=xg[:, s, :], out_offset=None, in_=rows_dram,
                                             in_offset=bass.IndirectOffsetOnAxis(ap=gidx[:, s:s + 1], axis=0)).then_inc(gathered, 16)
            with pool.Fori(0, TILES // 2) as j:
                root(j + 13)

        @block.scalar
        def _(act):
            def copy(o, i):
                return nc.scalar.activation(o, i, ACT.Copy)

            def split_wq(g):
                act.wait_ge(wq_loaded, 16 * g + 16)
                copy(wq[0][:], wq_in[:]).then_inc(wq_hi, 1)

            def split_wk(g):
                act.wait_ge(wk_loaded, 16 * g + 16)
                copy(wk[0][:], wk_in[:]).then_inc(wk_hi, 1)

            for b in range(BATCH):
                for k in range(KD):
                    act.wait_ge(x_turned, 2 * b + k + 1)
                    copy(xT[0][:, k, b * T:(b + 1) * T], ps[:, 2 * b + k, :]).then_inc(xhi_ready, 1)
            act.wait_ge(wd_loaded, 16)
            copy(wd[0][:], wd_in[:]).then_inc(wd_hi, 1)
            for b in range(BATCH):
                act.wait_ge(c_ready, 2 * b + 1)
                copy(cT[0][:, b * T:(b + 1) * T], ps[:, b, :]).then_inc(chi_ready, 1)
                act.wait_ge(c_ready, 2 * b + 2)
                copy(c_tok[:, b * TPB:(b + 1) * TPB, :],
                     ps[:, 4 + b, :].rearrange("p (i l) -> p i l", i=TPB)).then_inc(ctok_ready, 1)
            split_wq(0)
            split_wk(0)
            for j in range(4):
                act.wait_ge(wv_turned, j + 1)
                copy(wvT[:, 4 * j:4 * j + 4, :], ps[:, j, :].rearrange("p (i l) -> p i l", i=4)).then_inc(wvT_ready, 1)
            for j in range(8):
                act.wait_ge(u_ready, j + 1)
                copy(U[:, 2 * j:2 * j + 2, :], ps[:, (4 + j) % 8, :].rearrange("p (i l) -> p i l", i=2)).then_inc(u_copied, 1)

            def step(g, n, first, last):
                s = g * STEPS + n
                start = first and n == 0
                hh = n % 2
                def exps(i):
                    act.wait_ge(negmax_ready, 4 * s + i + 1)
                    if not (first and n < 2) and i == 0:
                        act.wait_ge(transposed, 3 * s - 3)
                    off = P * (i * (i + 1) // 2)
                    nc.scalar.activation(probs[hh][:, off:off + (i + 1) * P], ps[:, BS + i % 2, 0:(i + 1) * P], ACT.Exp,
                                         bias=nm[:, hh, i:i + 1], scale=SCALE,
                                         accum_out=rs[:, hh, i:i + 1]).then_inc(probs_ready, 1)
                exps(0)
                exps(1)
                if not start:
                    act.wait_ge(pv_done, s)
                    copy(oT[:], ps[:, BO, :]).then_inc(ot_copied, 1)
                exps(2)
                exps(3)
                if n == 1 and not last:
                    act.wait_ge(proj_ready, s + 6)
                    split_wq(g + 1)
                if n == 2 and not last:
                    act.wait_ge(proj_ready, s + 6)
                    split_wk(g + 1)
                act.wait_ge(transposed, 3 * s + 1)
                if not start:
                    act.wait_ge(pv_done, s)
                copy(pT[:, 0, 0:2 * P], ps[:, BW + 2, 0:2 * P])
                copy(pT[:, 1, P:2 * P], ps[:, BW + 2, 2 * P:3 * P]).then_inc(pt_copied, 1)
                for i in (2, 3):
                    act.wait_ge(transposed, 3 * s + i)
                    copy(pT[:, 0:i + 1, i * P:(i + 1) * P],
                         ps[:, BW + i - 2, 0:(i + 1) * P].rearrange("p (k q) -> p k q", q=P)).then_inc(pt_copied, 1)

            def pair(g, first, last):
                for n in range(STEPS):
                    step(g, n, first, last)

            pair(0, True, False)
            with act.Fori(1, PAIRS - 1) as g:
                pair(g, False, False)
            pair(PAIRS - 1, False, True)
            act.wait_ge(pv_done, STEPS * PAIRS)
            copy(oT[:], ps[:, BO, :]).then_inc(ot_copied, 1)

            def x1_halves(b):
                for k in range(KD):
                    act.wait_ge(x1_turned, b * KD + (k + 1))
                    copy(x1T[0][:, k, :], ps[:, 4 + k, :]).then_inc(x1hi_ready, 1)

            def scores0(b):
                act.wait_ge(logits_ready, b + 1)
                nc.scalar.activation(sig[:].rearrange("p (k i) e -> p k i e", k=2),
                                     ps[:, 6:8, 0:2 * NA].rearrange("p k (i c) -> p k i c", i=2)[:, :, :, 0:E0],
                                     ACT.Sigmoid).then_inc(sig_ready, 1)

            def ffn0(b, last):
                for w in range(2):
                    act.wait_ge(xa_turned, b * 2 + (w + 1))
                    copy(xaT[0][:, w, :], ps[0:NL, 4 + w, :]).then_inc(xahi_ready, 1)
                for m, (f, size) in enumerate(F0S):
                    act.wait_ge(gate_ready, b * FT0 + (m + 1))
                    if m >= 2:
                        act.wait_ge(hid_ready, b * FT0 + (m - 1))
                    nc.scalar.activation(gated[m % 2][0:size, :], ps[0:size, m % 2, :], ACT.Silu).then_inc(gated_ready, 1)
                if not last:
                    x1_halves(b + 1)
                    scores0(b + 1)
                act.wait_ge(ha_turned, b + 1)
                copy(haT[:], ps[0:NL, 4, :]).then_inc(haT_ready, 1)
                act.wait_ge(x2_ready, b * TPB + TPB)
                t = bass.ds(b * TPB, TPB)
                copy(x2[0][:, t, :], acc[:, t, :]).then_inc(x2hi_ready, 1)

            act.wait_ge(gu_loaded, 32)
            act.wait_ge(proj_ready, 6 + STEPS * (PAIRS - 1) + 2)
            copy(gu[0][:], gu_in[:]).then_inc(w0_hi, 1)
            act.wait_ge(lb_loaded, 64)
            copy(lb[0][:], lb_in[:]).then_inc(w0_hi, 1)
            act.wait_ge(la_loaded, 8 * 16)
            copy(la[0][:], la_in[:]).then_inc(w0_hi, 1)
            x1_halves(0)
            scores0(0)
            with act.Fori(0, BATCH - 1) as b:
                ffn0(b, False)
            ffn0(BATCH - 1, True)

            def halve_wv3(c):
                act.wait_ge(wv3_loaded, 16 * c + 16)
                copy(wv3[0][:], wv3_in[:]).then_inc(wv3_hi, 1)

            def relu(o, i):
                return nc.scalar.activation(o, i, ACT.Relu)

            def keys(n, p):
                act.wait_ge(k_ready, 4 * n + (p + 1))
                if p == 0 and not (isinstance(n, int) and n == 0):
                    act.wait_ge(g_ready, 2 * n)
                    act.wait_ge(ksummed, 7 * n)
                relu(k3[0][:, p, :], ps[:, 1, :]).then_inc(khi_ready, 1)

            def grams(n):
                for k in range(KD):
                    act.wait_ge(g_ready, 2 * n + (k + 1))
                    if k == 0 and not (isinstance(n, int) and n == 0):
                        act.wait_ge(kv_ready, n)
                    copy(g3[0][:, k, :], ps[:, 2 + k, :]).then_inc(ghi_ready, 1)

            def turned(u):
                act.wait_ge(yt_ready, u + 1)
                if not (isinstance(u, int) and u == 0):
                    act.wait_ge(out3_ready, u)
                copy(yT3[0][:], ps[:, 3, :]).then_inc(ythi_ready, 1)

            def chunk3(c, first, last):
                for b in range(BATCH):
                    n = c * BATCH + b
                    for p in range(PPC):
                        u = c * (BATCH * PPC) + (b * PPC + p)
                        act.wait_ge(q_ready, u + 1)
                        if not (first and b == 0 and p == 0):
                            act.wait_ge(qkv_ready, u)
                        relu(q3[0][:], ps[:, 0, :]).then_inc(qhi_ready, 1)
                        if p == 0:
                            act.wait_ge(kv_ready, n + 1)
                            if not (first and b == 0):
                                act.wait_ge(qkv_ready, u)
                            for h in range(2):
                                r = slice(64 * h, 64 * h + 64)
                                copy(kvs[0][r, :, r], ps[r, 2, :].rearrange("p (j e) -> p j e", j=PPC)[:, :, r]).then_inc(kvhi_ready, 1)
                                copy(kvs[0][r, :, P + h], ps[r, 5, 0:PPC]).then_inc(kvhi_ready, 1)
                        if not (last and b == 3):
                            keys(n + 1, p)
                        if not (first and b == 0 and p == 0):
                            turned(u - 1)
                        if b == 3 and p == 1 and not last:
                            halve_wv3(c + 1)
                        if p == 3 and not (last and b == 3):
                            grams(n + 1)

            for b in range(BATCH):
                for k in range(KD):
                    act.wait_ge(x2_turned, b * KD + (k + 1))
                    copy(x2T[0][:, k, b * T:(b + 1) * T], ps[:, 2 * b + k, :]).then_inc(x2Thi_ready, 1)
            halve_wv3(0)
            for p in range(PPC):
                keys(0, p)
            grams(0)
            act.wait_ge(zeroed, 5)
            chunk3(0, True, False)
            with act.Fori(1, CHUNKS - 1) as c:
                chunk3(c, False, False)
            chunk3(CHUNKS - 1, False, True)
            turned(BLOCKS * PPC - 1)

            act.wait_ge(sw_loaded, 64)
            act.wait_ge(out3_ready, BLOCKS * PPC)
            copy(sw[0][:], sw_in[:]).then_inc(sw_hi, 1)
            act.wait_ge(gw_turned, 1)
            copy(gwT[0][:], ps[:, 0, 0:KD * E1].rearrange("p (k e) -> p k e", k=KD)).then_inc(sw_hi, 1)

            def route4(b):
                for k in range(KD):
                    act.wait_ge(x3_turned, b * KD + (k + 1))
                    copy(x3T[0][:, k, :], ps[:, 4 + k, :]).then_inc(x3hi_ready, 1)
                act.wait_ge(nmx4_ready, b + 1)
                for i in range(TPB):
                    nc.scalar.activation(e4[:, i, :], ps[:, 6, i * E1:(i + 1) * E1], ACT.Exp, bias=nmx4[:, i:i + 1],
                                         accum_out=sm4[:, i:i + 1]).then_inc(exp4, 1)
                for m, (f, size) in enumerate(F1T):
                    act.wait_ge(gate4_ready, b * FT1 + (m + 1))
                    wait_past(act, hid4_ready, b * FT1 + max(m - 1, 0))
                    nc.scalar.activation(gated4[m % 2][0:size, :], ps[0:size, m % 2, :], ACT.Silu).then_inc(gated4_ready, 1)

            route4(0)
            with act.Fori(1, BATCH) as b:
                route4(b)
            act.wait_ge(gathered, 16 * GROUPS)

            def weights(s):
                if not (isinstance(s, int) and s == 0):
                    act.wait_ge(xs_turned, s)
                copy(xs[:], xg[:, bass.ds(s, 1), 0:D]).then_inc(xs_ready, 1)

            def turned_rows(s, parity):
                act.wait_ge(xs_turned, s + 1)
                if not (isinstance(s, int) and s < 2):
                    act.wait_ge(gu4_ready, s - 1)
                copy(xsT[parity][:], ps[:, 0, 0:KD * P].rearrange("p (k n) -> p k n", k=KD)).then_inc(xsT_ready, 1)

            def gate(s, i):
                act.wait_ge(gu4_ready, s + 1)
                nc.scalar.activation(actE[:], ps[:, 1 + i % 2, 0:I1], ACT.Silu).then_inc(actE_ready, 1)

            def outputs4(s, i):
                act.wait_ge(y_mm, s + 1)
                nc.scalar.activation(y4[0][:, bass.ds(s, 1), :], ps[:, 4 + i % 2, 0:D], ACT.Copy,
                                     scale=wslot[:, bass.ds(s, 1)]).then_inc(yhi_ready, 1)

            def experts(s, i, first, left):
                act.wait_ge(hE_turned, s + 1)
                copy(hET[:], ps[0:IH, 3, 0:2 * P].rearrange("p (k n) -> p k n", k=2)).then_inc(hET_ready, 1)
                if left > 2:
                    turned_rows(s + 2, i % 2)
                if left > 3:
                    weights(s + 3)
                if not first:
                    outputs4(s - 1, i + 1)
                if left > 1:
                    gate(s + 1, i + 1)

            weights(0)
            turned_rows(0, 0)
            weights(1)
            turned_rows(1, 1)
            weights(2)
            gate(0, 0)
            act.wait_ge(wslot_ready, 1)
            for i in range(4):
                experts(i, i, i == 0, GROUPS - i)
            with act.Fori(1, GROUPS // 4 - 1) as it:
                for i in range(4):
                    experts(it * 4 + i, i, False, 5)
            for i in range(4):
                experts(GROUPS - 4 + i, i, False, 4 - i)
            outputs4(GROUPS - 1, 3)

        @block.vector
        def _(dve):
            def rest(o, whole, hi):
                return nc.vector.tensor_tensor(o, whole, hi.bitcast(F32), ALU.subtract)

            def split_wq(g):
                dve.wait_ge(wq_hi, g + 1)
                rest(wq[1][:], wq_in[:], wq[0][:]).then_inc(wq_lo, 1)

            def split_wk(g):
                dve.wait_ge(wk_hi, g + 1)
                rest(wk[1][:], wk_in[:], wk[0][:]).then_inc(wk_lo, 1)

            def products(idx, parity, early):
                dve.wait_ge(proj_ready, idx + 1)
                if not early:
                    dve.wait_ge(roped, 4 * idx - 4)
                for w in range(2):
                    nc.vector.tensor_tensor(prod[parity][w][:], ps[:, BA:BA + 2, :],
                                            rope[:, w:w + 1, :].broadcast_to([P, 2, T]), ALU.mult).then_inc(products_ready, 1)

            for b in range(BATCH):
                for k in range(KD):
                    dve.wait_ge(xhi_ready, 2 * b + k + 1)
                    rest(xT[1][:, k, b * T:(b + 1) * T], ps[:, 2 * b + k, :],
                         xT[0][:, k, b * T:(b + 1) * T]).then_inc(xlo_ready, 1)
            dve.wait_ge(wd_hi, 1)
            rest(wd[1][:], wd_in[:], wd[0][:]).then_inc(wd_lo, 1)
            for b in range(BATCH):
                dve.wait_ge(chi_ready, b + 1)
                rest(cT[1][:, b * T:(b + 1) * T], ps[:, b, :], cT[0][:, b * T:(b + 1) * T]).then_inc(clo_ready, 1)
            split_wq(0)
            split_wk(0)
            dve.wait_ge(wo_loaded, 32)
            for b in range(BATCH - 1):
                products(2 * b, 0, b == 0)
                products(2 * b + 1, 1, b == 0)

            def step(g, n, first, last):
                s = g * STEPS + n
                hh = n % 2
                def top(i):
                    dve.wait_ge(scores_ready, 4 * s + i + 1)
                    nc.vector.tensor_reduce(mx[:, hh, i:i + 1], ps[:, BS + i % 2, 0:(i + 1) * P], AX_X,
                                            ALU.max).then_inc(max_ready, 1)
                    dve.wait_ge(max_ready, 4 * s + i + 1)
                    nc.vector.tensor_scalar(nm[:, hh, i:i + 1], mx[:, hh, i:i + 1], -SCALE, None,
                                            ALU.mult).then_inc(negmax_ready, 1)
                top(0)
                top(1)
                if not (first and n == 0) and (n <= 2 or not last):
                    products(s + 5, (n + 1) % 2, False)
                top(2)
                top(3)
                if n == 1 and not last:
                    split_wq(g + 1)
                if n == 2 and not last:
                    split_wk(g + 1)
                if not (first and n == 0):
                    add(s - 1, (n - 1) % STEPS)
                dve.wait_ge(probs_ready, 4 * s + 4)
                nc.vector.reciprocal(rinv[:, hh, :], rs[:, hh, :]).then_inc(rinv_ready, 1)

            def add(s, n):
                b, hh = n // 2, n % 2
                dve.wait_ge(rinv_ready, s + 1)
                for i in range(TPB):
                    dve.wait_ge(out_ready, 2 * s + i // 2 + 1)
                    if i == 0 and (not isinstance(s, int) or s > 0):
                        dve.wait_ge(acc_added, 4 * s)
                    a = acc[:, b * TPB + i, :]
                    nc.vector.scalar_tensor_tensor(out=a, in0=ps[:, BW + i // 2, (i % 2) * D:(i % 2 + 1) * D],
                                                   scalar=rinv[:, hh, i:i + 1], in1=a,
                                                   op0=ALU.mult, op1=ALU.add).then_inc(acc_added, 1)

            def pair(g, first, last):
                for n in range(STEPS):
                    step(g, n, first, last)

            pair(0, True, False)
            with dve.Fori(1, PAIRS - 1) as g:
                pair(g, False, False)
            pair(PAIRS - 1, False, True)
            add(STEPS * PAIRS - 1, STEPS - 1)

            for n, (w, w_in) in enumerate(((gu, gu_in), (lb, lb_in), (la, la_in))):
                dve.wait_ge(w0_hi, n + 1)
                rest(w[1][:], w_in[:], w[0][:]).then_inc(w0_lo, 1)
            done = [0, 0]

            def link(ins):
                done[1] += 1
                return ins.then_inc(dchain, 1)

            def settle():
                dve.wait_ge(dchain, done[0] + done[1])

            def settle_by_memset():
                settle()
                nc.vector.memset(scratch[:], 0.0)

            def tiles(b):
                return [acc[:, bass.ds(b * TPB + i, 1), :] for i in range(TPB)]

            def statistics(tiles, n):
                nc.vector.memset(scratch[:], 0.0)
                for i, a in enumerate(tiles):
                    link(nc.vector.bn_stats(stat[:, i, :], a))
                settle_by_memset()
                for i in range(len(tiles)):
                    link(nc.vector.bn_aggr(meanvar[:, i, :], stat[:, i, :]))
                settle()
                nc.vector.tensor_scalar(vareps[:], meanvar[:, :, 1], EPS, None, ALU.add).then_inc(var_ready, 1)
                if n is not None:
                    dve.wait_ge(rstd_ready, n)

            def norm1(b, first):
                statistics(tiles(b), 1 if first else 2 * b)
                if not first:
                    dve.wait_ge(x1_turned, 2 * b)
                for i, a in enumerate(tiles(b)):
                    nc.vector.tensor_scalar(x1s[:, i, :], a, meanvar[:, i, 0:1], rstd[:, i:i + 1],
                                            ALU.subtract, ALU.mult).then_inc(x1_ready, 1)
                for i, a in enumerate(tiles(b)):
                    link(nc.vector.tensor_scalar(a, a, meanvar[:, i, 0:1], rstd[:, i:i + 1], ALU.subtract, ALU.mult))

            def x1_rests(b):
                for k in range(KD):
                    dve.wait_ge(x1hi_ready, b * KD + (k + 1))
                    rest(x1T[1][:, k, :], ps[:, 4 + k, :], x1T[0][:, k, :]).then_inc(x1lo_ready, 1)

            def route0(b):
                dve.wait_ge(sig_ready, b + 1)
                link(nc.vector.tensor_tensor(biased[:], sig[:], ebias[:].rearrange("p (a e) -> p a e", a=1).broadcast_to([P, TPB, E0]),
                                             ALU.add))
                settle_by_memset()
                for i in range(TPB):
                    link(nc.vector.max(top8[:, i, :], biased[:, i, :]))
                settle_by_memset()
                for i in range(TPB):
                    link(nc.vector.max_index(topi[:, i, :], top8[:, i, :], biased[:, i, :]))
                settle()
                link(nc.vector.tensor_copy(topf[:], topi[:]))
                settle()
                for n, o in enumerate((one0, one1)):
                    link(nc.vector.tensor_tensor(o[:], iota8[:, 0:E0].rearrange("p (a e) -> p a e", a=1).broadcast_to([P, TPB, E0]),
                                                 topf[:, :, n:n + 1].broadcast_to([P, TPB, E0]), ALU.is_equal))
                settle()
                link(nc.vector.tensor_tensor(one0[:], one0[:], one1[:], ALU.add))
                settle()
                link(nc.vector.tensor_tensor(picked[:], one0[:], sig[:], ALU.mult))
                settle()
                link(nc.vector.tensor_reduce(den[:], picked[:], AX_X, ALU.add))
                settle()
                link(nc.vector.tensor_scalar(den[:], den[:], 1e-8, float(R0), ALU.add, ALU.mult))
                settle()
                link(nc.vector.reciprocal(den[:], den[:]))
                settle()
                link(nc.vector.tensor_tensor(wexp[:, :, 1:1 + E0], picked[:],
                                             den[:].rearrange("p (i a) -> p i a", a=1).broadcast_to([P, TPB, E0]), ALU.mult))
                settle()
                for i in range(TPB):
                    w = wexp[:, i:i + 1, :].rearrange("p a (e r) -> p a e r", r=1).broadcast_to([P, 2, 1 + E0, R0])
                    nc.vector.tensor_tensor(
                        xa[:, i, :].rearrange("p (w e r) -> p w e r", w=2, r=R0),
                        ps[:, 6 + i // 2, (i % 2) * NA + E0:(i % 2 + 1) * NA].rearrange("p (w e r) -> p w e r", w=2, r=R0),
                        w, ALU.mult).then_inc(xa_ready, 1)

            def ffn0(b, last):
                for w in range(2):
                    dve.wait_ge(xahi_ready, b * 2 + (w + 1))
                    rest(xaT[1][:, w, :], ps[0:NL, 4 + w, :], xaT[0][:, w, :]).then_inc(xalo_ready, 1)
                for m, (f, size) in enumerate(F0S):
                    dve.wait_ge(gated_ready, b * FT0 + (m + 1))
                    if m == 0 and not (isinstance(b, int) and b == 0):
                        wait_past(dve, down_ready, b * TPB)
                    nc.vector.tensor_tensor(hidT[0:size, m, :], gated[m % 2][0:size, :], ps[0:size, 2 + m % 2, :],
                                            ALU.mult).then_inc(hid_ready, 1)
                    if m == 1 and not last:
                        norm1(b + 1, False)
                if not last:
                    x1_rests(b + 1)
                for i in range(TPB):
                    dve.wait_ge(down_ready, b * TPB + (i + 1))
                    nc.vector.tensor_tensor(ha[:, i, :].rearrange("p (e r) -> p e r", r=R0),
                                            ps[:, i, D:D + NL].rearrange("p (e r) -> p e r", r=R0),
                                            wexp[:, i, :].rearrange("p (e r) -> p e r", r=1).broadcast_to([P, 1 + E0, R0]),
                                            ALU.mult).then_inc(ha_ready, 1)
                if not last:
                    route0(b + 1)
                for i, a in enumerate(tiles(b)):
                    dve.wait_ge(ffn_ready, b * TPB + (i + 1))
                    nc.vector.tensor_tensor(a, a, ps[:, i:i + 1, 0:D], ALU.add).then_inc(ffn_added, 1)
                dve.wait_ge(ffn_added, b * TPB + TPB)
                statistics(tiles(b), 2 * BATCH if last else 2 * b + 3)
                for i, a in enumerate(tiles(b)):
                    nc.vector.tensor_scalar(a, a, meanvar[:, i, 0:1], rstd[:, i:i + 1],
                                            ALU.subtract, ALU.mult).then_inc(x2_ready, 1)

            dve.wait_ge(la_loaded, 8 * 16)
            dve.wait_ge(acc_added, 4 * STEPS * PAIRS)
            link(nc.vector.memset(wexp[:], 1.0 / R0))
            norm1(0, True)
            x1_rests(0)
            route0(0)
            before = done[1]
            done[0], done[1] = before, 0
            ffn0(0, False)
            with dve.Fori(1, BATCH - 1) as b:
                done[0], done[1] = b * LINKS0 + before, 0
                ffn0(b, False)
                assert done[1] == LINKS0, done
            done[0], done[1] = before + LINKS0 * (BATCH - 1), 0
            ffn0(BATCH - 1, True)

            def relu_rest(o, whole, hi):
                return nc.vector.scalar_tensor_tensor(out=o, in0=whole, scalar=0.0, in1=hi.bitcast(F32),
                                                      op0=ALU.max, op1=ALU.subtract)

            def halve_wv3(c):
                dve.wait_ge(wv3_hi, c + 1)
                rest(wv3[1][:], wv3_in[:], wv3[0][:]).then_inc(wv3_lo, 1)

            def keys(n, p):
                dve.wait_ge(khi_ready, 4 * n + (p + 1))
                relu_rest(k3[1][:, p, :], ps[:, 1, :], k3[0][:, p, :]).then_inc(klo_ready, 1)

            def grams(n):
                for k in range(KD):
                    dve.wait_ge(ghi_ready, 2 * n + (k + 1))
                    rest(g3[1][:, k, :], ps[:, 2 + k, :], g3[0][:, k, :]).then_inc(glo_ready, 1)

            def turned(u):
                dve.wait_ge(ythi_ready, u + 1)
                rest(yT3[1][:], ps[:, 3, :], yT3[0][:]).then_inc(ytlo_ready, 1)

            def add3(n, b, first):
                for i in range(TPB):
                    a = acc[:, b * TPB + i, :]
                    dve.wait_ge(out3_ready, 4 * n + 4)
                    nc.vector.tensor_tensor(a, a, ps[:, 6 + i // 2, (i % 2) * D:(i % 2 + 1) * D], ALU.add).then_inc(added3, 1)

            def chunk3(c, first, last):
                for b in range(BATCH):
                    n = c * BATCH + b
                    for p in range(PPC):
                        u = c * (BATCH * PPC) + (b * PPC + p)
                        dve.wait_ge(qhi_ready, u + 1)
                        relu_rest(q3[1][:], ps[:, 0, :], q3[0][:]).then_inc(qlo_ready, 1)
                        if p == 1 and not (first and b == 0):
                            add3(n - 1, (b - 1) % BATCH, first or (b == 0 and False))
                        if p == 0:
                            dve.wait_ge(kvhi_ready, 4 * n + 4)
                            for h in range(2):
                                r = slice(64 * h, 64 * h + 64)
                                rest(kvs[1][r, :, r], ps[r, 2, :].rearrange("p (j e) -> p j e", j=PPC)[:, :, r],
                                     kvs[0][r, :, r]).then_inc(kvlo_ready, 1)
                                rest(kvs[1][r, :, P + h], ps[r, 5, 0:PPC], kvs[0][r, :, P + h]).then_inc(kvlo_ready, 1)
                        if not (last and b == 3):
                            keys(n + 1, p)
                        if not (first and b == 0 and p == 0):
                            turned(u - 1)
                        dve.wait_ge(qkv_ready, u + 1)
                        both = ps[:, 4:6, 0:2 * (P + 2)].rearrange("p k (i e) -> p k i e", i=2)
                        nc.vector.tensor_scalar(nrm[:], both[:, :, :, P:P + 2], 1e-6, None, ALU.max).then_inc(norm_ready, 1)
                        dve.wait_ge(norm_ready, 2 * u + 1)
                        nc.vector.reciprocal(rnm[:], nrm[:].rearrange("p k i h -> p (k i) h")).then_inc(norm_ready, 1)
                        dve.wait_ge(norm_ready, 2 * u + 2)
                        if not (first and b == 0 and p == 0):
                            dve.wait_ge(yt_ready, u)
                        for k in range(2):
                            nc.vector.tensor_tensor(
                                y3[:, 2 * k:2 * k + 2, :].rearrange("p i (h e) -> p i h e", h=2),
                                both[:, k, :, 0:P].rearrange("p i (h e) -> p i h e", h=2),
                                rnm[:, 2 * k:2 * k + 2, :].rearrange("p i (h a) -> p i h a", a=1).broadcast_to([P, 2, 2, 64]),
                                ALU.mult).then_inc(y_ready, 1)
                        if b == 3 and p == 1 and not last:
                            halve_wv3(c + 1)
                        if p == 3 and not (last and b == 3):
                            grams(n + 1)

            for b in range(BATCH):
                for k in range(KD):
                    dve.wait_ge(x2Thi_ready, b * KD + (k + 1))
                    rest(x2T[1][:, k, b * T:(b + 1) * T], ps[:, 2 * b + k, :],
                         x2T[0][:, k, b * T:(b + 1) * T]).then_inc(x2Tlo_ready, 1)
            halve_wv3(0)
            for p in range(PPC):
                keys(0, p)
            grams(0)
            dve.wait_ge(bo_loaded, 16)
            dve.wait_ge(x2lo_ready, BATCH)
            for b in range(BATCH):
                r = acc[:, b * TPB:(b + 1) * TPB, :]
                link(nc.vector.tensor_tensor(r, r, bo_sb[:].rearrange("p (a n) -> p a n", a=1).broadcast_to([P, TPB, D]), ALU.add))
            settle()
            dve.wait_ge(zeroed, 5)
            chunk3(0, True, False)
            with dve.Fori(1, CHUNKS - 1) as c:
                chunk3(c, False, False)
            chunk3(CHUNKS - 1, False, True)
            turned(BLOCKS * PPC - 1)
            add3(BLOCKS - 1, BATCH - 1, False)

            dve.wait_ge(sw_hi, 1)
            rest(sw[1][:], sw_in[:], sw[0][:]).then_inc(sw_lo, 1)
            dve.wait_ge(sw_hi, 2)
            rest(gwT[1][:], ps[:, 0, 0:KD * E1].rearrange("p (k e) -> p k e", k=KD), gwT[0][:]).then_inc(sw_lo, 1)
            link(nc.vector.memset(slots[:], 0.0))
            dve.wait_ge(added3, 4 * BLOCKS)
            settle()

            def hidden4(b, m):
                f, size = F1T[m]
                dve.wait_ge(gated4_ready, b * FT1 + (m + 1))
                nc.vector.tensor_tensor(hid4[0:size, m, :], gated4[m % 2][0:size, :], ps[0:size, 2 + m % 2, :],
                                        ALU.mult).then_inc(hid4_ready, 1)

            def bcast(ap, shape):
                return ap.broadcast_to(shape)

            def route4(b):
                statistics(tiles(b), b + 9)
                wait_past(dve, rows_stored, 16 * b)
                for i, a in enumerate(tiles(b)):
                    nc.vector.tensor_scalar(rows[:, i, 0:D], a, meanvar[:, i, 0:1], rstd[:, i:i + 1],
                                            ALU.subtract, ALU.mult).then_inc(x3_ready, 1)
                for i, a in enumerate(tiles(b)):
                    link(nc.vector.tensor_scalar(a, a, meanvar[:, i, 0:1], rstd[:, i:i + 1], ALU.subtract, ALU.mult))
                for k in range(KD):
                    dve.wait_ge(x3hi_ready, b * KD + (k + 1))
                    rest(x3T[1][:, k, :], ps[:, 4 + k, :], x3T[0][:, k, :]).then_inc(x3lo_ready, 1)
                dve.wait_ge(logits4, b + 1)
                link(nc.vector.tensor_reduce(mx4[:], ps[:, 6, 0:TPB * E1].rearrange("p (i e) -> p i e", i=TPB), AX_X, ALU.max))
                settle()
                nc.vector.tensor_scalar(nmx4[:], mx4[:], -1.0, None, ALU.mult).then_inc(nmx4_ready, 1)
                dve.wait_ge(exp4, b * TPB + TPB)
                link(nc.vector.reciprocal(sm4[:], sm4[:]))
                settle()
                nc.vector.tensor_tensor(rows[:, :, D:ROW], e4[:], bcast(sm4[:].rearrange("p (i a) -> p i a", a=1), [P, TPB, E1]),
                                        ALU.mult).then_inc(scored, 1)
                dve.wait_ge(scored, b + 1)
                nc.vector.memset(scratch[:], 0.0)
                for i in range(TPB):
                    link(nc.vector.max(top4[:, i, :], rows[:, i, D:ROW]))
                settle_by_memset()
                for i in range(TPB):
                    link(nc.vector.max_index(top4i[:, i, :], top4[:, i, :], rows[:, i, D:ROW]))
                settle()
                link(nc.vector.tensor_copy(top4f[:], top4i[:]))
                hidden4(b, 0)
                for k in range(TOP1):
                    settle()
                    for i in range(TPB):
                        which = top4f[:, i, k:k + 1]
                        if k == 0:
                            ins = nc.vector.tensor_scalar(sel[:, i, :], iota8[:], which, None, ALU.is_equal)
                        else:
                            ins = nc.vector.scalar_tensor_tensor(out=sel[:, i, :], in0=iota8[:], scalar=which, in1=sel[:, i, :],
                                                                 op0=ALU.is_equal, op1=ALU.add)
                        if k < TOP1 - 1:
                            link(ins)
                        else:
                            ins.then_inc(sel_ready, 1)
                dve.wait_ge(sel_ready, b * TPB + TPB)
                link(nc.vector.tensor_scalar(pm[:], sel[:], -2.0 * CAP, 2.0 * CAP, ALU.mult, ALU.add))
                link(nc.vector.tensor_reduce(selsum[:], sel[:].rearrange("p i e -> p e i"), AX_X, ALU.add))
                hidden4(b, 1)
                hidden4(b, 2)
                dve.wait_ge(pos_ready, b + 1)
                settle()
                link(nc.vector.scalar_tensor_tensor(out=posb[:].rearrange("p i e -> p (i e)"), in0=ps[:, 7, 0:TPB * E1], scalar=float(CAP),
                                                    in1=pm[:].rearrange("p i e -> p (i e)"), op0=ALU.min, op1=ALU.add))
                nc.vector.tensor_tensor(carry[:], carry[:], selsum[:], ALU.add).then_inc(carry_ready, 1)
                settle()
                for i in range(TPB):
                    if i >= 2:
                        dve.wait_ge(onehot_used, b * TPB + (i - 1))
                    nc.vector.tensor_tensor(onehot[i % 2][:], bcast(posb[:, i, :].rearrange("p (e a) -> p e a", a=1), [P, E1, CAP]), capi[:],
                                            ALU.is_equal).then_inc(onehot_ready, 1)
                for i, a in enumerate(tiles(b)):
                    dve.wait_ge(down4, b * TPB + (2 if i < 2 else 4))
                    nc.vector.tensor_tensor(a, a, ps[:, 4 + i // 2, (i % 2) * D:(i % 2 + 1) * D].rearrange("p (a n) -> p a n", a=1),
                                            ALU.add).then_inc(added4, 1)
                dve.wait_ge(onehot_used, b * TPB + TPB)
                flat = slots[:].rearrange("p s c -> p (s c)")
                nc.vector.tensor_tensor(flat, flat, ps[:, 6, 0:4 * GROUPS], ALU.add).then_inc(slots_added, 1)
                dve.wait_ge(slots_added, b + 1)

            before4 = done[0] + done[1]
            done[0], done[1] = before4, 0
            route4(0)
            with dve.Fori(1, BATCH) as b:
                done[0], done[1] = b * LINKS4 + before4, 0
                route4(b)
                assert done[1] == LINKS4, done
            done[0], done[1] = before4 + LINKS4 * BATCH, 0
            link(nc.vector.scalar_tensor_tensor(out=idxf[:], in0=slots[:, :, 0], scalar=-1.0, in1=slots[:, :, 1],
                                                op0=ALU.add, op1=ALU.add))
            settle()
            link(nc.vector.tensor_tensor(idxf[:], idxf[:], slots[:, :, 2], ALU.add))
            settle()
            nc.vector.tensor_scalar(gidx[:], idxf[:], 0.0, None, ALU.max).then_inc(gidx_ready, 1)
            dve.wait_ge(gathered, 16 * GROUPS)
            for s in range(GROUPS):
                link(nc.vector.tensor_tensor(wtmp[:, s, :], xg[:, s, D + 4 * s:D + 4 * s + 4], quarter[:], ALU.mult))
            settle()
            nc.vector.tensor_reduce(wslot[:], wtmp[:], AX_X, ALU.add).then_inc(wslot_ready, 1)
            dve.wait_ge(wslot_ready, 1)

            def pick_tokens(t, buf):
                nc.vector.scalar_tensor_tensor(
                    out=pick[buf][:], in0=bcast(iota_t[:].rearrange("p (a n) -> p a n", a=1), [P, GROUPS, P]),
                    scalar=tbase[:, bass.ds(t, 1)], in1=bcast(idxf[:].rearrange("p (s a) -> p s a", a=1), [P, GROUPS, P]),
                    op0=ALU.add, op1=ALU.is_equal).then_inc(pick_ready, 1)

            def hidden_rows(s, i):
                dve.wait_ge(actE_ready, s + 1)
                nc.vector.tensor_tensor(hE[:], actE[:], ps[:, 1 + i % 2, I1:2 * I1], ALU.mult).then_inc(hE_ready, 1)

            def rest_of_outputs(s, i):
                dve.wait_ge(yhi_ready, s + 1)
                at = bass.ds(s, 1)
                nc.vector.scalar_tensor_tensor(out=y4[1][:, at, :].rearrange("p a n -> p (a n)"), in0=ps[:, 4 + i % 2, 0:D],
                                               scalar=wslot[:, at], in1=y4[0][:, at, :].rearrange("p a n -> p (a n)").bitcast(F32),
                                               op0=ALU.mult, op1=ALU.subtract).then_inc(ylo_ready, 1)

            pick_tokens(0, 0)
            pick_tokens(1, 1)
            hidden_rows(0, 0)
            hidden_rows(1, 1)
            for i in range(1, 4):
                rest_of_outputs(i - 1, i + 1)
                hidden_rows(i + 1, i + 1)
            with dve.Fori(1, GROUPS // 4 - 1) as it:
                for i in range(4):
                    rest_of_outputs(it * 4 + i - 1, i + 1)
                    hidden_rows(it * 4 + (i + 1), i + 1)
            for i in range(4):
                rest_of_outputs(GROUPS - 5 + i, i + 1)
                if i < 3:
                    hidden_rows(GROUPS - 3 + i, i + 1)
            rest_of_outputs(GROUPS - 1, 3)

            def pair_of(j):
                return [acc[:, bass.ds(2 * j + i, 1), :] for i in range(2)]

            def normalise(j):
                dve.wait_ge(rstd_ready, j + 13)
                wait_past(dve, stored, 16 * j)
                for i, a in enumerate(pair_of(j)):
                    nc.vector.tensor_scalar(fin[:, i, :], a, meanvar[:, i, 0:1], rstd[:, i:i + 1],
                                            ALU.subtract, ALU.mult).then_inc(fin_ready, 1)

            def combine(j, first, last):
                pair = pair_of(j)
                for i, a in enumerate(pair):
                    t = 2 * j + i
                    dve.wait_ge(comb_ready, t + 1)
                    if not last:
                        pick_tokens(t + 2, i)
                    nc.vector.tensor_tensor(a, a, ps[:, 6 + i, 0:D].rearrange("p (a n) -> p a n", a=1), ALU.add).then_inc(comb_added, 1)
                    if i == 0 and not first:
                        normalise(j - 1)
                dve.wait_ge(comb_added, 2 * j + 2)
                statistics(pair, None)

            before5 = done[0] + done[1]
            done[0], done[1] = before5, 0
            combine(0, True, False)
            done[0], done[1] = before5 + 4, 0
            combine(1, False, False)
            with dve.Fori(2, TILES // 2 - 1) as j:
                done[0], done[1] = j * 4 + before5, 0
                combine(j, False, False)
                assert done[1] == 4, done
            done[0], done[1] = before5 + 4 * (TILES // 2 - 1), 0
            combine(TILES // 2 - 1, False, True)
            normalise(TILES // 2 - 1)

        @block.tensor
        def _(pe):
            def mm3(o, lhs, rhs, start, stop):
                for j, (a, c) in enumerate(HALVES):
                    last = pe.matmul(o, lhs(a), rhs(c), start=start and j == 0, stop=stop and j == 2)
                return last

            pe.wait_ge(consts_ready, 6)
            for b in range(BATCH):
                pe.wait_ge(x_in[b], 16)
                for k in range(KD):
                    for i in range(TPB):
                        last = pe.transpose(ps[:, 2 * b + k, i * P:(i + 1) * P],
                                            acc[:, b * TPB + i, k * P:(k + 1) * P], ident[:])
                    last.then_inc(x_turned, 1)
            pe.wait_ge(wd_lo, 1)
            for b in range(BATCH):
                pe.wait_ge(xlo_ready, 8 if b else 8)
                for k in range(KD):
                    last = mm3(ps[:, b, :], lambda a: wd[a][:, k, :],
                               lambda c: xT[c][:, k, b * T:(b + 1) * T], k == 0, k == KD - 1)
                last.then_inc(c_ready, 1)
                for i in range(TPB):
                    t0 = b * T + i * P
                    for k in range(KD):
                        last = mm3(ps[:, 4 + b, i * P:(i + 1) * P], lambda a: xT[a][:, k, t0:t0 + P],
                                   lambda c: wd[c][:, k, :], k == 0, k == KD - 1)
                last.then_inc(c_ready, 1)
            pe.wait_ge(wv_loaded, 16)
            pe.wait_ge(clo_ready, 4)
            for j in range(4):
                for i in range(4):
                    last = pe.transpose(ps[:, j, i * P:(i + 1) * P], wv[:, 4 * j + i, :], ident[:])
                last.then_inc(wv_turned, 1)
            pe.wait_ge(wo_loaded, 32)
            pe.wait_ge(ctok_ready, 4)
            for j in range(8):
                pe.wait_ge(wvT_ready, 4 if j >= 4 else j // 2 + 1)
                for i in range(2):
                    last = pe.matmul(ps[:, (4 + j) % 8, i * D:(i + 1) * D], wvT[:, 2 * j + i, :], wo[:, 2 * j + i, :],
                                     start=True, stop=True)
                last.then_inc(u_ready, 1)

            def project(which, b, idx, g):
                if not (isinstance(idx, int) and idx == 0):
                    pe.wait_ge(products_ready, 2 * idx)
                pe.wait_ge(wq_lo if which == 0 else wk_lo, g + 1)
                t = slice(b * T, (b + 1) * T)
                for half in range(2):
                    o = ps[:, BA + half, :]
                    if which == 0:
                        for k in range(KD):
                            last = mm3(o, lambda a: wq[a][:, k, half:2 * DH:2], lambda c: xT[c][:, k, t], k == 0, k == KD - 1)
                    else:
                        last = mm3(o, lambda a: wk[a][:, half:2 * DH:2], lambda c: cT[c][:, t], True, True)
                last.then_inc(proj_ready, 1)

            pe.wait_ge(u_copied, 8)
            for b in range(BATCH - 1):
                for w in range(2):
                    project(w, b, 2 * b + w, 0)

            def pv_and(s, n):
                b = n // 2
                pe.wait_ge(pt_copied, 3 * s + 3)
                if not isinstance(s, int) or s > 0:
                    pe.wait_ge(ot_copied, s)
                for k in range(TPB):
                    last = pe.matmul(ps[:, BO, k * P:T], c_tok[:, b * TPB + k, :], pT[:, k, k * P:T],
                                     start=k == 0, stop=k == TPB - 1)
                last.then_inc(pv_done, 1)

            def project_out(s, g, n):
                pe.wait_ge(ot_copied, s + 1)
                for i in range(TPB):
                    last = pe.matmul(ps[:, BW + i // 2, (i % 2) * D:(i % 2 + 1) * D], oT[:, i * P:(i + 1) * P],
                                     U[:, bass.ds(2 * g + n % 2, 1), :], start=True, stop=True)
                    if i % 2:
                        last.then_inc(out_ready, 1)

            def step(g, n, first, last_pair):
                s = g * STEPS + n
                b, hh = n // 2, n % 2
                before = (s - 1, g if n else g - 1, (n - 1) % STEPS)

                def scores(i):
                    if not (first and n == 0 and i < 2):
                        pe.wait_ge(probs_ready, 4 * s + i - 1)
                    bank = BS + i % 2
                    pe.matmul(ps[:, bank, 0:(i + 1) * P], qT[:, hh, b, i * P:(i + 1) * P], kT[:, hh, b, 0:(i + 1) * P],
                              start=True, stop=False)
                    pe.matmul(ps[:, bank, i * P:(i + 1) * P], identb[:], maskb[:],
                              start=False, stop=True).then_inc(scores_ready, 1)

                pe.wait_ge(roped, g * (4 * STEPS) + 4 * (2 * b + 2))
                scores(0)
                scores(1)
                if not (first and n == 0):
                    pv_and(before[0], before[2])
                scores(2)
                scores(3)
                if not (first and n == 0):
                    project_out(*before)
                if n < 2 or not last_pair:
                    project(n % 2, (3, 0, 1, 2)[n // 2], s + 6, g if n < 2 else g + 1)
                for i in range(TPB):
                    pe.wait_ge(probs_ready, 4 * s + i + 1)
                    if not (first and n == 0):
                        if i == 0:
                            pe.wait_ge(pt_copied, 3 * s - 2)
                        if i >= 2:
                            pe.wait_ge(acc_added, 4 * s - 4 + 2 * (i - 1))
                    bank = BW + (2, 2, 0, 1)[i]
                    for k in range(i + 1):
                        at = k if i != 1 else k + 1
                        off = P * (i * (i + 1) // 2 + k)
                        last = pe.transpose(ps[:, bank, at * P:(at + 1) * P], probs[hh][:, off:off + P], ident[:])
                    if i:
                        last.then_inc(transposed, 1)

            def pair(g, first, last):
                for n in range(STEPS):
                    step(g, n, first, last)

            pair(0, True, False)
            with pe.Fori(1, PAIRS - 1) as g:
                pair(g, False, False)
            pair(PAIRS - 1, False, True)
            pv_and(STEPS * PAIRS - 1, STEPS - 1)
            project_out(STEPS * PAIRS - 1, PAIRS - 1, STEPS - 1)

            def turn_x1(b, first):
                pe.wait_ge(x1_ready, b * TPB + TPB)
                if first:
                    pe.wait_ge(pt_copied, 3 * STEPS * PAIRS)
                    pe.wait_ge(acc_added, 4 * STEPS * PAIRS)
                else:
                    pe.wait_ge(xalo_ready, b * 2)
                for k in range(KD):
                    for i in range(TPB):
                        last = pe.transpose(ps[:, 4 + k, i * P:(i + 1) * P], x1s[:, i, k * P:(k + 1) * P], ident[:])
                    last.then_inc(x1_turned, 1)

            def first_products(b, first):
                pe.wait_ge(x1lo_ready, b * KD + KD)
                if not first:
                    pe.wait_ge(xa_ready, b * TPB)
                for i in range(TPB):
                    for k in range(KD):
                        last = mm3(ps[:, 6 + i // 2, (i % 2) * NA:(i % 2 + 1) * NA],
                                   lambda a: x1T[a][:, k, i * P:(i + 1) * P], lambda c: la[c][:, k, :], k == 0, k == KD - 1)
                last.then_inc(logits_ready, 1)

            def ffn0(b, first, last_one):
                def base(m, w):
                    f, size = F0S[m]
                    for k in range(KD):
                        mm3(ps[0:size, 2 * w + m % 2, :], lambda a: gu[a][:, k, w, f:f + size],
                            lambda c: x1T[c][:, k, :], k == 0, False)

                def lora(m, w):
                    f, size = F0S[m]
                    last = mm3(ps[0:size, 2 * w + m % 2, :], lambda a: lb[a][:, w, f:f + size],
                               lambda c: xaT[c][:, w, :], False, True)
                    if w:
                        last.then_inc(gate_ready, 1)

                if not first:
                    pe.wait_ge(ffn_added, b * TPB)
                for m in range(2):
                    for w in range(2):
                        base(m, w)
                pe.wait_ge(xa_ready, b * TPB + TPB)
                for w in range(2):
                    if w == 0:
                        pe.wait_ge(x1lo_ready, b * KD + KD)
                        if not first:
                            pe.wait_ge(haT_ready, b)
                    for i in range(TPB):
                        last = pe.transpose(ps[0:NL, 4 + w, i * P:(i + 1) * P], xa[:, i, w * NL:(w + 1) * NL], ident[:])
                    last.then_inc(xa_turned, 1)
                pe.wait_ge(xalo_ready, b * 2 + 2)
                for m in range(FT0):
                    if m >= 2:
                        pe.wait_ge(hid_ready, b * FT0 + (m - 1))
                        for w in range(2):
                            base(m, w)
                    for w in range(2):
                        lora(m, w)
                if not last_one:
                    turn_x1(b + 1, False)
                    first_products(b + 1, False)
                pe.wait_ge(hid_ready, b * FT0 + FT0)
                for i in range(TPB):
                    for m, (f, size) in enumerate(F0S):
                        last = pe.matmul(ps[:, i, 0:D + NL], hidT[0:size, m, i * P:(i + 1) * P], dn[0:size, m, :],
                                         start=m == 0, stop=m == FT0 - 1)
                    last.then_inc(down_ready, 1)
                pe.wait_ge(ha_ready, b * TPB + TPB)
                for i in range(TPB):
                    last = pe.transpose(ps[0:NL, 4, i * P:(i + 1) * P], ha[:, i, :], ident[:])
                last.then_inc(ha_turned, 1)
                pe.wait_ge(haT_ready, b + 1)
                for i in range(TPB):
                    pe.matmul(ps[:, i, 0:D], haT[:, i * P:(i + 1) * P], ldn[:], start=False, stop=True,
                              skip_group_check=True).then_inc(ffn_ready, 1)

            turn_x1(0, True)
            pe.wait_ge(w0_lo, 3)
            first_products(0, True)
            pe.wait_ge(dn_loaded, 12 * 16)
            ffn0(0, True, False)
            with pe.Fori(1, BATCH - 1) as b:
                ffn0(b, False, False)
            ffn0(BATCH - 1, False, True)

            def queries(u, b, p):
                if not (isinstance(u, int) and u == 0):
                    pe.wait_ge(qlo_ready, u)
                j = slice(p * P, (p + 1) * P)
                for k in range(KD):
                    last = mm3(ps[:, 0, :], lambda a: wq3[a][:, k, j], lambda c: x2T[c][:, k, b * T:(b + 1) * T],
                               k == 0, k == KD - 1)
                last.then_inc(q_ready, 1)

            def keys(n, c, b, p):
                if not (isinstance(n, int) and n == 0 and p == 0):
                    pe.wait_ge(klo_ready, 4 * n + p)
                t0 = b * T + p * P
                for k in range(KD):
                    last = mm3(ps[:, 1, :], lambda a: x2T[a][:, k, t0:t0 + P],
                               lambda h: wk3[h][:, bass.ds(c, 1), k, :], k == 0, k == KD - 1)
                last.then_inc(k_ready, 1)

            def grams(n, b):
                pe.wait_ge(klo_ready, 4 * n + 4)
                for k in range(KD):
                    if not (isinstance(n, int) and n == 0):
                        if k == 0:
                            pe.wait_ge(kvlo_ready, 4 * n)
                        else:
                            pe.wait_ge(ytlo_ready, 4 * n - 1)
                    for i in range(TPB):
                        last = mm3(ps[:, 2 + k, :], lambda a: x2[a][:, b * TPB + i, k * P:(k + 1) * P],
                                   lambda c: k3[c][:, i, :], i == 0, i == TPB - 1)
                    last.then_inc(g_ready, 1)

            def key_values(n):
                pe.wait_ge(glo_ready, 2 * n + 2)
                for p in range(PPC):
                    j = slice(p * P, (p + 1) * P)
                    for k in range(KD):
                        mm3(ps[:, 2, j], lambda a: g3[a][:, k, j], lambda c: wv3[c][:, k, j], k == 0, k == KD - 1)
                pe.wait_ge(ksummed, 7 * n + 7)
                if not (isinstance(n, int) and n == 0):
                    pe.wait_ge(y_ready, 8 * n)
                for p in range(PPC):
                    last = pe.matmul(ps[:, 5, p:p + 1], ks4[:, p * P:(p + 1) * P], ones[:], start=True, stop=True)
                last.then_inc(kv_ready, 1)

            def turn(u):
                pe.wait_ge(y_ready, 2 * u + 2)
                if not (isinstance(u, int) and u == 0):
                    pe.wait_ge(ytlo_ready, u)
                for i in range(TPB):
                    last = pe.transpose(ps[:, 3, i * P:(i + 1) * P], y3[:, i, :], ident[:])
                last.then_inc(yt_ready, 1)

            def query_values(u, n, p):
                pe.wait_ge(qlo_ready, u + 1)
                pe.wait_ge(kvlo_ready, 4 * n + 4)
                if not (isinstance(u, int) and u == 0):
                    pe.wait_ge(y_ready, 2 * u)
                for i in range(TPB):
                    last = mm3(ps[:, 4 + i // 2, (i % 2) * (P + 2):(i % 2 + 1) * (P + 2)],
                               lambda a: q3[a][:, i * P:(i + 1) * P], lambda c: kvs[c][:, p, :], True, True)
                last.then_inc(qkv_ready, 1)

            def outputs(u, n, p, c):
                pe.wait_ge(ytlo_ready, u + 1)
                pe.wait_ge(wo3_ready, c * PPC + (p + 1))
                if p == 0 and not (isinstance(n, int) and n == 0):
                    pe.wait_ge(added3, 4 * n)
                for i in range(TPB):
                    for j, (a, h) in enumerate(HALVES):
                        last = pe.matmul(ps[:, 6 + i // 2, (i % 2) * D:(i % 2 + 1) * D], yT3[a][:, i * P:(i + 1) * P],
                                         wo3[h][:, p, :], start=p == 0 and j == 0 and i % 2 == 0,
                                         stop=p == PPC - 1 and j == 2, skip_group_check=True)
                last.then_inc(out3_ready, 1)

            def chunk3(c, first, last):
                for b in range(BATCH):
                    n = c * BATCH + b
                    for p in range(PPC):
                        u = c * (BATCH * PPC) + (b * PPC + p)
                        pe.wait_ge(wq3_ready, c * PPC + (p + 1))
                        queries(u, b, p)
                        if not (first and b == 0 and p < 2):
                            back = b * PPC + p - 2
                            outputs(u - 2, c * BATCH + back // PPC, back % PPC, c if back >= 0 else c - 1)
                        if p == 0:
                            pe.wait_ge(wv3_lo, c + 1)
                            key_values(n)
                        if not (last and b == 3):
                            if b == 3:
                                pe.wait_ge(wk3_ready, c + 2)
                            keys(n + 1, c if b < 3 else c + 1, (b + 1) % BATCH, p)
                        if not (first and b == 0 and p == 0):
                            turn(u - 1)
                        query_values(u, n, p)
                        if p == 3 and not (last and b == 3):
                            grams(n + 1, (b + 1) % BATCH)

            pe.wait_ge(ffn_added, TILES)
            for b in range(BATCH):
                pe.wait_ge(x2_ready, b * TPB + TPB)
                for k in range(KD):
                    for i in range(TPB):
                        last = pe.transpose(ps[:, 2 * b + k, i * P:(i + 1) * P],
                                            acc[:, b * TPB + i, k * P:(k + 1) * P], ident[:])
                    last.then_inc(x2_turned, 1)
            pe.wait_ge(x2Tlo_ready, BATCH * KD)
            pe.wait_ge(wk3_ready, 1)
            for p in range(PPC):
                keys(0, 0, 0, p)
            pe.wait_ge(x2lo_ready, BATCH)
            grams(0, 0)
            pe.wait_ge(zeroed, 5)
            chunk3(0, True, False)
            with pe.Fori(1, CHUNKS - 1) as c:
                chunk3(c, False, False)
            chunk3(CHUNKS - 1, False, True)
            outputs(BLOCKS * PPC - 2, BLOCKS - 1, 2, CHUNKS - 1)
            turn(BLOCKS * PPC - 1)
            outputs(BLOCKS * PPC - 1, BLOCKS - 1, 3, CHUNKS - 1)

            pe.wait_ge(gw_loaded, 16)
            for k in range(KD):
                last = pe.transpose(ps[:, 0, k * E1:(k + 1) * E1], gw_in[:, k * P:(k + 1) * P], ident[0:E1, 0:E1])
            last.then_inc(gw_turned, 1)
            pe.wait_ge(added3, 4 * BLOCKS)

            def route4(b):
                pe.wait_ge(x3_ready, b * TPB + TPB)
                wait_past(pe, added4, b * TPB)
                for k in range(KD):
                    for i in range(TPB):
                        last = pe.transpose(ps[:, 4 + k, i * P:(i + 1) * P], rows[:, i, k * P:(k + 1) * P], ident[:])
                    last.then_inc(x3_turned, 1)
                pe.wait_ge(x3lo_ready, b * KD + KD)
                pe.wait_ge(sw_lo, 2)
                wait_past(pe, slots_added, b)
                for i in range(TPB):
                    for k in range(KD):
                        last = mm3(ps[:, 6, i * E1:(i + 1) * E1], lambda a: x3T[a][:, k, i * P:(i + 1) * P],
                                   lambda c: gwT[c][:, k, :], k == 0, k == KD - 1)
                last.then_inc(logits4, 1)
                for m, (f, size) in enumerate(F1T):
                    wait_past(pe, hid4_ready, b * FT1 + max(m - 1, 0))
                    for w in range(2):
                        for k in range(KD):
                            last = mm3(ps[0:size, 2 * w + m % 2, :], lambda a: sw[a][:, k, w, f:f + size],
                                       lambda c: x3T[c][:, k, :], k == 0, k == KD - 1)
                    last.then_inc(gate4_ready, 1)
                pe.wait_ge(sel_ready, b * TPB + TPB)
                pe.wait_ge(consts4, 14)
                wait_past(pe, carry_ready, b)
                for i in range(TPB):
                    o = ps[:, 7, i * E1:(i + 1) * E1]
                    pe.matmul(o, tri[:], sel[:, i, :], start=True, stop=False)
                    for j in range(i):
                        pe.matmul(o, onesb[:], sel[:, j, :], start=False, stop=False)
                    last = pe.matmul(o, onesb[:], carry[:], start=False, stop=True)
                last.then_inc(pos_ready, 1)
                pe.wait_ge(hid4_ready, b * FT1 + FT1)
                for i in range(TPB):
                    for m, (f, size) in enumerate(F1T):
                        last = pe.matmul(ps[:, 4 + i // 2, (i % 2) * D:(i % 2 + 1) * D], hid4[0:size, m, i * P:(i + 1) * P],
                                         swd[0:size, m, :], start=m == 0, stop=m == FT1 - 1)
                    last.then_inc(down4, 1)
                for i in range(TPB):
                    pe.wait_ge(onehot_ready, b * TPB + (i + 1))
                    for s in range(GROUPS):
                        last = pe.matmul(ps[:, 6, 4 * s:4 * s + 4],
                                         onehot[i % 2][:, 4 * s:4 * s + 4, :].rearrange("p e c -> p (e c)"),
                                         tokv[:, bass.ds(b * TPB + i, 1), :], start=i == 0 and s == 0, stop=i == TPB - 1,
                                         skip_group_check=True)
                    last.then_inc(onehot_used, 1)

            route4(0)
            with pe.Fori(1, BATCH) as b:
                route4(b)

            def rows_of(s):
                pe.wait_ge(xs_ready, s + 1)
                if not (isinstance(s, int) and s == 0):
                    pe.wait_ge(xsT_ready, s)
                for k in range(KD):
                    last = pe.transpose(ps[:, 0, k * P:(k + 1) * P], xs[:, k:D:2], ident[:])
                last.then_inc(xs_turned, 1)

            def gate_up(s, i, it):
                pe.wait_ge(xsT_ready, s + 1)
                pe.wait_ge(e_loaded[i], 48 * it + (16 + 48))
                if not (isinstance(s, int) and s < 2):
                    pe.wait_ge(hE_ready, s - 1)
                for k in range(KD):
                    for x in range(4):
                        r = slice(32 * x, 32 * x + 32)
                        last = pe.matmul(ps[r, 1 + i % 2, 0:2 * I1], xsT[i % 2][:, k, r], eg[i][:, x, :, k, :],
                                         start=k == 0, stop=k == KD - 1, skip_group_check=True)
                last.then_inc(gu4_ready, 1)

            def experts(s, i, it, left):
                pe.wait_ge(hE_ready, s + 1)
                if not (isinstance(s, int) and s == 0):
                    pe.wait_ge(hET_ready, s)
                for k in range(2):
                    last = pe.transpose(ps[0:IH, 3, k * P:(k + 1) * P], hE[:, k:I1:2], ident[:])
                last.then_inc(hE_turned, 1)
                if left > 2:
                    rows_of(s + 2)
                if left > 1:
                    gate_up(s + 1, (i + 1) % 4, it if i < 3 else it + 1)
                pe.wait_ge(hET_ready, s + 1)
                if not (isinstance(s, int) and s < 2):
                    pe.wait_ge(ylo_ready, s - 1)
                for k in range(2):
                    for x in range(4):
                        r = slice(32 * x, 32 * x + 32)
                        last = pe.matmul(ps[r, 4 + i % 2, 0:D], hET[:, k, r], ed[i][:, x, k, :],
                                         start=k == 0, stop=k == 1, skip_group_check=True)
                last.then_inc(y_mm, 1)

            pe.wait_ge(added4, TILES)
            rows_of(0)
            rows_of(1)
            gate_up(0, 0, 0)
            for i in range(4):
                experts(i, i, 0, GROUPS - i)
            with pe.Fori(1, GROUPS // 4 - 1) as it:
                for i in range(4):
                    experts(it * 4 + i, i, it, 5)
            for i in range(4):
                experts(GROUPS - 4 + i, i, GROUPS // 4 - 1, 4 - i)
            pe.wait_ge(ylo_ready, GROUPS)
            pe.wait_ge(slots_added, BATCH)

            def combine(j):
                for i in range(2):
                    pe.wait_ge(pick_ready, 2 * j + (i + 1))
                    wait_past(pe, comb_added, 2 * j)
                    for s in range(GROUPS):
                        for h in range(2):
                            last = pe.matmul(ps[:, 6 + i, 0:D], pick[i][:, s, :], y4[h][:, s, :],
                                             start=s == 0 and h == 0, stop=s == GROUPS - 1 and h == 1)
                    last.then_inc(comb_ready, 1)

            combine(0)
            with pe.Fori(1, TILES // 2) as j:
                combine(j)


def rope_tables():
    inv = (1.0 / np.float32(ROPE_BASE) ** (np.arange(0, DH, 2, dtype=np.float32) / np.float32(DH))).astype(np.float32)
    angle = (np.arange(T, dtype=np.float32)[None, :] * inv[:, None]).astype(np.float32)
    angle = np.concatenate([angle, angle], 0)
    return np.stack([np.cos(angle), np.sin(angle)]).astype(np.float32)


_INS = [
    "L0_attn_x", "L0_attn_wq", "L0_attn_w_down", "L0_attn_w_up",
    "L0_attn_wo", "L0_ffn_W_router", "L0_ffn_W_gate", "L0_ffn_W_up",
    "L0_ffn_W_down", "L0_ffn_sA_gate", "L0_ffn_sB_gate", "L0_ffn_sA_up",
    "L0_ffn_sB_up", "L0_ffn_sA_down", "L0_ffn_sB_down", "L0_ffn_A_gate",
    "L0_ffn_B_gate", "L0_ffn_A_up", "L0_ffn_B_up", "L0_ffn_A_down",
    "L0_ffn_B_down", "L0_ffn_expert_bias", "L1_attn_Wq", "L1_attn_Wk",
    "L1_attn_Wv", "L1_attn_Wo", "L1_attn_bo", "L1_ffn_gate_w",
    "L1_ffn_w_gate", "L1_ffn_w_up", "L1_ffn_w_down", "L1_ffn_sw_gate",
    "L1_ffn_sw_up", "L1_ffn_sw_down",
]


def kernel(**inputs):
    import concourse.bacc as bacc
    from concourse.bass_utils import run_bass_kernel_spmd

    nc = bacc.Bacc("TRN2", target_bir_lowering=False, num_devices=1)
    arrays, io = {}, {}
    for name in _INS + ["rope"]:
        a = rope_tables() if name == "rope" else np.ascontiguousarray(inputs[name])
        arrays[f"in_{name}_dram"] = a
        io[name] = nc.dram_tensor(f"in_{name}_dram", a.shape, mybir.dt.from_np(a.dtype), kind="ExternalInput").ap()
    out = nc.dram_tensor("out_0_dram", (BATCH, T, D), F32, kind="ExternalOutput").ap()
    program(nc, io, out)
    return run_bass_kernel_spmd(nc, [arrays], core_ids=[0]).results[0]["out_0_dram"]
```

```python
from contextlib import ExitStack

import numpy as np

import concourse.bass as bass
from concourse import mybir

ALU = mybir.AluOpType
ACT = mybir.ActivationFunctionType
AX_X = mybir.AxisListType.X
F32 = mybir.dt.float32
F32R = mybir.dt.float32r
BF16 = mybir.dt.bfloat16
U32 = mybir.dt.uint32

P = 128
BATCH, T, D = 4, 512, 256
TOK = BATCH * T
TILES = TOK // P
TPB = T // P
KD = D // P
HEADS, DH = 16, 128
PAIRS = HEADS // 2
STEPS = 2 * BATCH
EPS = 1e-5
F0, E0, R0 = 688, 8, 8
NL = (1 + E0) * R0
NA = E0 + 2 * NL
FT0 = 6
F0S = [(i * 115, 115) for i in range(4)] + [(460, 114), (574, 114)]
M0 = 115
E1, I1, CAP, TOP1 = 64, 176, 32, 6
IH = I1 // 2
GROUPS = E1 * CAP // P
ROW = D + E1
F1S = 352
F1T = [(0, 118), (118, 117), (235, 117)]
FT1, M1 = 3, 118
LINKS4 = 46
FIRST_KEYS = (0, 1, 4, 5)
CHUNKS = 4
PPC = 4
BLOCKS = CHUNKS * BATCH
LINKS0 = 39
SCALE = float(DH) ** -0.5
MASKED = -1.0e30
ROPE_BASE = 10000.0
HALVES = ((0, 0), (1, 0), (0, 1))


def program(nc, io, out):
    ctx = ExitStack()
    with ctx:
        def sem(name):
            return ctx.enter_context(nc.semaphore(name))

        def wait_past(engine, signal, count):
            if not (isinstance(count, int) and count <= 0):
                engine.wait_ge(signal, count)

        ps = ctx.enter_context(nc.psum_tensor("ps", [P, 8, 512], F32))
        BS, BA, BW, BO = 0, 2, 4, 7
        WV_BANKS, U_BANKS = (0, 1, 4, 5), (6, 7, 0, 1, 4, 5, 6, 7)

        def place(name, kb, shape, dt=F32):
            with ExitStack() as stack:
                if kb:
                    stack.enter_context(nc.sbuf_tensor(name + "_below", [P, int(kb * 256)], F32))
                return stack.enter_context(nc.sbuf_tensor(name, shape, dt))

        acc = place("acc", 0, [P, TILES, D])
        ident = place("ident", 16, [P, P])
        identb = place("identb", 16.5, [P, P], BF16)
        maskb = place("maskb", 16.75, [P, P], BF16)
        halfp = place("halfp", 17, [P, TPB])
        iota8 = place("iota8", 17.25, [P, 64])
        ebias = place("ebias", 17.5, [P, E0])
        scratch = place("scratch", 17.75, [P, 1])

        xT = [place(f"xT{h}", 20 + 16 * h, [P, KD, TOK], F32R) for h in range(2)]
        cT = [place(f"cT{h}", 52 + 8 * h, [P, TOK], F32R) for h in range(2)]
        c_tok = place("c_tok", 68, [P, TILES, DH])
        rope = place("rope_sb", 76, [P, 2, T])
        wq_in = place("wq_in", 80, [P, KD, 2 * DH])
        wk_in = place("wk_in", 82, [P, 2 * DH])
        wq = [place(f"wq{h}", 83 + 2 * h, [P, KD, 2 * DH], F32R) for h in range(2)]
        wk = [place(f"wk{h}", 87 + h, [P, 2 * DH], F32R) for h in range(2)]
        U = place("U", 89, [P, HEADS, D])
        qT = place("qT", 105, [P, 2, BATCH, T])
        kT = place("kT", 121, [P, 2, BATCH, T])
        prod = [[place(f"prod{i}{j}", 137 + 8 * i + 4 * j, [P, 2, T]) for j in range(2)] for i in range(2)]
        mx = place("mx", 153, [P, 2, TPB])
        nm = place("nm", 153.25, [P, 2, TPB])
        rs = place("rs", 153.5, [P, 2, TPB])
        rinv = place("rinv", 153.75, [P, 2, TPB])
        wd_in = place("wd_in", 154, [P, KD, DH])
        wd = [place(f"wd{h}", 155 + h, [P, KD, DH], F32R) for h in range(2)]
        wv = place("wv", 157, [P, HEADS, DH])
        wvT = place("wvT", 165, [P, HEADS, DH])
        wo = place("wo", 173, [P, HEADS, D])
        identr = place("identr", 189.25, [P, P], F32R)
        probs = [place(f"probs{i}", 154 + 5 * i, [P, 10 * P]) for i in range(2)]
        pT = place("pT", 164, [P, TPB, T])
        oT = place("oT", 172, [P, T])

        gu_in = place("gu_in", 174, [P, KD, 2, F0])
        lb_in = place("lb_in", 185, [NL, 2, F0])
        dn = place("dn", 191, [M0, FT0, D + NL])
        la_in = place("la_in", 199, [P, KD, NA])
        ldn = place("ldn", 200.5, [NL, D])
        gu = [place(f"gu{h}", 20 + 11 * h, [P, KD, 2, F0], F32R) for h in range(2)]
        lb = [place(f"lb{h}", 42 + 5.5 * h, [NL, 2, F0], F32R) for h in range(2)]
        la = [place(f"la{h}", 53 + 1.25 * h, [P, KD, NA], F32R) for h in range(2)]
        x1T = [place(f"x1T{h}", 56 + 4 * h, [P, KD, T], F32R) for h in range(2)]
        xaT = [place(f"xaT{h}", 64 + 4 * h, [NL, 2, T], F32R) for h in range(2)]
        gated = [place(f"gated{h}", 72 + 2 * h, [M0, T]) for h in range(2)]
        hidT = place("hidT", 76, [M0, FT0, T])
        haT = place("haT", 88, [NL, T])
        xa = place("xa", 90, [P, TPB, 2 * NL])
        ha = place("ha", 92.5, [P, TPB, NL])
        x1s = place("x1s", 94, [P, TPB, D])
        stat = place("stat", 19.25, [P, TPB, 6])
        meanvar = place("meanvar", 19.375, [P, TPB, 2])
        vareps = place("vareps", 19.5, [P, TPB])
        rstd = place("rstd", 19.625, [P, TPB])
        sig = place("sig", 99, [P, TPB, E0])
        biased = place("biased", 99.25, [P, TPB, E0])
        top8 = place("top8", 99.5, [P, TPB, 8])
        topi = place("topi", 99.75, [P, TPB, 8], U32)
        topf = place("topf", 100, [P, TPB, 8])
        one0 = place("one0", 100.25, [P, TPB, E0])
        one1 = place("one1", 100.5, [P, TPB, E0])
        picked = place("picked", 100.75, [P, TPB, E0])
        den = place("den", 101, [P, TPB])
        wexp = place("wexp", 101.25, [P, TPB, 1 + E0])
        wnext = place("wnext", 101.5, [P, TPB, 1 + E0])
        x2 = [place(f"x2{h}", 158 + 16 * h, [P, TILES, D], F32R) for h in range(2)]

        CH = 4 * P
        wq3_in = place("wq3_in", 110, [P, KD, CH])
        wv3_in = place("wv3_in", 114, [P, KD, CH])
        wo3_in = place("wo3_in", 118, [P, 4, D])
        wk3_in = place("wk3_in", 122, [P, KD, CH])
        wq3 = [place(f"wq3{h}", 126 + 4 * h, [P, KD, CH], F32R) for h in range(2)]
        wv3 = [place(f"wv3{h}", 134 + 4 * h, [P, KD, CH], F32R) for h in range(2)]
        wo3 = [place(f"wo3{h}", 142 + 4 * h, [P, 4, D], F32R) for h in range(2)]
        wk3 = [place("wk30", 190, [P, CHUNKS, KD, CH], F32R), place("wk31", 94, [P, CHUNKS, KD, CH], F32R)]
        x2T = [place(f"x2T{h}", 20 + 16 * h, [P, KD, TOK], F32R) for h in range(2)]
        k3 = [place(f"k3{h}", 52 + 8 * h, [P, TPB, CH], F32R) for h in range(2)]
        g3 = [place(f"g3{h}", 68 + 4 * h, [P, KD, CH], F32R) for h in range(2)]
        kvT = [place(f"kvT{h}", 76 + 2 * h, [P, PPC, P], F32R) for h in range(2)]
        ksb = place("ksb", 80, [P, CH])
        q3 = place("q3", 82, [P, CH])
        qk = place("qk", 84, [P, CH])
        qs = place("qs", 86, [P, CH])
        nrm = place("nrm", 88, [P, CH // 64])
        onesr = place("onesr", 88.5, [P, P], F32R)
        qn3 = [place(f"qn3{h}", 90 + 2 * h, [P, PPC, P], F32R) for h in range(2)]
        kvo = [place(f"kvo{h}", 150 + 4 * h, [P, PPC, D], F32R) for h in range(2)]
        sw_in = place("sw_in", 94, [P, KD, 2, F1S])
        swd = place("swd", 99.5, [M1, FT1, D])
        gw_in = place("gw_in", 103, [E1, D])
        sw = [place(f"sw{h}", 20 + 5.5 * h, [P, KD, 2, F1S], F32R) for h in range(2)]
        gwT = [place(f"gwT{h}", 31 + 0.5 * h, [P, KD, E1], F32R) for h in range(2)]
        rows = place("rows", 32, [P, TPB, ROW])
        x3T = [place(f"x3T{h}", 37 + 4 * h, [P, KD, T], F32R) for h in range(2)]
        gated4 = [place(f"gated4{h}", 45 + 2 * h, [M1, T]) for h in range(2)]
        hid4 = place("hid4", 49, [M1, FT1, T])
        onehot = [place(f"onehot{h}", 55 + 4 * h, [P, E1, CAP], BF16) for h in range(2)]
        capi = place("capi", 63, [P, E1, CAP], BF16)
        tokv = place("tokv", 67, [P, TILES, 4], BF16)
        tri = place("tri", 67.25, [P, P], BF16)
        onesb = place("onesb", 67.5, [P, P], BF16)
        carry = place("carry", 67.75, [P, E1], BF16)
        sel = place("sel", 68, [P, TPB, E1], BF16)
        selsum = place("selsum", 68.5, [P, E1])
        e4 = place("e4", 69, [P, TPB, E1])
        posb = place("posb", 70, [P, TPB, E1], BF16)
        pm = place("pm", 70.5, [P, TPB, E1])
        mx4 = place("mx4", 71.5, [P, TPB])
        nmx4 = place("nmx4", 71.75, [P, TPB])
        sm4 = place("sm4", 72, [P, TPB])
        top4 = place("top4", 72.25, [P, TPB, 8])
        top4i = place("top4i", 72.5, [P, TPB, 8], U32)
        top4f = place("top4f", 72.75, [P, TPB, 8])
        slots = place("slots", 73, [P, GROUPS, 4])
        xg = place("xg", 20, [P, GROUPS, ROW])
        xs = place("xs", 40, [P, D])
        xsT = [place(f"xsT{h}", 41 + 22 * h, [P, KD, P]) for h in range(2)]
        actE = place("actE", 42, [P, I1])
        hE = place("hE", 43, [P, I1])
        hET = place("hET", 44, [IH, 2, P])
        pick = [place(f"pick{h}", 45 + 8 * h, [P, GROUPS, P], F32R) for h in range(2)]
        fin = place("fin", 61, [P, 2, D])
        y4 = [place("y40", 74, [P, GROUPS, D], F32R), place("y41", 104, [P, GROUPS, D], F32R)]
        iota_t = place("iota_t", 90, [P, P])
        tbase = place("tbase", 90.75, [P, TILES])
        quarter = place("quarter", 91, [P, 4])
        wslot = place("wslot", 91.25, [P, GROUPS])
        idxf = place("idxf", 91.5, [P, GROUPS])
        gidx = place("gidx", 91.75, [P, GROUPS], U32)
        wtmp = place("wtmp", 92, [P, GROUPS, 4])
        eg = [place(f"eg{i}", 131 + 19 * i, [P, 4, 2, 2, I1]) for i in range(4)]
        ed = [place(f"ed{i}", 142 + 19 * i, [IH, 4, 2, D]) for i in range(4)]
        rows_dram = nc.dram_tensor("rows_dram", [TOK, ROW], F32, kind="Internal").ap()
        bo_sb = place("bo_sb", 18, [P, D])
        ones = place("ones", 19, [P, 1])

        x_in = [sem(f"x_in{b}") for b in range(BATCH)]
        wd_loaded, wvo_loaded = sem("wd_loaded"), sem("wvo_loaded")
        wq_loaded, wk_loaded = sem("wq_loaded"), sem("wk_loaded")
        zeroed, consts_ready = sem("zeroed"), sem("consts_ready")
        x_turned, xhi_ready, xlo_ready = sem("x_turned"), sem("xhi_ready"), sem("xlo_ready")
        wd_hi, wd_lo = sem("wd_hi"), sem("wd_lo")
        c_ready, chi_ready, clo_ready, ctok_ready = sem("c_ready"), sem("chi_ready"), sem("clo_ready"), sem("ctok_ready")
        c_turned, rope_loaded = sem("c_turned"), sem("rope_loaded")
        wv_turned, wvT_ready, u_ready, u_copied = sem("wv_turned"), sem("wvT_ready"), sem("u_ready"), sem("u_copied")
        wq_hi, wq_lo, wk_hi, wk_lo = sem("wq_hi"), sem("wq_lo"), sem("wk_hi"), sem("wk_lo")
        proj_ready, products_ready, roped = sem("proj_ready"), sem("products_ready"), sem("roped")
        scores_ready, max_ready, negmax_ready, probs_ready = (
            sem("scores_ready"), sem("max_ready"), sem("negmax_ready"), sem("probs_ready"))
        transposed, pt_copied, pv_done, ot_copied = sem("transposed"), sem("pt_copied"), sem("pv_done"), sem("ot_copied")
        out_ready, acc_added, rinv_ready = sem("out_ready"), sem("acc_added"), sem("rinv_ready")
        stored = sem("stored")
        sw_loaded, sw_hi, sw_lo = sem("sw_loaded"), sem("sw_hi"), sem("sw_lo")
        gw_turned, consts4 = sem("gw_turned"), sem("consts4")
        x3_ready, x3_turned, x3hi_ready, x3lo_ready = sem("x3_ready"), sem("x3_turned"), sem("x3hi_ready"), sem("x3lo_ready")
        logits4, nmx4_ready, exp4, scored = sem("logits4"), sem("nmx4_ready"), sem("exp4"), sem("scored")
        rows_stored, gate4_ready, gated4_ready, hid4_ready = (
            sem("rows_stored"), sem("gate4_ready"), sem("gated4_ready"), sem("hid4_ready"))
        sel_ready, carry_ready, pos_ready = sem("sel_ready"), sem("carry_ready"), sem("pos_ready")
        onehot_ready, onehot_used, down4, added4 = sem("onehot_ready"), sem("onehot_used"), sem("down4"), sem("added4")
        slots_added, slot_data_ready, gathered = (
            sem("slots_added"), sem("slot_data_ready"), [sem(f"gathered{q}") for q in range(4)])
        e_loaded = x_in
        xs_ready, xs_turned, xsT_ready = sem("xs_ready"), sem("xs_turned"), sem("xsT_ready")
        gu4_ready, actE_ready, hE_ready, hE_turned, hET_ready = (
            sem("gu4_ready"), sem("actE_ready"), sem("hE_ready"), sem("hE_turned"), sem("hET_ready"))
        y_mm, yhi_ready, ylo_ready = sem("y_mm"), sem("yhi_ready"), sem("ylo_ready")
        pick_ready, comb_ready, comb_added, fin_ready = (
            sem("pick_ready"), sem("comb_ready"), sem("comb_added"), sem("fin_ready"))
        wq3_loaded, wk3_loaded, wv3_loaded, wo3_loaded = (
            sem("wq3_loaded"), sem("wk3_loaded"), sem("wv3_loaded"), sem("wo3_loaded"))
        wq3_ready, wk3_ready, wo3_ready = sem("wq3_ready"), sem("wk3_ready"), sem("wo3_ready")
        pool3, wv3_hi, wv3_lo = sem("pool3"), sem("wv3_hi"), sem("wv3_lo")
        x2_turned, x2Thi_ready, x2Tlo_ready = sem("x2_turned"), sem("x2Thi_ready"), sem("x2Tlo_ready")
        q_ready, q_copied, qs_ready = sem("q_ready"), sem("q_copied"), sem("qs_ready")
        k_ready, khi_ready, klo_ready = sem("k_ready"), sem("khi_ready"), sem("klo_ready")
        g_ready, ghi_ready, glo_ready = sem("g_ready"), sem("ghi_ready"), sem("glo_ready")
        ks_ready, ksb_ready, kv_ready, kvhi_ready, kvlo_ready = (
            sem("ks_ready"), sem("ksb_ready"), sem("kv_ready"), sem("kvhi_ready"), sem("kvlo_ready"))
        qk_ready, norm_ready, kvo_ready = sem("qk_ready"), sem("norm_ready"), sem("kvo_ready")
        qt_ready, qnhi_ready, qnlo_ready, kvohi_ready, kvolo_ready = (
            sem("qt_ready"), sem("qnhi_ready"), sem("qnlo_ready"), sem("kvohi_ready"), sem("kvolo_ready"))
        out3_ready, added3 = sem("out3_ready"), sem("added3")
        gu_loaded, lb_loaded, la_loaded, dn_loaded = sem("gu_loaded"), sem("lb_loaded"), sem("la_loaded"), sem("dn_loaded")
        w0_hi, w0_lo = sem("w0_hi"), sem("w0_lo")
        dchain = sem("dchain")
        var_ready, rstd_ready = sem("var_ready"), sem("rstd_ready")
        x1_ready, x1_turned, x1hi_ready, x1lo_ready = sem("x1_ready"), sem("x1_turned"), sem("x1hi_ready"), sem("x1lo_ready")
        logits_ready, sig_ready, xa_ready, xa_turned = sem("logits_ready"), sem("sig_ready"), sem("xa_ready"), sem("xa_turned")
        xahi_ready, xalo_ready = sem("xahi_ready"), sem("xalo_ready")
        gate_ready, gated_ready, hid_ready = sem("gate_ready"), sem("gated_ready"), sem("hid_ready")
        down_ready, ha_ready, ha_turned, haT_ready, ffn_ready = (
            sem("down_ready"), sem("ha_ready"), sem("ha_turned"), sem("haT_ready"), sem("ffn_ready"))
        ffn_added = sem("ffn_added")
        x2_ready, x2hi_ready, x2lo_ready = sem("x2_ready"), sem("x2hi_ready"), sem("x2lo_ready")

        x_dram = io["L0_attn_x"].rearrange("b (i p) d -> b p i d", p=P)
        out_dram = out.rearrange("b (i p) d -> b p i d", p=P)
        wq_dram = io["L0_attn_wq"].rearrange("(k p) n -> p k n", p=P)
        wup_dram = io["L0_attn_w_up"].rearrange("p (h w d) -> p h w d", w=2, d=DH)
        wo_dram = io["L0_attn_wo"].rearrange("(h p) n -> p h n", p=DH)
        def wait_gathered(engine, quarters):
            for q in quarters:
                engine.wait_ge(gathered[q], 16 * (GROUPS // 4))

        w0_pieces = [([h[:, k, w, :] for h in gu], gu_in[:, k, w, :]) for k in range(KD) for w in range(2)]
        w0_pieces += [([h[:] for h in lb], lb_in[:]), ([h[:] for h in la], la_in[:])]

        block = ctx.enter_context(nc.Block())

        @block.sync
        def _(sp):
            for b in range(BATCH):
                sp.dma_start(acc[:, b * TPB:(b + 1) * TPB, :], x_dram[b]).then_inc(x_in[b], 16)
            sp.dma_start(wd_in[:], io["L0_attn_w_down"].rearrange("(k p) n -> p k n", p=P)).then_inc(wd_loaded, 16)
            def load_pair(g):
                wait_past(sp, wq_lo, g)
                sp.dma_start(wq_in[:], wq_dram[:, :, bass.ds(g * (2 * DH), 2 * DH)]).then_inc(wq_loaded, 16)
                wait_past(sp, wk_lo, g)
                sp.dma_start(wk_in[:].rearrange("p (h d) -> p h d", h=2),
                             wup_dram[:, bass.ds(g * 2, 2), 0, :]).then_inc(wk_loaded, 16)

            load_pair(0)
            sp.dma_start(rope[:], io["rope"].rearrange("w p t -> p w t")).then_inc(rope_loaded, 16)
            sp.dma_start(wv[:], wup_dram[:, :, 1, :]).then_inc(wvo_loaded, 16)
            sp.dma_start(wo[:], wo_dram).then_inc(wvo_loaded, 16)
            with sp.Fori(1, PAIRS) as g:
                load_pair(g)
            sp.wait_ge(u_ready, 8)
            for w, name in enumerate(("gate", "up")):
                sp.dma_start(gu_in[:, :, w, :], io["L0_ffn_W_" + name].rearrange("(k p) n -> p k n", p=P)).then_inc(gu_loaded, 16)
            for w, name in enumerate(("gate", "up")):
                sp.dma_start(lb_in[0:R0, w, :], io["L0_ffn_sB_" + name]).then_inc(lb_loaded, 16)
                sp.dma_start(lb_in[R0:NL, w, :], io["L0_ffn_B_" + name].rearrange("e r n -> (e r) n")).then_inc(lb_loaded, 16)
            sp.dma_start(la_in[:, :, 0:E0], io["L0_ffn_W_router"].rearrange("(k p) n -> p k n", p=P)).then_inc(la_loaded, 16)
            for w, name in enumerate(("gate", "up")):
                at = E0 + w * NL
                sp.dma_start(la_in[:, :, at:at + R0], io["L0_ffn_sA_" + name].rearrange("(k p) n -> p k n", p=P)).then_inc(la_loaded, 16)
                for k in range(KD):
                    sp.dma_start(la_in[:, k, at + R0:at + NL].rearrange("p (e r) -> p e r", r=R0),
                                 io["L0_ffn_A_" + name].rearrange("e (k p) r -> k p e r", p=P)[k]).then_inc(la_loaded, 16)
            for lo, hi, size in ((0, 4, 115), (4, 6, 114)):
                inner = slice(F0S[lo][0], F0S[hi - 1][0] + size)
                sp.dma_start(dn[0:size, lo:hi, 0:D],
                             io["L0_ffn_W_down"][inner, :].rearrange("(i p) n -> p i n", p=size)).then_inc(dn_loaded, 16)
                sp.dma_start(dn[0:size, lo:hi, D:D + R0],
                             io["L0_ffn_sA_down"][inner, :].rearrange("(i p) n -> p i n", p=size)).then_inc(dn_loaded, 16)
                for i in range(lo, hi):
                    sp.dma_start(dn[0:size, i, D + R0:D + NL].rearrange("p (e r) -> p e r", r=R0),
                                 io["L0_ffn_A_down"][:, F0S[i][0]:F0S[i][0] + size, :].rearrange("e p r -> p e r")).then_inc(dn_loaded, 16)
            sp.dma_start(ldn[0:R0, :], io["L0_ffn_sB_down"]).then_inc(dn_loaded, 16)
            sp.dma_start(ldn[R0:NL, :], io["L0_ffn_B_down"].rearrange("e r n -> (e r) n")).then_inc(dn_loaded, 16)
            sp.dma_start(ebias[:], io["L0_ffn_expert_bias"].rearrange("(a e) -> a e", a=1).broadcast_to([P, E0])).then_inc(la_loaded, 16)
            w3 = {n: io["L1_attn_W" + n].rearrange("(k p) n -> p k n", p=P) for n in "qkv"}
            wo3_dram = io["L1_attn_Wo"].rearrange("(j p) n -> p j n", p=P)
            sp.dma_start(bo_sb[:], io["L1_attn_bo"].rearrange("(a e) -> a e", a=1).broadcast_to([P, D])).then_inc(dn_loaded, 16)
            sp.wait_ge(acc_added, 4 * STEPS * PAIRS)

            def load_chunk(c):
                cols = bass.ds(c * CH, CH)
                wait_past(sp, wq3_ready, PPC * c)
                sp.dma_start(wq3_in[:], w3["q"][:, :, cols]).then_inc(wq3_loaded, 16)
                wait_past(sp, wv3_lo, c)
                sp.dma_start(wv3_in[:], w3["v"][:, :, cols]).then_inc(wv3_loaded, 16)
                wait_past(sp, wo3_ready, PPC * c)
                sp.dma_start(wo3_in[:], wo3_dram[:, bass.ds(c * PPC, PPC), :]).then_inc(wo3_loaded, 16)
                wait_past(sp, wk3_ready, c)
                sp.dma_start(wk3_in[:], w3["k"][:, :, cols]).then_inc(wk3_loaded, 16)

            load_chunk(0)
            with sp.Fori(1, CHUNKS) as c:
                load_chunk(c)
            sp.wait_ge(k_ready, 4 * BLOCKS)
            for w, name in enumerate(("gate", "up")):
                sp.dma_start(sw_in[:, :, w, :], io["L1_ffn_sw_" + name].rearrange("(k p) n -> p k n", p=P)).then_inc(sw_loaded, 16)
            sp.dma_start(gw_in[:], io["L1_ffn_gate_w"]).then_inc(sw_loaded, 16)
            sp.dma_start(swd[:, 0, :], io["L1_ffn_sw_down"][0:118, :]).then_inc(sw_loaded, 16)
            sp.dma_start(swd[0:117, 1:3, :], io["L1_ffn_sw_down"][118:352, :].rearrange("(i p) n -> p i n", p=117)).then_inc(sw_loaded, 16)

            def experts_of(s):
                return slice(4 * s, 4 * s + 4) if isinstance(s, int) else bass.ds(4 * s, 4)

            def load_hidden(s, i):
                for w, name in enumerate(("gate", "up")):
                    sp.dma_start(eg[i][:, :, w, :, :].rearrange("p x k n -> p x (k n)"),
                                 io["L1_ffn_w_" + name].rearrange("x (p k) n -> p x (k n)", k=2)[:, experts_of(s), :]).then_inc(e_loaded[i], 16)

            def load_down(s, i):
                sp.dma_start(ed[i][:].rearrange("p x k n -> p x (k n)"),
                             io["L1_ffn_w_down"].rearrange("x (p k) n -> p x (k n)", k=2)[:, experts_of(s), :]).then_inc(e_loaded[i], 16)

            def load_experts(s, i):
                load_hidden(s, i)
                load_down(s, i)

            sp.wait_ge(g_ready, 2 * BLOCKS)
            for i in (2, 3):
                load_experts(i, i)
            sp.wait_ge(out3_ready, BLOCKS * PPC)
            for i in (0, 1):
                load_experts(i, i)
            with sp.Fori(0, BATCH) as b:
                sp.wait_ge(scored, b + 1)
                sp.dma_start(rows_dram[bass.ds(b * T, T), :].rearrange("(i p) n -> p i n", p=P), rows[:]).then_inc(rows_stored, 16)
            with sp.Fori(1, GROUPS // 4) as it:
                for i in range(4):
                    sp.wait_ge(gu4_ready, it * 4 + (i - 3))
                    load_hidden(it * 4 + i, i)
                    sp.wait_ge(y_mm, it * 4 + (i - 3))
                    load_down(it * 4 + i, i)
            with sp.Fori(0, TILES // 2) as j:
                sp.wait_ge(fin_ready, 2 * j + 2)
                sp.dma_start(out.rearrange("b t d -> (b t) d")[bass.ds(j * (2 * P), 2 * P), :].rearrange("(i p) n -> p i n", p=P),
                             fin[:]).then_inc(stored, 16)
            sp.wait_ge(stored, 16 * (TILES // 2))
        @block.gpsimd
        def _(pool):
            nc.gpsimd.memset(ident[:], 0.0).then_inc(zeroed, 1)
            nc.gpsimd.memset(identb[:], 0.0).then_inc(zeroed, 1)
            nc.gpsimd.memset(maskb[:], 0.0).then_inc(zeroed, 1)
            nc.gpsimd.memset(ones[:], 1.0).then_inc(consts_ready, 1)
            nc.gpsimd.memset(halfp[:], -0.5).then_inc(consts_ready, 1)
            nc.gpsimd.iota(iota8[:], pattern=[[1, 64]], base=0, channel_multiplier=0,
                           allow_small_or_imprecise_dtypes=True).then_inc(consts_ready, 1)
            pool.wait_ge(zeroed, 3)
            for m in (ident, identb):
                nc.gpsimd.affine_select(out=m[:], in_=m[:], compare_op=ALU.not_equal, fill=1.0, base=0,
                                        pattern=[[-1, P]], channel_multiplier=1).then_inc(consts_ready, 1)
            nc.gpsimd.affine_select(out=maskb[:], in_=maskb[:], compare_op=ALU.is_ge, fill=MASKED, base=0,
                                    pattern=[[-1, P]], channel_multiplier=1).then_inc(consts_ready, 1)

            def rotate(dst, b, idx, parity, scores_before):
                pool.wait_ge(products_ready, 2 * idx + 2)
                if scores_before is not None:
                    pool.wait_ge(scores_ready, scores_before)
                byc, bys = prod[parity]
                for h in range(2):
                    r = slice(64 * h, 64 * h + 64)
                    nc.gpsimd.tensor_tensor(dst[0:64, h, b, :], byc[r, 0, :], bys[r, 1, :],
                                            ALU.subtract).then_inc(roped, 1)
                    nc.gpsimd.tensor_tensor(dst[64:128, h, b, :], bys[r, 0, :], byc[r, 1, :],
                                            ALU.add).then_inc(roped, 1)

            for b in range(BATCH - 1):
                rotate(qT, b, 2 * b, 0, None)
                rotate(kT, b, 2 * b + 1, 1, None)

            def pair(g, first, last):
                for n in range(2 if last else STEPS):
                    idx = g * STEPS + (6 + n)
                    b = (3, 0, 1, 2)[n // 2]
                    if n < 2:
                        before = None if first else g * (4 * STEPS)
                    else:
                        before = g * (4 * STEPS) + 4 * (2 * b + 2)
                    rotate((qT, kT)[n % 2], b, idx, n % 2, before)

            pair(0, True, False)
            with pool.Fori(1, PAIRS - 1) as g:
                pair(g, False, False)
            pair(PAIRS - 1, False, True)

            def root(n):
                pool.wait_ge(var_ready, n)
                nc.gpsimd.tensor_tensor(rstd[:], vareps[:], halfp[:], ALU.pow).then_inc(rstd_ready, 1)

            def x2_rest(b):
                pool.wait_ge(x2hi_ready, b + 1)
                t = bass.ds(b * TPB, TPB)
                nc.gpsimd.tensor_tensor(x2[1][:, t, :], acc[:, t, :], x2[0][:, t, :].bitcast(F32),
                                        ALU.subtract).then_inc(x2lo_ready, 1)

            pool.wait_ge(roped, 4 * (6 + STEPS * (PAIRS - 1) + 2))
            root(1)
            root(2)
            root(3)
            x2_rest(0)
            pool.wait_ge(acc_added, 4 * STEPS * PAIRS)
            pool3_done = [0, 0]

            def halve(whole, hi, lo, ready, between=None):
                one = ones[0:whole.shape[0], :]
                if len(whole.shape) == 3:
                    one = one.rearrange("p (a n) -> p a n", a=1)
                nc.gpsimd.tensor_tensor(hi, whole, one.broadcast_to(list(whole.shape)), ALU.mult).then_inc(pool3, 1)
                pool3_done[1] += 1
                if between:
                    between()
                pool.wait_ge(pool3, pool3_done[0] + pool3_done[1])
                nc.gpsimd.tensor_tensor(lo, whole, hi.bitcast(F32), ALU.subtract).then_inc(ready, 1)

            def halve_wq3(p):
                j = slice(p * P, (p + 1) * P)
                halve(wq3_in[:, :, j], wq3[0][:, :, j], wq3[1][:, :, j], wq3_ready)

            def halve_wo3(p):
                halve(wo3_in[:, p, :], wo3[0][:, p, :], wo3[1][:, p, :], wo3_ready)

            def halve_wk3(c, between=None):
                pool.wait_ge(wk3_loaded, 16 * c + 16)
                if isinstance(c, int):
                    o = [w[:, c, :, :] for w in wk3]
                else:
                    o = [w[:, bass.ds(c, 1), :, :].rearrange("p c k n -> p (c k) n") for w in wk3]
                halve(wk3_in[:], o[0], o[1], wk3_ready, between)

            pool.wait_ge(consts_ready, 6)
            pool.wait_ge(wq3_loaded, 16)
            halve_wq3(0)
            halve_wq3(1)
            root(4)
            root(5)
            x2_rest(1)
            halve_wq3(2)
            halve_wq3(3)
            pool.wait_ge(wo3_loaded, 16)
            root(6)
            root(7)
            x2_rest(2)
            for p in range(PPC):
                halve_wo3(p)
            pool.wait_ge(ffn_ready, TILES)
            halve_wk3(0, lambda: root(8))
            x2_rest(3)
            pool.wait_ge(x2_ready, TILES)
            nc.gpsimd.memset(kvT[0][:].bitcast(F32), 0.0).then_inc(zeroed, 1)
            nc.gpsimd.memset(kvT[1][:].bitcast(F32), 0.0).then_inc(zeroed, 1)
            nc.gpsimd.memset(onesr[:].bitcast(F32), 1.0).then_inc(zeroed, 1)

            def chunk3(c, first, last):
                for b in range(BATCH):
                    n = c * BATCH + b
                    for i in range(TPB):
                        u = c * (BATCH * TPB) + (b * TPB + i)
                        pool.wait_ge(q_copied, u + 1)
                        if i == 0:
                            pool.wait_ge(ksb_ready, n + 1)
                        if not (first and b == 0 and i == 0):
                            pool.wait_ge(norm_ready, 3 * u - 2)
                        nc.gpsimd.tensor_tensor(qk[:], q3[:], ksb[:], ALU.mult).then_inc(qk_ready, 1)
                        if b == 3 and i == 1 and not last:
                            pool.wait_ge(wo3_loaded, 16 * c + 32)
                            pool.wait_ge(kvo_ready, 2 * n + 2)
                            for p in range(PPC):
                                halve_wo3(p)
                    if b == 1 and not last:
                        halve_wk3(c + 1)
                    if b == 3 and not last:
                        pool.wait_ge(wq3_loaded, 16 * c + 32)
                        pool.wait_ge(q_ready, 4 * n + 4)
                        for p in range(PPC):
                            halve_wq3(p)

            pool3_done[0], pool3_done[1] = pool3_done[1], 0
            first_base = pool3_done[0]
            chunk3(0, True, False)
            per = pool3_done[1]
            with pool.Fori(1, CHUNKS - 1) as c:
                pool3_done[0], pool3_done[1] = first_base + c * per, 0
                chunk3(c, False, False)
                assert pool3_done[1] == per
            pool3_done[0], pool3_done[1] = first_base + (CHUNKS - 1) * per, 0
            chunk3(CHUNKS - 1, False, True)

            root(9)
            pool.wait_ge(added3, 4 * BLOCKS)
            nc.gpsimd.memset(tri[:], 1.0).then_inc(zeroed, 1)
            nc.gpsimd.memset(onesb[:], 1.0).then_inc(consts4, 1)
            nc.gpsimd.memset(carry[:], 0.0).then_inc(consts4, 1)
            nc.gpsimd.memset(quarter[:], 0.0).then_inc(zeroed, 1)
            pool.wait_ge(zeroed, 8)
            nc.gpsimd.affine_select(out=tri[:], in_=tri[:], compare_op=ALU.is_gt, fill=0.0, base=0,
                                    pattern=[[1, P]], channel_multiplier=-1).then_inc(consts4, 1)
            for j in range(4):
                pool.wait_ge(consts4, 3 + j)
                nc.gpsimd.memset(quarter[32 * j:32 * j + 32, j:j + 1], 1.0).then_inc(consts4, 1)

            pool.wait_ge(consts4, 7)

            def iota(o, pattern, mult):
                nc.gpsimd.iota(o, pattern=pattern, base=0, channel_multiplier=mult,
                               allow_small_or_imprecise_dtypes=True).then_inc(consts4, 1)

            iota(tokv[:, :, 0], [[0, TILES]], 1)
            iota(tokv[:, :, 1], [[P, TILES]], 0)
            nc.gpsimd.memset(tokv[:, :, 2:3], 1.0).then_inc(consts4, 1)
            nc.gpsimd.memset(tokv[:, :, 3:4], 0.0).then_inc(consts4, 1)
            iota(iota_t[:], [[1, P]], 0)
            iota(tbase[:], [[P, TILES]], 0)
            iota(capi[:], [[0, E1], [1, CAP]], 0)
            with pool.Fori(1, BATCH) as b:
                root(b + 9)
            pool.wait_ge(slot_data_ready, 1)
            pool.wait_ge(rows_stored, 16 * BATCH)
            pool.wait_ge(gate4_ready, BATCH * FT1)
            for s in range(GROUPS):
                nc.gpsimd.indirect_dma_start(out=xg[:, s, :], out_offset=None, in_=rows_dram,
                                             in_offset=bass.IndirectOffsetOnAxis(ap=gidx[:, s:s + 1], axis=0)).then_inc(gathered[s // 4], 16)
            with pool.Fori(0, TILES // 2) as j:
                root(j + 13)

        @block.scalar
        def _(act):
            def copy(o, i):
                return nc.scalar.activation(o, i, ACT.Copy)

            def split_wq(g):
                act.wait_ge(wq_loaded, 16 * g + 16)
                copy(wq[0][:], wq_in[:]).then_inc(wq_hi, 1)

            def split_wk(g):
                act.wait_ge(wk_loaded, 16 * g + 16)
                copy(wk[0][:], wk_in[:]).then_inc(wk_hi, 1)

            for b in range(BATCH):
                for k in range(KD):
                    act.wait_ge(x_turned, 2 * b + k + 1)
                    copy(xT[0][:, k, b * T:(b + 1) * T], ps[:, 2 * b + k, :]).then_inc(xhi_ready, 1)
            act.wait_ge(wd_loaded, 16)
            copy(wd[0][:], wd_in[:]).then_inc(wd_hi, 1)
            act.wait_ge(consts_ready, 6)
            copy(identr[:], ident[:]).then_inc(consts_ready, 1)
            for b in range(BATCH):
                act.wait_ge(c_ready, b + 1)
                copy(cT[0][:, b * T:(b + 1) * T], ps[:, b, :]).then_inc(chi_ready, 1)
            split_wq(0)
            split_wk(0)
            for b in range(BATCH):
                act.wait_ge(c_turned, b + 1)
                copy(c_tok[:, b * TPB:(b + 1) * TPB, :],
                     ps[:, 4 + b, :].rearrange("p (i l) -> p i l", i=TPB)).then_inc(ctok_ready, 1)
            for j in range(4):
                act.wait_ge(wv_turned, j + 1)
                copy(wvT[:, 4 * j:4 * j + 4, :], ps[:, WV_BANKS[j], :].rearrange("p (i l) -> p i l", i=4)).then_inc(wvT_ready, 1)
            for j in range(8):
                act.wait_ge(u_ready, j + 1)
                copy(U[:, 2 * j:2 * j + 2, :], ps[:, U_BANKS[j], :].rearrange("p (i l) -> p i l", i=2)).then_inc(u_copied, 1)

            def ffn_weights_halves(n):
                if n == 3:
                    act.wait_ge(gu_loaded, 32)
                    act.wait_ge(proj_ready, 6 + STEPS * (PAIRS - 1) + 2)
                if n == 5:
                    act.wait_ge(lb_loaded, 64)
                    act.wait_ge(la_loaded, 8 * 16)
                for halves, whole in w0_pieces[2 * (n - 3):2 * (n - 2)]:
                    copy(halves[0], whole).then_inc(w0_hi, 1)

            def step(g, n, first, last):
                s = g * STEPS + n
                start = first and n == 0
                hh = n % 2
                def exps(i):
                    act.wait_ge(negmax_ready, 4 * s + i + 1)
                    if not (first and n < 2) and i == 0:
                        act.wait_ge(transposed, 3 * s - 3)
                    off = P * (i * (i + 1) // 2)
                    nc.scalar.activation(probs[hh][:, off:off + (i + 1) * P], ps[:, BS + i % 2, 0:(i + 1) * P], ACT.Exp,
                                         bias=nm[:, hh, i:i + 1], scale=SCALE,
                                         accum_out=rs[:, hh, i:i + 1]).then_inc(probs_ready, 1)
                exps(0)
                exps(1)
                if not start:
                    act.wait_ge(pv_done, s)
                    copy(oT[:], ps[:, BO, :]).then_inc(ot_copied, 1)
                exps(2)
                exps(3)
                if n == 1 and not last:
                    act.wait_ge(proj_ready, s + 6)
                    split_wq(g + 1)
                if n == 2 and not last:
                    act.wait_ge(proj_ready, s + 6)
                    split_wk(g + 1)
                act.wait_ge(transposed, 3 * s + 1)
                if not start:
                    act.wait_ge(pv_done, s)
                copy(pT[:, 0, 0:2 * P], ps[:, BW + 2, 0:2 * P])
                copy(pT[:, 1, P:2 * P], ps[:, BW + 2, 2 * P:3 * P]).then_inc(pt_copied, 1)
                for i in (2, 3):
                    act.wait_ge(transposed, 3 * s + i)
                    copy(pT[:, 0:i + 1, i * P:(i + 1) * P],
                         ps[:, BW + i - 2, 0:(i + 1) * P].rearrange("p (k q) -> p k q", q=P)).then_inc(pt_copied, 1)
                if last and 3 <= n <= 5:
                    ffn_weights_halves(n)

            def pair(g, first, last):
                for n in range(STEPS):
                    step(g, n, first, last)

            pair(0, True, False)
            with act.Fori(1, PAIRS - 1) as g:
                pair(g, False, False)
            pair(PAIRS - 1, False, True)
            act.wait_ge(pv_done, STEPS * PAIRS)
            copy(oT[:], ps[:, BO, :]).then_inc(ot_copied, 1)

            def x1_halves(b):
                for k in range(KD):
                    act.wait_ge(x1_turned, b * KD + (k + 1))
                    copy(x1T[0][:, k, :], ps[:, 4 + k, :]).then_inc(x1hi_ready, 1)

            def scores0(b):
                act.wait_ge(logits_ready, b + 1)
                nc.scalar.activation(sig[:].rearrange("p (k i) e -> p k i e", k=2),
                                     ps[:, 6:8, 0:2 * NA].rearrange("p k (i c) -> p k i c", i=2)[:, :, :, 0:E0],
                                     ACT.Sigmoid).then_inc(sig_ready, 1)

            def xa_halves(b):
                for w in range(2):
                    act.wait_ge(xa_turned, b * 2 + (w + 1))
                    copy(xaT[0][:, w, :], ps[0:NL, 4 + w, :]).then_inc(xahi_ready, 1)

            def ffn0(b, last):
                for m, (f, size) in enumerate(F0S):
                    act.wait_ge(gate_ready, b * FT0 + (m + 1))
                    if m >= 2:
                        act.wait_ge(hid_ready, b * FT0 + (m - 1))
                    nc.scalar.activation(gated[m % 2][0:size, :], ps[0:size, m % 2, :], ACT.Silu).then_inc(gated_ready, 1)
                if not last:
                    x1_halves(b + 1)
                    scores0(b + 1)
                    xa_halves(b + 1)
                act.wait_ge(ha_turned, b + 1)
                copy(haT[:], ps[0:NL, 6, :]).then_inc(haT_ready, 1)
                act.wait_ge(x2_ready, b * TPB + TPB)
                t = bass.ds(b * TPB, TPB)
                copy(x2[0][:, t, :], acc[:, t, :]).then_inc(x2hi_ready, 1)

            x1_halves(0)
            scores0(0)
            xa_halves(0)
            with act.Fori(0, BATCH - 1) as b:
                ffn0(b, False)
            ffn0(BATCH - 1, True)

            def halve_wv3(c):
                act.wait_ge(wv3_loaded, 16 * c + 16)
                copy(wv3[0][:], wv3_in[:]).then_inc(wv3_hi, 1)

            def relu(o, i):
                return nc.scalar.activation(o, i, ACT.Relu)

            def keys(n, p, bank=1):
                act.wait_ge(k_ready, 4 * n + (p + 1))
                if p == 0 and not (isinstance(n, int) and n == 0):
                    act.wait_ge(g_ready, 2 * n)
                    act.wait_ge(ks_ready, n)
                relu(k3[0][:, p, :], ps[:, bank, :]).then_inc(khi_ready, 1)

            def grams(n):
                for k in range(KD):
                    act.wait_ge(g_ready, 2 * n + (k + 1))
                    if k == 0 and not (isinstance(n, int) and n == 0):
                        act.wait_ge(kv_ready, n)
                    copy(g3[0][:, k, :], ps[:, 2 + k, :]).then_inc(ghi_ready, 1)

            def key_sums(n):
                act.wait_ge(ks_ready, n + 1)
                if not (isinstance(n, int) and n == 0):
                    act.wait_ge(qk_ready, 4 * n)
                copy(ksb[:], ps[:, 5, :]).then_inc(ksb_ready, 1)

            def turned(u):
                act.wait_ge(qt_ready, u + 1)
                if not (isinstance(u, int) and u == 0):
                    act.wait_ge(out3_ready, u)
                copy(qn3[0][:], ps[:, 4, :].rearrange("p (j t) -> p j t", j=PPC)).then_inc(qnhi_ready, 1)

            def chunk3(c, first, last):
                for b in range(BATCH):
                    n = c * BATCH + b
                    for i in range(TPB):
                        u = c * (BATCH * TPB) + (b * TPB + i)
                        start = first and b == 0
                        act.wait_ge(q_ready, u + 1)
                        if not (start and i == 0):
                            act.wait_ge(qs_ready, u)
                        relu(q3[:], ps[:, 0, :]).then_inc(q_copied, 1)
                        if i == 0 and not (last and b == 3):
                            keys(n + 1, 0)
                        if i == 0:
                            act.wait_ge(kv_ready, n + 1)
                            if not start:
                                act.wait_ge(kvo_ready, 2 * n)
                            for h in range(2):
                                r = slice(64 * h, 64 * h + 64)
                                copy(kvT[0][r, :, r], ps[r, 2, :].rearrange("p (j e) -> p j e", j=PPC)[:, :, r]).then_inc(kvhi_ready, 1)
                        if i == 1:
                            for k in range(2):
                                act.wait_ge(kvo_ready, 2 * n + (k + 1))
                                if not start:
                                    act.wait_ge(out3_ready, 4 * n)
                                copy(kvo[0][:, 2 * k:2 * k + 2, :], ps[:, 3 + 2 * k, :].rearrange("p (j n) -> p j n", j=2)
                                     ).then_inc(kvohi_ready, 1)
                        if not (start and i == 0):
                            turned(u - 1)
                        if i < 3 and not (last and b == 3):
                            keys(n + 1, i + 1)
                        if b == 3 and i == 1 and not last:
                            halve_wv3(c + 1)
                        if i == 3 and not (last and b == 3):
                            grams(n + 1)
                            key_sums(n + 1)

            for b in range(BATCH):
                for k in range(KD):
                    act.wait_ge(x2_turned, b * KD + (k + 1))
                    copy(x2T[0][:, k, b * T:(b + 1) * T], ps[:, 2 * b + k, :]).then_inc(x2Thi_ready, 1)
            halve_wv3(0)
            for p in range(PPC):
                keys(0, p, FIRST_KEYS[p])
            grams(0)
            key_sums(0)
            act.wait_ge(zeroed, 6)
            chunk3(0, True, False)
            with act.Fori(1, CHUNKS - 1) as c:
                chunk3(c, False, False)
            chunk3(CHUNKS - 1, False, True)
            turned(BLOCKS * TPB - 1)

            def x3_halves(b):
                for k in range(KD):
                    act.wait_ge(x3_turned, b * KD + (k + 1))
                    copy(x3T[0][:, k, :], ps[:, k, :]).then_inc(x3hi_ready, 1)

            def route4(b, last):
                act.wait_ge(nmx4_ready, b + 1)
                for i in range(TPB):
                    nc.scalar.activation(e4[:, i, :], ps[:, 6, i * E1:(i + 1) * E1], ACT.Exp, bias=nmx4[:, i:i + 1],
                                         accum_out=sm4[:, i:i + 1]).then_inc(exp4, 1)
                for m, (f, size) in enumerate(F1T):
                    act.wait_ge(gate4_ready, b * FT1 + (m + 1))
                    wait_past(act, hid4_ready, b * FT1 + max(m - 1, 0))
                    nc.scalar.activation(gated4[m % 2][0:size, :], ps[0:size, m % 2, :], ACT.Silu).then_inc(gated4_ready, 1)
                if not last:
                    x3_halves(b + 1)

            x3_halves(0)
            act.wait_ge(gw_turned, 1)
            copy(gwT[0][:], ps[:, 2, 0:KD * E1].rearrange("p (k e) -> p k e", k=KD)).then_inc(sw_hi, 1)
            act.wait_ge(sw_loaded, 5 * 16)
            act.wait_ge(q_ready, BLOCKS * TPB)
            copy(sw[0][:], sw_in[:]).then_inc(sw_hi, 1)
            route4(0, False)
            with act.Fori(1, BATCH - 1) as b:
                route4(b, False)
            route4(BATCH - 1, True)
            wait_gathered(act, (0,))

            def weights(s):
                if not (isinstance(s, int) and s == 0):
                    act.wait_ge(xs_turned, s)
                copy(xs[:], xg[:, bass.ds(s, 1), 0:D]).then_inc(xs_ready, 1)

            def turned_rows(s, parity):
                act.wait_ge(xs_turned, s + 1)
                if not (isinstance(s, int) and s < 2):
                    act.wait_ge(gu4_ready, s - 1)
                copy(xsT[parity][:], ps[:, 0, 0:KD * P].rearrange("p (k n) -> p k n", k=KD)).then_inc(xsT_ready, 1)

            def gate(s, i):
                act.wait_ge(gu4_ready, s + 1)
                nc.scalar.activation(actE[:], ps[:, 1 + i % 2, 0:I1], ACT.Silu).then_inc(actE_ready, 1)

            def outputs4(s, i):
                act.wait_ge(y_mm, s + 1)
                nc.scalar.activation(y4[0][:, bass.ds(s, 1), :], ps[:, 4 + i % 2, 0:D], ACT.Copy,
                                     scale=wslot[:, bass.ds(s, 1)]).then_inc(yhi_ready, 1)

            def experts(s, i, first, left):
                act.wait_ge(hE_turned, s + 1)
                copy(hET[:], ps[0:IH, 3, 0:2 * P].rearrange("p (k n) -> p k n", k=2)).then_inc(hET_ready, 1)
                if left > 2:
                    turned_rows(s + 2, i % 2)
                if left > 3:
                    weights(s + 3)
                if not first:
                    outputs4(s - 1, i + 1)
                if left > 1:
                    gate(s + 1, i + 1)

            weights(0)
            turned_rows(0, 0)
            weights(1)
            turned_rows(1, 1)
            weights(2)
            gate(0, 0)
            for i in range(4):
                if i == 1:
                    act.wait_ge(slot_data_ready, 2)
                    wait_gathered(act, (1,))
                experts(i, i, i == 0, GROUPS - i)
            wait_gathered(act, (2, 3))
            with act.Fori(1, GROUPS // 4 - 1) as it:
                for i in range(4):
                    experts(it * 4 + i, i, False, 5)
            for i in range(4):
                experts(GROUPS - 4 + i, i, False, 4 - i)
            outputs4(GROUPS - 1, 3)

        @block.vector
        def _(dve):
            def rest(o, whole, hi):
                return nc.vector.tensor_tensor(o, whole, hi.bitcast(F32), ALU.subtract)

            def split_wq(g):
                dve.wait_ge(wq_hi, g + 1)
                rest(wq[1][:], wq_in[:], wq[0][:]).then_inc(wq_lo, 1)

            def split_wk(g):
                dve.wait_ge(wk_hi, g + 1)
                rest(wk[1][:], wk_in[:], wk[0][:]).then_inc(wk_lo, 1)

            def products(idx, parity, early):
                dve.wait_ge(proj_ready, idx + 1)
                if not early:
                    dve.wait_ge(roped, 4 * idx - 4)
                for w in range(2):
                    nc.vector.tensor_tensor(prod[parity][w][:], ps[:, BA:BA + 2, :],
                                            rope[:, w:w + 1, :].broadcast_to([P, 2, T]), ALU.mult).then_inc(products_ready, 1)

            for b in range(BATCH):
                for k in range(KD):
                    dve.wait_ge(xhi_ready, 2 * b + k + 1)
                    rest(xT[1][:, k, b * T:(b + 1) * T], ps[:, 2 * b + k, :],
                         xT[0][:, k, b * T:(b + 1) * T]).then_inc(xlo_ready, 1)
            dve.wait_ge(wd_hi, 1)
            rest(wd[1][:], wd_in[:], wd[0][:]).then_inc(wd_lo, 1)
            for b in range(BATCH):
                dve.wait_ge(chi_ready, b + 1)
                rest(cT[1][:, b * T:(b + 1) * T], ps[:, b, :], cT[0][:, b * T:(b + 1) * T]).then_inc(clo_ready, 1)
            split_wq(0)
            split_wk(0)
            dve.wait_ge(rope_loaded, 16)
            for b in range(BATCH - 1):
                products(2 * b, 0, b == 0)
                products(2 * b + 1, 1, b == 0)

            done = [0, 0]

            def link(ins):
                done[1] += 1
                return ins.then_inc(dchain, 1)

            def settle():
                dve.wait_ge(dchain, done[0] + done[1])

            def settle_by_memset():
                settle()
                nc.vector.memset(scratch[:], 0.0)

            def tiles(b):
                return [acc[:, bass.ds(b * TPB + i, 1), :] for i in range(TPB)]

            def statistics(tiles, n):
                nc.vector.memset(scratch[:], 0.0)
                for i, a in enumerate(tiles):
                    link(nc.vector.bn_stats(stat[:, i, :], a))
                settle_by_memset()
                for i in range(len(tiles)):
                    link(nc.vector.bn_aggr(meanvar[:, i, :], stat[:, i, :]))
                settle()
                nc.vector.tensor_scalar(vareps[:], meanvar[:, :, 1], EPS, None, ALU.add).then_inc(var_ready, 1)
                if n is not None:
                    dve.wait_ge(rstd_ready, n)

            def step(g, n, first, last):
                s = g * STEPS + n
                hh = n % 2
                def top(i):
                    dve.wait_ge(scores_ready, 4 * s + i + 1)
                    nc.vector.tensor_reduce(mx[:, hh, i:i + 1], ps[:, BS + i % 2, 0:(i + 1) * P], AX_X,
                                            ALU.max).then_inc(max_ready, 1)
                    dve.wait_ge(max_ready, 4 * s + i + 1)
                    nc.vector.tensor_scalar(nm[:, hh, i:i + 1], mx[:, hh, i:i + 1], -SCALE, None,
                                            ALU.mult).then_inc(negmax_ready, 1)
                top(0)
                top(1)
                if not (first and n == 0) and (n <= 2 or not last):
                    products(s + 5, (n + 1) % 2, False)
                top(2)
                top(3)
                if n == 1 and not last:
                    split_wq(g + 1)
                if n == 2 and not last:
                    split_wk(g + 1)
                if not (first and n == 0):
                    add(s - 1, (n - 1) % STEPS)
                dve.wait_ge(probs_ready, 4 * s + 4)
                nc.vector.reciprocal(rinv[:, hh, :], rs[:, hh, :]).then_inc(rinv_ready, 1)
                if last:
                    if n == 2:
                        dve.wait_ge(acc_added, 4 * s)
                        statistics(tiles(0), None)
                    if n == 3:
                        dve.wait_ge(rstd_ready, 1)
                        for i, a in enumerate(tiles(0)):
                            nc.vector.tensor_scalar(a, a, meanvar[:, i, 0:1], rstd[:, i:i + 1],
                                                    ALU.subtract, ALU.mult).then_inc(x1_ready, 1)
                    if n >= 4 and n <= 6:
                        for m in (2 * (n - 4), 2 * (n - 4) + 1):
                            halves, whole = w0_pieces[m]
                            dve.wait_ge(w0_hi, m + 1)
                            rest(halves[1], whole, halves[0]).then_inc(w0_lo, 1)

            def add(s, n):
                b, hh = n // 2, n % 2
                dve.wait_ge(rinv_ready, s + 1)
                for i in range(TPB):
                    dve.wait_ge(out_ready, 2 * s + i // 2 + 1)
                    if i == 0 and (not isinstance(s, int) or s > 0):
                        dve.wait_ge(acc_added, 4 * s)
                    a = acc[:, b * TPB + i, :]
                    nc.vector.scalar_tensor_tensor(out=a, in0=ps[:, BW + i // 2, (i % 2) * D:(i % 2 + 1) * D],
                                                   scalar=rinv[:, hh, i:i + 1], in1=a,
                                                   op0=ALU.mult, op1=ALU.add).then_inc(acc_added, 1)

            def pair(g, first, last):
                for n in range(STEPS):
                    step(g, n, first, last)

            pair(0, True, False)
            with dve.Fori(1, PAIRS - 1) as g:
                pair(g, False, False)
            pair(PAIRS - 1, False, True)
            add(STEPS * PAIRS - 1, STEPS - 1)

            def norm1(b):
                statistics(tiles(b), 2 * b)
                dve.wait_ge(x1_turned, 2 * b)
                for i, a in enumerate(tiles(b)):
                    nc.vector.tensor_scalar(x1s[:, i, :], a, meanvar[:, i, 0:1], rstd[:, i:i + 1],
                                            ALU.subtract, ALU.mult).then_inc(x1_ready, 1)
                for i, a in enumerate(tiles(b)):
                    link(nc.vector.tensor_scalar(a, a, meanvar[:, i, 0:1], rstd[:, i:i + 1], ALU.subtract, ALU.mult))

            def x1_rests(b):
                for k in range(KD):
                    dve.wait_ge(x1hi_ready, b * KD + (k + 1))
                    rest(x1T[1][:, k, :], ps[:, 4 + k, :], x1T[0][:, k, :]).then_inc(x1lo_ready, 1)

            def route0(b):
                dve.wait_ge(sig_ready, b + 1)
                link(nc.vector.tensor_tensor(biased[:], sig[:], ebias[:].rearrange("p (a e) -> p a e", a=1).broadcast_to([P, TPB, E0]),
                                             ALU.add))
                settle_by_memset()
                for i in range(TPB):
                    link(nc.vector.max(top8[:, i, :], biased[:, i, :]))
                settle_by_memset()
                for i in range(TPB):
                    link(nc.vector.max_index(topi[:, i, :], top8[:, i, :], biased[:, i, :]))
                settle()
                link(nc.vector.tensor_copy(topf[:], topi[:]))
                settle()
                for n, o in enumerate((one0, one1)):
                    link(nc.vector.tensor_tensor(o[:], iota8[:, 0:E0].rearrange("p (a e) -> p a e", a=1).broadcast_to([P, TPB, E0]),
                                                 topf[:, :, n:n + 1].broadcast_to([P, TPB, E0]), ALU.is_equal))
                settle()
                link(nc.vector.tensor_tensor(one0[:], one0[:], one1[:], ALU.add))
                settle()
                link(nc.vector.tensor_tensor(picked[:], one0[:], sig[:], ALU.mult))
                settle()
                link(nc.vector.tensor_reduce(den[:], picked[:], AX_X, ALU.add))
                settle()
                link(nc.vector.tensor_scalar(den[:], den[:], 1e-8, float(R0), ALU.add, ALU.mult))
                settle()
                link(nc.vector.reciprocal(den[:], den[:]))
                settle()
                link(nc.vector.tensor_tensor(wnext[:, :, 1:1 + E0], picked[:],
                                             den[:].rearrange("p (i a) -> p i a", a=1).broadcast_to([P, TPB, E0]), ALU.mult))
                settle()
                for i in range(TPB):
                    w = wnext[:, i:i + 1, :].rearrange("p a (e r) -> p a e r", r=1).broadcast_to([P, 2, 1 + E0, R0])
                    nc.vector.tensor_tensor(
                        xa[:, i, :].rearrange("p (w e r) -> p w e r", w=2, r=R0),
                        ps[:, 6 + i // 2, (i % 2) * NA + E0:(i % 2 + 1) * NA].rearrange("p (w e r) -> p w e r", w=2, r=R0),
                        w, ALU.mult).then_inc(xa_ready, 1)

            def take_weights():
                link(nc.vector.tensor_scalar(wexp[:], wnext[:], 1.0, None, ALU.mult))

            def xa_rests(b):
                for w in range(2):
                    dve.wait_ge(xahi_ready, b * 2 + (w + 1))
                    rest(xaT[1][:, w, :], ps[0:NL, 4 + w, :], xaT[0][:, w, :]).then_inc(xalo_ready, 1)

            def ffn0(b, last):
                for m, (f, size) in enumerate(F0S):
                    dve.wait_ge(gated_ready, b * FT0 + (m + 1))
                    if m == 0 and not (isinstance(b, int) and b == 0):
                        wait_past(dve, down_ready, b * TPB)
                    nc.vector.tensor_tensor(hidT[0:size, m, :], gated[m % 2][0:size, :], ps[0:size, 2 + m % 2, :],
                                            ALU.mult).then_inc(hid_ready, 1)
                    if m == 1 and not last:
                        norm1(b + 1)
                if not last:
                    x1_rests(b + 1)
                    route0(b + 1)
                for i in range(TPB):
                    dve.wait_ge(down_ready, b * TPB + (i + 1))
                    nc.vector.tensor_tensor(ha[:, i, :].rearrange("p (e r) -> p e r", r=R0),
                                            ps[:, i, D:D + NL].rearrange("p (e r) -> p e r", r=R0),
                                            wexp[:, i, :].rearrange("p (e r) -> p e r", r=1).broadcast_to([P, 1 + E0, R0]),
                                            ALU.mult).then_inc(ha_ready, 1)
                if not last:
                    dve.wait_ge(ha_ready, b * TPB + TPB)
                    take_weights()
                    xa_rests(b + 1)
                for i, a in enumerate(tiles(b)):
                    dve.wait_ge(ffn_ready, b * TPB + (i + 1))
                    nc.vector.tensor_tensor(a, a, ps[:, i:i + 1, 0:D], ALU.add).then_inc(ffn_added, 1)
                dve.wait_ge(ffn_added, b * TPB + TPB)
                statistics(tiles(b), 2 * BATCH if last else 2 * b + 3)
                for i, a in enumerate(tiles(b)):
                    nc.vector.tensor_scalar(a, a, meanvar[:, i, 0:1], rstd[:, i:i + 1],
                                            ALU.subtract, ALU.mult).then_inc(x2_ready, 1)

            dve.wait_ge(la_loaded, 8 * 16)
            dve.wait_ge(acc_added, 4 * STEPS * PAIRS)
            link(nc.vector.memset(wnext[:], 1.0 / R0))
            dve.wait_ge(x1_ready, TPB)
            x1_rests(0)
            route0(0)
            take_weights()
            xa_rests(0)
            before = done[1]
            done[0], done[1] = before, 0
            ffn0(0, False)
            with dve.Fori(1, BATCH - 1) as b:
                done[0], done[1] = b * LINKS0 + before, 0
                ffn0(b, False)
                assert done[1] == LINKS0, done
            done[0], done[1] = before + LINKS0 * (BATCH - 1), 0
            ffn0(BATCH - 1, True)

            def relu_rest(o, whole, hi):
                return nc.vector.scalar_tensor_tensor(out=o, in0=whole, scalar=0.0, in1=hi.bitcast(F32),
                                                      op0=ALU.max, op1=ALU.subtract)

            def halve_wv3(c):
                dve.wait_ge(wv3_hi, c + 1)
                rest(wv3[1][:], wv3_in[:], wv3[0][:]).then_inc(wv3_lo, 1)

            def keys(n, p, bank=1):
                dve.wait_ge(khi_ready, 4 * n + (p + 1))
                relu_rest(k3[1][:, p, :], ps[:, bank, :], k3[0][:, p, :]).then_inc(klo_ready, 1)

            def grams(n):
                for k in range(KD):
                    dve.wait_ge(ghi_ready, 2 * n + (k + 1))
                    rest(g3[1][:, k, :], ps[:, 2 + k, :], g3[0][:, k, :]).then_inc(glo_ready, 1)

            def turned(u):
                dve.wait_ge(qnhi_ready, u + 1)
                rest(qn3[1][:], ps[:, 4, :].rearrange("p (j t) -> p j t", j=PPC), qn3[0][:]).then_inc(qnlo_ready, 1)

            def add3(u, tile):
                a = acc[:, tile, :]
                dve.wait_ge(out3_ready, u + 1)
                nc.vector.tensor_tensor(a, a, ps[:, 6 + tile % 2, 0:D], ALU.add).then_inc(added3, 1)

            def chunk3(c, first, last):
                for b in range(BATCH):
                    n = c * BATCH + b
                    for i in range(TPB):
                        u = c * (BATCH * TPB) + (b * TPB + i)
                        start = first and b == 0
                        if i == 0 and not (last and b == 3):
                            keys(n + 1, 0)
                        if not (start and i < 2):
                            add3(u - 2, (b * TPB + i - 2) % TILES)
                        if i == 0:
                            dve.wait_ge(kvhi_ready, 2 * n + 2)
                            for h in range(2):
                                r = slice(64 * h, 64 * h + 64)
                                rest(kvT[1][r, :, r], ps[r, 2, :].rearrange("p (j e) -> p j e", j=PPC)[:, :, r],
                                     kvT[0][r, :, r]).then_inc(kvlo_ready, 1)
                        if i == 1:
                            for k in range(2):
                                dve.wait_ge(kvohi_ready, 2 * n + (k + 1))
                                at = slice(2 * k, 2 * k + 2)
                                rest(kvo[1][:, at, :], ps[:, 3 + 2 * k, :].rearrange("p (j n) -> p j n", j=2),
                                     kvo[0][:, at, :]).then_inc(kvolo_ready, 1)
                        if not (start and i == 0):
                            turned(u - 1)
                        dve.wait_ge(qk_ready, u + 1)
                        if not (start and i == 0):
                            dve.wait_ge(qs_ready, u)
                        nc.vector.tensor_reduce(nrm[:], qk[:].rearrange("p (h e) -> p h e", e=64), AX_X, ALU.add).then_inc(norm_ready, 1)
                        dve.wait_ge(norm_ready, 3 * u + 1)
                        nc.vector.tensor_scalar(nrm[:], nrm[:], 1e-6, None, ALU.max).then_inc(norm_ready, 1)
                        dve.wait_ge(norm_ready, 3 * u + 2)
                        nc.vector.reciprocal(nrm[:], nrm[:]).then_inc(norm_ready, 1)
                        dve.wait_ge(norm_ready, 3 * u + 3)
                        if not (start and i == 0):
                            dve.wait_ge(qt_ready, u)
                        nc.vector.tensor_tensor(qs[:].rearrange("p (h e) -> p h e", e=64), q3[:].rearrange("p (h e) -> p h e", e=64),
                                                nrm[:].rearrange("p (h a) -> p h a", a=1).broadcast_to([P, CH // 64, 64]),
                                                ALU.mult).then_inc(qs_ready, 1)
                        if i < 3 and not (last and b == 3):
                            keys(n + 1, i + 1)
                        if b == 3 and i == 1 and not last:
                            halve_wv3(c + 1)
                        if i == 3 and not (last and b == 3):
                            grams(n + 1)

            for b in range(BATCH):
                for k in range(KD):
                    dve.wait_ge(x2Thi_ready, b * KD + (k + 1))
                    rest(x2T[1][:, k, b * T:(b + 1) * T], ps[:, 2 * b + k, :],
                         x2T[0][:, k, b * T:(b + 1) * T]).then_inc(x2Tlo_ready, 1)
            halve_wv3(0)
            for p in range(PPC):
                keys(0, p, FIRST_KEYS[p])
            grams(0)
            dve.wait_ge(dn_loaded, 13 * 16)
            dve.wait_ge(x2lo_ready, BATCH)
            for b in range(BATCH):
                r = acc[:, b * TPB:(b + 1) * TPB, :]
                link(nc.vector.tensor_tensor(r, r, bo_sb[:].rearrange("p (a n) -> p a n", a=1).broadcast_to([P, TPB, D]), ALU.add))
            settle()
            dve.wait_ge(zeroed, 6)
            chunk3(0, True, False)
            with dve.Fori(1, CHUNKS - 1) as c:
                chunk3(c, False, False)
            chunk3(CHUNKS - 1, False, True)
            add3(BLOCKS * TPB - 2, TILES - 2)
            dve.wait_ge(added3, BLOCKS * TPB - 1)
            link(nc.vector.memset(slots[:], 0.0))
            statistics(tiles(0), None)
            turned(BLOCKS * TPB - 1)

            def hidden4(b, m):
                f, size = F1T[m]
                dve.wait_ge(gated4_ready, b * FT1 + (m + 1))
                nc.vector.tensor_tensor(hid4[0:size, m, :], gated4[m % 2][0:size, :], ps[0:size, 2 + m % 2, :],
                                        ALU.mult).then_inc(hid4_ready, 1)

            def bcast(ap, shape):
                return ap.broadcast_to(shape)

            def rows4(b):
                dve.wait_ge(rstd_ready, b + 9)
                wait_past(dve, rows_stored, 16 * b)
                for i, a in enumerate(tiles(b)):
                    nc.vector.tensor_scalar(rows[:, i, 0:D], a, meanvar[:, i, 0:1], rstd[:, i:i + 1],
                                            ALU.subtract, ALU.mult).then_inc(x3_ready, 1)

            def norm4(b):
                for i, a in enumerate(tiles(b)):
                    link(nc.vector.tensor_scalar(a, a, meanvar[:, i, 0:1], rstd[:, i:i + 1], ALU.subtract, ALU.mult))

            def x3_rests(b):
                for k in range(KD):
                    dve.wait_ge(x3hi_ready, b * KD + (k + 1))
                    rest(x3T[1][:, k, :], ps[:, k, :], x3T[0][:, k, :]).then_inc(x3lo_ready, 1)

            def route4(b, last):
                dve.wait_ge(logits4, b + 1)
                link(nc.vector.tensor_reduce(mx4[:], ps[:, 6, 0:TPB * E1].rearrange("p (i e) -> p i e", i=TPB), AX_X, ALU.max))
                settle()
                nc.vector.tensor_scalar(nmx4[:], mx4[:], -1.0, None, ALU.mult).then_inc(nmx4_ready, 1)
                dve.wait_ge(exp4, b * TPB + TPB)
                link(nc.vector.reciprocal(sm4[:], sm4[:]))
                settle()
                nc.vector.tensor_tensor(rows[:, :, D:ROW], e4[:], bcast(sm4[:].rearrange("p (i a) -> p i a", a=1), [P, TPB, E1]),
                                        ALU.mult).then_inc(scored, 1)
                dve.wait_ge(scored, b + 1)
                nc.vector.memset(scratch[:], 0.0)
                for i in range(TPB):
                    link(nc.vector.max(top4[:, i, :], rows[:, i, D:ROW]))
                settle_by_memset()
                for i in range(TPB):
                    link(nc.vector.max_index(top4i[:, i, :], top4[:, i, :], rows[:, i, D:ROW]))
                settle()
                link(nc.vector.tensor_copy(top4f[:], top4i[:]))
                hidden4(b, 0)
                for k in range(TOP1):
                    settle()
                    for i in range(TPB):
                        which = top4f[:, i, k:k + 1]
                        if k == 0:
                            ins = nc.vector.tensor_scalar(sel[:, i, :], iota8[:], which, None, ALU.is_equal)
                        else:
                            ins = nc.vector.scalar_tensor_tensor(out=sel[:, i, :], in0=iota8[:], scalar=which, in1=sel[:, i, :],
                                                                 op0=ALU.is_equal, op1=ALU.add)
                        if k < TOP1 - 1:
                            link(ins)
                        else:
                            ins.then_inc(sel_ready, 1)
                dve.wait_ge(sel_ready, b * TPB + TPB)
                if not last:
                    statistics(tiles(b + 1), None)
                link(nc.vector.tensor_scalar(pm[:], sel[:], -2.0 * CAP, 2.0 * CAP, ALU.mult, ALU.add))
                link(nc.vector.tensor_reduce(selsum[:], sel[:].rearrange("p i e -> p e i"), AX_X, ALU.add))
                hidden4(b, 1)
                hidden4(b, 2)
                if not last:
                    rows4(b + 1)
                dve.wait_ge(pos_ready, b + 1)
                settle()
                link(nc.vector.scalar_tensor_tensor(out=posb[:].rearrange("p i e -> p (i e)"), in0=ps[:, 7, 0:TPB * E1], scalar=float(CAP),
                                                    in1=pm[:].rearrange("p i e -> p (i e)"), op0=ALU.min, op1=ALU.add))
                nc.vector.tensor_tensor(carry[:], carry[:], selsum[:], ALU.add).then_inc(carry_ready, 1)
                settle()
                for i in range(TPB):
                    if i == 2 and not last:
                        x3_rests(b + 1)
                    if i >= 2:
                        dve.wait_ge(onehot_used, b * TPB + (i - 1))
                    nc.vector.tensor_tensor(onehot[i % 2][:], bcast(posb[:, i, :].rearrange("p (e a) -> p e a", a=1), [P, E1, CAP]), capi[:],
                                            ALU.is_equal).then_inc(onehot_ready, 1)
                if not last:
                    norm4(b + 1)
                for i, a in enumerate(tiles(b)):
                    dve.wait_ge(down4, b * TPB + (2 if i < 2 else 4))
                    nc.vector.tensor_tensor(a, a, ps[:, 4 + i // 2, (i % 2) * D:(i % 2 + 1) * D].rearrange("p (a n) -> p a n", a=1),
                                            ALU.add).then_inc(added4, 1)
                dve.wait_ge(onehot_used, b * TPB + TPB)
                flat = slots[:].rearrange("p s c -> p (s c)")
                nc.vector.tensor_tensor(flat, flat, ps[:, 7, TPB * E1:TPB * E1 + 4 * GROUPS], ALU.add).then_inc(slots_added, 1)
                dve.wait_ge(slots_added, b + 1)

            rows4(0)
            add3(BLOCKS * TPB - 1, TILES - 1)
            norm4(0)
            x3_rests(0)
            dve.wait_ge(sw_hi, 1)
            rest(gwT[1][:], ps[:, 2, 0:KD * E1].rearrange("p (k e) -> p k e", k=KD), gwT[0][:]).then_inc(sw_lo, 1)
            dve.wait_ge(sw_hi, 2)
            rest(sw[1][:], sw_in[:], sw[0][:]).then_inc(sw_lo, 1)
            before4 = done[0] + done[1]
            done[0], done[1] = before4, 0
            route4(0, False)
            with dve.Fori(1, BATCH - 1) as b:
                done[0], done[1] = b * LINKS4 + before4, 0
                route4(b, False)
                assert done[1] == LINKS4, done
            done[0], done[1] = before4 + LINKS4 * (BATCH - 1), 0
            route4(BATCH - 1, True)
            link(nc.vector.scalar_tensor_tensor(out=idxf[:], in0=slots[:, :, 0], scalar=-1.0, in1=slots[:, :, 1],
                                                op0=ALU.add, op1=ALU.add))
            settle()
            link(nc.vector.tensor_tensor(idxf[:], idxf[:], slots[:, :, 2], ALU.add))
            settle()
            nc.vector.tensor_scalar(gidx[:], idxf[:], 0.0, None, ALU.max).then_inc(slot_data_ready, 1)
            def pick_tokens(t, buf):
                nc.vector.scalar_tensor_tensor(
                    out=pick[buf][:], in0=bcast(iota_t[:].rearrange("p (a n) -> p a n", a=1), [P, GROUPS, P]),
                    scalar=tbase[:, bass.ds(t, 1)], in1=bcast(idxf[:].rearrange("p (s a) -> p s a", a=1), [P, GROUPS, P]),
                    op0=ALU.add, op1=ALU.is_equal).then_inc(pick_ready, 1)

            def hidden_rows(s, i):
                dve.wait_ge(actE_ready, s + 1)
                nc.vector.tensor_tensor(hE[:], actE[:], ps[:, 1 + i % 2, I1:2 * I1], ALU.mult).then_inc(hE_ready, 1)

            def rest_of_outputs(s, i):
                dve.wait_ge(yhi_ready, s + 1)
                at = bass.ds(s, 1)
                nc.vector.scalar_tensor_tensor(out=y4[1][:, at, :].rearrange("p a n -> p (a n)"), in0=ps[:, 4 + i % 2, 0:D],
                                               scalar=wslot[:, at], in1=y4[0][:, at, :].rearrange("p a n -> p (a n)").bitcast(F32),
                                               op0=ALU.mult, op1=ALU.subtract).then_inc(ylo_ready, 1)

            settle()
            pick_tokens(0, 0)
            pick_tokens(1, 1)
            hidden_rows(0, 0)
            hidden_rows(1, 1)
            wait_gathered(dve, range(4))
            for s in range(GROUPS):
                link(nc.vector.tensor_tensor(wtmp[:, s, :], xg[:, s, D + 4 * s:D + 4 * s + 4], quarter[:], ALU.mult))
            settle()
            nc.vector.tensor_reduce(wslot[:], wtmp[:], AX_X, ALU.add).then_inc(slot_data_ready, 1)
            dve.wait_ge(slot_data_ready, 2)

            for i in range(1, 4):
                rest_of_outputs(i - 1, i + 1)
                hidden_rows(i + 1, i + 1)
            with dve.Fori(1, GROUPS // 4 - 1) as it:
                for i in range(4):
                    rest_of_outputs(it * 4 + i - 1, i + 1)
                    hidden_rows(it * 4 + (i + 1), i + 1)
            for i in range(4):
                rest_of_outputs(GROUPS - 5 + i, i + 1)
                if i < 3:
                    hidden_rows(GROUPS - 3 + i, i + 1)
            rest_of_outputs(GROUPS - 1, 3)

            def pair_of(j):
                return [acc[:, bass.ds(2 * j + i, 1), :] for i in range(2)]

            def normalise(j):
                dve.wait_ge(rstd_ready, j + 13)
                wait_past(dve, stored, 16 * j)
                for i, a in enumerate(pair_of(j)):
                    nc.vector.tensor_scalar(fin[:, i, :], a, meanvar[:, i, 0:1], rstd[:, i:i + 1],
                                            ALU.subtract, ALU.mult).then_inc(fin_ready, 1)

            def combine(j, first, last):
                pair = pair_of(j)
                for i, a in enumerate(pair):
                    t = 2 * j + i
                    dve.wait_ge(comb_ready, t + 1)
                    if not last:
                        pick_tokens(t + 2, i)
                    nc.vector.tensor_tensor(a, a, ps[:, 6 + i, 0:D].rearrange("p (a n) -> p a n", a=1), ALU.add).then_inc(comb_added, 1)
                    if i == 0 and not first:
                        normalise(j - 1)
                dve.wait_ge(comb_added, 2 * j + 2)
                statistics(pair, None)

            before5 = done[0] + done[1]
            done[0], done[1] = before5, 0
            combine(0, True, False)
            done[0], done[1] = before5 + 4, 0
            combine(1, False, False)
            with dve.Fori(2, TILES // 2 - 1) as j:
                done[0], done[1] = j * 4 + before5, 0
                combine(j, False, False)
                assert done[1] == 4, done
            done[0], done[1] = before5 + 4 * (TILES // 2 - 1), 0
            combine(TILES // 2 - 1, False, True)
            normalise(TILES // 2 - 1)

        @block.tensor
        def _(pe):
            def mm3(o, lhs, rhs, start, stop):
                for j, (a, c) in enumerate(HALVES):
                    last = pe.matmul(o, lhs(a), rhs(c), start=start and j == 0, stop=stop and j == 2)
                return last

            pe.wait_ge(consts_ready, 6)
            for b in range(BATCH):
                pe.wait_ge(x_in[b], 16)
                for k in range(KD):
                    for i in range(TPB):
                        last = pe.transpose(ps[:, 2 * b + k, i * P:(i + 1) * P],
                                            acc[:, b * TPB + i, k * P:(k + 1) * P], ident[:])
                    last.then_inc(x_turned, 1)
            pe.wait_ge(wd_lo, 1)
            for b in range(BATCH):
                pe.wait_ge(xlo_ready, 2 * b + 2)
                for k in range(KD):
                    last = mm3(ps[:, b, :], lambda a: wd[a][:, k, :],
                               lambda c: xT[c][:, k, b * T:(b + 1) * T], k == 0, k == KD - 1)
                last.then_inc(c_ready, 1)
            for b in range(BATCH):
                if b == 0:
                    pe.wait_ge(consts_ready, 7)
                pe.wait_ge(clo_ready, b + 1)
                for i in range(TPB):
                    t0 = b * T + i * P
                    for h in range(2):
                        last = pe.matmul(ps[:, 4 + b, i * P:(i + 1) * P], cT[h][:, t0:t0 + P], identr[:],
                                         start=h == 0, stop=h == 1)
                last.then_inc(c_turned, 1)
            def project(which, b, idx, g):
                if not (isinstance(idx, int) and idx == 0):
                    pe.wait_ge(products_ready, 2 * idx)
                pe.wait_ge(wq_lo if which == 0 else wk_lo, g + 1)
                t = slice(b * T, (b + 1) * T)
                for half in range(2):
                    o = ps[:, BA + half, :]
                    if which == 0:
                        for k in range(KD):
                            last = mm3(o, lambda a: wq[a][:, k, half:2 * DH:2], lambda c: xT[c][:, k, t], k == 0, k == KD - 1)
                    else:
                        last = mm3(o, lambda a: wk[a][:, half:2 * DH:2], lambda c: cT[c][:, t], True, True)
                last.then_inc(proj_ready, 1)

            def turn_wv():
                pe.wait_ge(wvo_loaded, 32)
                for j in range(4):
                    if j == 2:
                        pe.wait_ge(ctok_ready, 4)
                    for i in range(4):
                        last = pe.transpose(ps[:, WV_BANKS[j], i * P:(i + 1) * P], wv[:, 4 * j + i, :], ident[:])
                    last.then_inc(wv_turned, 1)

            def multiply_wv_wo(j):
                turned_here = WV_BANKS.index(U_BANKS[j]) + 1 if U_BANKS[j] in WV_BANKS else 0
                pe.wait_ge(wvT_ready, max(j // 2 + 1, turned_here))
                if j >= 6:
                    pe.wait_ge(u_copied, j - 5)
                for i in range(2):
                    last = pe.matmul(ps[:, U_BANKS[j], i * D:(i + 1) * D], wvT[:, 2 * j + i, :],
                                     wo[:, 2 * j + i, :], start=True, stop=True)
                last.then_inc(u_ready, 1)

            project(0, 0, 0, 0)
            turn_wv()
            for idx in range(1, 2 * (BATCH - 1)):
                project(idx % 2, idx // 2, idx, 0)
                for j in range(2 * idx - 2, min(2 * idx, 8)):
                    multiply_wv_wo(j)
            pe.wait_ge(u_copied, 8)

            def pv_and(s, n):
                b = n // 2
                pe.wait_ge(pt_copied, 3 * s + 3)
                if not isinstance(s, int) or s > 0:
                    pe.wait_ge(ot_copied, s)
                for k in range(TPB):
                    last = pe.matmul(ps[:, BO, k * P:T], c_tok[:, b * TPB + k, :], pT[:, k, k * P:T],
                                     start=k == 0, stop=k == TPB - 1)
                last.then_inc(pv_done, 1)

            def project_out(s, g, n):
                pe.wait_ge(ot_copied, s + 1)
                for i in range(TPB):
                    last = pe.matmul(ps[:, BW + i // 2, (i % 2) * D:(i % 2 + 1) * D], oT[:, i * P:(i + 1) * P],
                                     U[:, bass.ds(2 * g + n % 2, 1), :], start=True, stop=True)
                    if i % 2:
                        last.then_inc(out_ready, 1)

            def step(g, n, first, last_pair):
                s = g * STEPS + n
                b, hh = n // 2, n % 2
                before = (s - 1, g if n else g - 1, (n - 1) % STEPS)

                def scores(i):
                    if not (first and n == 0 and i < 2):
                        pe.wait_ge(probs_ready, 4 * s + i - 1)
                    bank = BS + i % 2
                    pe.matmul(ps[:, bank, 0:(i + 1) * P], qT[:, hh, b, i * P:(i + 1) * P], kT[:, hh, b, 0:(i + 1) * P],
                              start=True, stop=False)
                    pe.matmul(ps[:, bank, i * P:(i + 1) * P], identb[:], maskb[:],
                              start=False, stop=True).then_inc(scores_ready, 1)

                pe.wait_ge(roped, g * (4 * STEPS) + 4 * (2 * b + 2))
                scores(0)
                scores(1)
                if not (first and n == 0):
                    pv_and(before[0], before[2])
                scores(2)
                scores(3)
                if not (first and n == 0):
                    project_out(*before)
                if n < 2 or not last_pair:
                    project(n % 2, (3, 0, 1, 2)[n // 2], s + 6, g if n < 2 else g + 1)
                for i in range(TPB):
                    pe.wait_ge(probs_ready, 4 * s + i + 1)
                    if not (first and n == 0):
                        if i == 0:
                            pe.wait_ge(pt_copied, 3 * s - 2)
                        if i >= 2:
                            pe.wait_ge(acc_added, 4 * s - 4 + 2 * (i - 1))
                    bank = BW + (2, 2, 0, 1)[i]
                    for k in range(i + 1):
                        at = k if i != 1 else k + 1
                        off = P * (i * (i + 1) // 2 + k)
                        last = pe.transpose(ps[:, bank, at * P:(at + 1) * P], probs[hh][:, off:off + P], ident[:])
                    if i:
                        last.then_inc(transposed, 1)

            def pair(g, first, last):
                for n in range(STEPS):
                    step(g, n, first, last)

            pair(0, True, False)
            with pe.Fori(1, PAIRS - 1) as g:
                pair(g, False, False)
            pair(PAIRS - 1, False, True)
            pv_and(STEPS * PAIRS - 1, STEPS - 1)
            project_out(STEPS * PAIRS - 1, PAIRS - 1, STEPS - 1)

            def turn_x1(b, first):
                pe.wait_ge(x1_ready, b * TPB + TPB)
                if first:
                    pe.wait_ge(pt_copied, 3 * STEPS * PAIRS)
                    pe.wait_ge(acc_added, 4 * STEPS * PAIRS)
                else:
                    pe.wait_ge(xalo_ready, b * 2)
                for k in range(KD):
                    for i in range(TPB):
                        rows_in = acc if first else x1s
                        last = pe.transpose(ps[:, 4 + k, i * P:(i + 1) * P], rows_in[:, i, k * P:(k + 1) * P], ident[:])
                    last.then_inc(x1_turned, 1)

            def first_products(b, first):
                pe.wait_ge(x1lo_ready, b * KD + KD)
                if not first:
                    pe.wait_ge(xa_ready, b * TPB)
                for i in range(TPB):
                    for k in range(KD):
                        last = mm3(ps[:, 6 + i // 2, (i % 2) * NA:(i % 2 + 1) * NA],
                                   lambda a: x1T[a][:, k, i * P:(i + 1) * P], lambda c: la[c][:, k, :], k == 0, k == KD - 1)
                last.then_inc(logits_ready, 1)

            def turn_xa(b):
                pe.wait_ge(xa_ready, b * TPB + TPB)
                pe.wait_ge(x1lo_ready, b * KD + KD)
                for w in range(2):
                    for i in range(TPB):
                        last = pe.transpose(ps[0:NL, 4 + w, i * P:(i + 1) * P], xa[:, i, w * NL:(w + 1) * NL], ident[:])
                    last.then_inc(xa_turned, 1)

            def ffn0(b, first, last_one):
                def base(m, w):
                    f, size = F0S[m]
                    for k in range(KD):
                        mm3(ps[0:size, 2 * w + m % 2, :], lambda a: gu[a][:, k, w, f:f + size],
                            lambda c: x1T[c][:, k, :], k == 0, False)

                def lora(m, w):
                    f, size = F0S[m]
                    last = mm3(ps[0:size, 2 * w + m % 2, :], lambda a: lb[a][:, w, f:f + size],
                               lambda c: xaT[c][:, w, :], False, True)
                    if w:
                        last.then_inc(gate_ready, 1)

                if not first:
                    pe.wait_ge(ffn_added, b * TPB)
                for m in range(2):
                    for w in range(2):
                        base(m, w)
                if first:
                    turn_xa(0)
                pe.wait_ge(xalo_ready, b * 2 + 2)
                for m in range(FT0):
                    if m >= 2:
                        pe.wait_ge(hid_ready, b * FT0 + (m - 1))
                        for w in range(2):
                            base(m, w)
                    for w in range(2):
                        lora(m, w)
                if not last_one:
                    turn_x1(b + 1, False)
                    first_products(b + 1, False)
                pe.wait_ge(hid_ready, b * FT0 + FT0)
                for i in range(TPB):
                    for m, (f, size) in enumerate(F0S):
                        last = pe.matmul(ps[:, i, 0:D + NL], hidT[0:size, m, i * P:(i + 1) * P], dn[0:size, m, :],
                                         start=m == 0, stop=m == FT0 - 1)
                    last.then_inc(down_ready, 1)
                if not last_one:
                    turn_xa(b + 1)
                pe.wait_ge(ha_ready, b * TPB + TPB)
                for i in range(TPB):
                    last = pe.transpose(ps[0:NL, 6, i * P:(i + 1) * P], ha[:, i, :], ident[:])
                last.then_inc(ha_turned, 1)
                pe.wait_ge(haT_ready, b + 1)
                for i in range(TPB):
                    pe.matmul(ps[:, i, 0:D], haT[:, i * P:(i + 1) * P], ldn[:], start=False, stop=True,
                              skip_group_check=True).then_inc(ffn_ready, 1)

            turn_x1(0, True)
            pe.wait_ge(w0_lo, 6)
            first_products(0, True)
            pe.wait_ge(dn_loaded, 13 * 16)
            ffn0(0, True, False)
            with pe.Fori(1, BATCH - 1) as b:
                ffn0(b, False, False)
            ffn0(BATCH - 1, False, True)

            def queries(u, b, i):
                if not (isinstance(u, int) and u == 0):
                    pe.wait_ge(q_copied, u)
                t0 = b * T + i * P
                for k in range(KD):
                    last = mm3(ps[:, 0, :], lambda a: x2T[a][:, k, t0:t0 + P], lambda h: wq3[h][:, k, :], k == 0, k == KD - 1)
                last.then_inc(q_ready, 1)

            def keys(n, c, b, p, bank=1):
                if not (isinstance(n, int) and n == 0):
                    pe.wait_ge(klo_ready, 4 * n + p)
                t0 = b * T + p * P
                for k in range(KD):
                    last = mm3(ps[:, bank, :], lambda a: x2T[a][:, k, t0:t0 + P],
                               lambda h: wk3[h][:, bass.ds(c, 1), k, :], k == 0, k == KD - 1)
                last.then_inc(k_ready, 1)

            def grams(n, b):
                pe.wait_ge(klo_ready, 4 * n + 4)
                for k in range(KD):
                    if not (isinstance(n, int) and n == 0):
                        if k == 0:
                            pe.wait_ge(kvlo_ready, 2 * n)
                        else:
                            pe.wait_ge(kvolo_ready, 2 * n)
                    for i in range(TPB):
                        last = mm3(ps[:, 2 + k, :], lambda a: x2[a][:, b * TPB + i, k * P:(k + 1) * P],
                                   lambda c: k3[c][:, i, :], i == 0, i == TPB - 1)
                    last.then_inc(g_ready, 1)

            def key_sums(n):
                if not (isinstance(n, int) and n == 0):
                    pe.wait_ge(kvolo_ready, 2 * n)
                for i in range(TPB):
                    for h in range(2):
                        last = pe.matmul(ps[:, 5, :], onesr[:], k3[h][:, i, :], start=i == 0 and h == 0,
                                         stop=i == TPB - 1 and h == 1)
                last.then_inc(ks_ready, 1)

            def key_values(n):
                pe.wait_ge(glo_ready, 2 * n + 2)
                for p in range(PPC):
                    j = slice(p * P, (p + 1) * P)
                    for k in range(KD):
                        last = mm3(ps[:, 2, j], lambda a: wv3[a][:, k, j], lambda c: g3[c][:, k, j], k == 0, k == KD - 1)
                last.then_inc(kv_ready, 1)

            def turn(u):
                pe.wait_ge(qs_ready, u + 1)
                if not (isinstance(u, int) and u == 0):
                    pe.wait_ge(qnlo_ready, u)
                for p in range(PPC):
                    last = pe.transpose(ps[:, 4, p * P:(p + 1) * P], qs[:, p * P:(p + 1) * P], ident[:])
                last.then_inc(qt_ready, 1)

            def key_value_outputs(n, c):
                pe.wait_ge(kvlo_ready, 2 * n + 2)
                pe.wait_ge(wo3_ready, c * PPC + PPC)
                pe.wait_ge(ksb_ready, n + 1)
                for p in range(PPC):
                    last = mm3(ps[:, 3 + p // 2 * 2, (p % 2) * D:(p % 2 + 1) * D], lambda a: kvT[a][:, p, :],
                               lambda h: wo3[h][:, p, :], True, True)
                    if p % 2:
                        last.then_inc(kvo_ready, 1)

            def outputs(u, n, i):
                pe.wait_ge(qnlo_ready, u + 1)
                if i == 0:
                    pe.wait_ge(kvolo_ready, 2 * n + 2)
                if not (isinstance(u, int) and u < 2):
                    pe.wait_ge(added3, u - 1)
                for p in range(PPC):
                    last = mm3(ps[:, 6 + i % 2, 0:D], lambda a: qn3[a][:, p, :], lambda h: kvo[h][:, p, :],
                               p == 0, p == PPC - 1)
                last.then_inc(out3_ready, 1)

            def chunk3(c, first, last):
                for b in range(BATCH):
                    n = c * BATCH + b
                    for i in range(TPB):
                        u = c * (BATCH * TPB) + (b * TPB + i)
                        start = first and b == 0
                        if b == 0 and i == 0:
                            pe.wait_ge(wq3_ready, c * PPC + PPC)
                        queries(u, b, i)
                        c_next = c if b < 3 else c + 1
                        if i == 0 and not (last and b == 3):
                            if b == 3:
                                pe.wait_ge(wk3_ready, c + 2)
                            keys(n + 1, c_next, (b + 1) % BATCH, 0)
                        if not (start and i < 2):
                            outputs(u - 2, n if i >= 2 else n - 1, (i - 2) % TPB)
                        if i == 0:
                            pe.wait_ge(wv3_lo, c + 1)
                            key_values(n)
                        if i == 1:
                            key_value_outputs(n, c)
                        if not (start and i == 0):
                            turn(u - 1)
                        if i < 3 and not (last and b == 3):
                            keys(n + 1, c_next, (b + 1) % BATCH, i + 1)
                        if i == 3 and not (last and b == 3):
                            grams(n + 1, (b + 1) % BATCH)
                            key_sums(n + 1)

            pe.wait_ge(ffn_added, TILES)
            for b in range(BATCH):
                pe.wait_ge(x2_ready, b * TPB + TPB)
                for k in range(KD):
                    for i in range(TPB):
                        last = pe.transpose(ps[:, 2 * b + k, i * P:(i + 1) * P],
                                            acc[:, b * TPB + i, k * P:(k + 1) * P], ident[:])
                    last.then_inc(x2_turned, 1)
            pe.wait_ge(x2Tlo_ready, BATCH * KD)
            pe.wait_ge(wk3_ready, 1)
            for p in range(PPC):
                keys(0, 0, 0, p, FIRST_KEYS[p])
            pe.wait_ge(x2lo_ready, BATCH)
            grams(0, 0)
            pe.wait_ge(zeroed, 6)
            key_sums(0)
            chunk3(0, True, False)
            with pe.Fori(1, CHUNKS - 1) as c:
                chunk3(c, False, False)
            chunk3(CHUNKS - 1, False, True)
            outputs(BLOCKS * TPB - 2, BLOCKS - 1, TPB - 2)
            turn(BLOCKS * TPB - 1)

            def turn_x3(b):
                pe.wait_ge(x3_ready, b * TPB + TPB)
                wait_past(pe, hid4_ready, b * FT1)
                for k in range(KD):
                    for i in range(TPB):
                        last = pe.transpose(ps[:, k, i * P:(i + 1) * P], rows[:, i, k * P:(k + 1) * P], ident[:])
                    last.then_inc(x3_turned, 1)

            def logits(b):
                pe.wait_ge(x3lo_ready, b * KD + KD)
                pe.wait_ge(sw_lo, 1)
                wait_past(pe, exp4, b * TPB)
                for i in range(TPB):
                    for k in range(KD):
                        last = mm3(ps[:, 6, i * E1:(i + 1) * E1], lambda a: x3T[a][:, k, i * P:(i + 1) * P],
                                   lambda c: gwT[c][:, k, :], k == 0, k == KD - 1)
                last.then_inc(logits4, 1)

            def route4(b, last_batch):
                for m, (f, size) in enumerate(F1T):
                    wait_past(pe, hid4_ready, b * FT1 + max(m - 1, 0))
                    for w in range(2):
                        for k in range(KD):
                            last = mm3(ps[0:size, 2 * w + m % 2, :], lambda a: sw[a][:, k, w, f:f + size],
                                       lambda c: x3T[c][:, k, :], k == 0, k == KD - 1)
                    last.then_inc(gate4_ready, 1)
                pe.wait_ge(sel_ready, b * TPB + TPB)
                pe.wait_ge(consts4, 14)
                wait_past(pe, carry_ready, b)
                wait_past(pe, slots_added, b)
                for i in range(TPB):
                    o = ps[:, 7, i * E1:(i + 1) * E1]
                    pe.matmul(o, tri[:], sel[:, i, :], start=True, stop=False)
                    for j in range(i):
                        pe.matmul(o, onesb[:], sel[:, j, :], start=False, stop=False)
                    last = pe.matmul(o, onesb[:], carry[:], start=False, stop=True)
                last.then_inc(pos_ready, 1)
                pe.wait_ge(hid4_ready, b * FT1 + FT1)
                if not last_batch:
                    turn_x3(b + 1)
                wait_past(pe, added4, b * TPB)
                for i in range(TPB):
                    for m, (f, size) in enumerate(F1T):
                        last = pe.matmul(ps[:, 4 + i // 2, (i % 2) * D:(i % 2 + 1) * D], hid4[0:size, m, i * P:(i + 1) * P],
                                         swd[0:size, m, :], start=m == 0, stop=m == FT1 - 1)
                    last.then_inc(down4, 1)
                for i in range(TPB):
                    if i == 2 and not last_batch:
                        logits(b + 1)
                    pe.wait_ge(onehot_ready, b * TPB + (i + 1))
                    for s in range(GROUPS):
                        last = pe.matmul(ps[:, 7, TPB * E1 + 4 * s:TPB * E1 + 4 * s + 4],
                                         onehot[i % 2][:, 4 * s:4 * s + 4, :].rearrange("p e c -> p (e c)"),
                                         tokv[:, bass.ds(b * TPB + i, 1), :], start=i == 0 and s == 0, stop=i == TPB - 1,
                                         skip_group_check=True)
                    last.then_inc(onehot_used, 1)

            pe.wait_ge(q_copied, BLOCKS * TPB)
            turn_x3(0)
            outputs(BLOCKS * TPB - 1, BLOCKS - 1, TPB - 1)
            pe.wait_ge(sw_loaded, 5 * 16)
            for k in range(KD):
                last = pe.transpose(ps[:, 2, k * E1:(k + 1) * E1], gw_in[:, k * P:(k + 1) * P], ident[0:E1, 0:E1])
            last.then_inc(gw_turned, 1)
            pe.wait_ge(added3, BLOCKS * TPB)
            logits(0)
            pe.wait_ge(sw_lo, 2)
            route4(0, False)
            with pe.Fori(1, BATCH - 1) as b:
                route4(b, False)
            route4(BATCH - 1, True)

            def rows_of(s):
                pe.wait_ge(xs_ready, s + 1)
                if not (isinstance(s, int) and s == 0):
                    pe.wait_ge(xsT_ready, s)
                for k in range(KD):
                    last = pe.transpose(ps[:, 0, k * P:(k + 1) * P], xs[:, k:D:2], ident[:])
                last.then_inc(xs_turned, 1)

            def gate_up(s, i, it):
                pe.wait_ge(xsT_ready, s + 1)
                pe.wait_ge(e_loaded[i], 48 * it + (16 + 48))
                if not (isinstance(s, int) and s < 2):
                    pe.wait_ge(hE_ready, s - 1)
                for k in range(KD):
                    for x in range(4):
                        r = slice(32 * x, 32 * x + 32)
                        last = pe.matmul(ps[r, 1 + i % 2, 0:2 * I1], xsT[i % 2][:, k, r], eg[i][:, x, :, k, :],
                                         start=k == 0, stop=k == KD - 1, skip_group_check=True)
                last.then_inc(gu4_ready, 1)

            def experts(s, i, it, left):
                pe.wait_ge(hE_ready, s + 1)
                if not (isinstance(s, int) and s == 0):
                    pe.wait_ge(hET_ready, s)
                for k in range(2):
                    last = pe.transpose(ps[0:IH, 3, k * P:(k + 1) * P], hE[:, k:I1:2], ident[:])
                last.then_inc(hE_turned, 1)
                if left > 2:
                    rows_of(s + 2)
                if left > 1:
                    gate_up(s + 1, (i + 1) % 4, it if i < 3 else it + 1)
                pe.wait_ge(hET_ready, s + 1)
                if not (isinstance(s, int) and s < 2):
                    pe.wait_ge(ylo_ready, s - 1)
                for k in range(2):
                    for x in range(4):
                        r = slice(32 * x, 32 * x + 32)
                        last = pe.matmul(ps[r, 4 + i % 2, 0:D], hET[:, k, r], ed[i][:, x, k, :],
                                         start=k == 0, stop=k == 1, skip_group_check=True)
                last.then_inc(y_mm, 1)

            pe.wait_ge(added4, TILES)
            rows_of(0)
            rows_of(1)
            gate_up(0, 0, 0)
            for i in range(4):
                experts(i, i, 0, GROUPS - i)
            with pe.Fori(1, GROUPS // 4 - 1) as it:
                for i in range(4):
                    experts(it * 4 + i, i, it, 5)
            for i in range(4):
                experts(GROUPS - 4 + i, i, GROUPS // 4 - 1, 4 - i)
            pe.wait_ge(ylo_ready, GROUPS)
            pe.wait_ge(slots_added, BATCH)

            def combine(j):
                for i in range(2):
                    pe.wait_ge(pick_ready, 2 * j + (i + 1))
                    wait_past(pe, comb_added, 2 * j)
                    for s in range(GROUPS):
                        for h in range(2):
                            last = pe.matmul(ps[:, 6 + i, 0:D], pick[i][:, s, :], y4[h][:, s, :],
                                             start=s == 0 and h == 0, stop=s == GROUPS - 1 and h == 1)
                    last.then_inc(comb_ready, 1)

            combine(0)
            with pe.Fori(1, TILES // 2) as j:
                combine(j)


def rope_tables():
    inv = (1.0 / np.float32(ROPE_BASE) ** (np.arange(0, DH, 2, dtype=np.float32) / np.float32(DH))).astype(np.float32)
    angle = (np.arange(T, dtype=np.float32)[None, :] * inv[:, None]).astype(np.float32)
    angle = np.concatenate([angle, angle], 0)
    return np.stack([np.cos(angle), np.sin(angle)]).astype(np.float32)


_INS = [
    "L0_attn_x", "L0_attn_wq", "L0_attn_w_down", "L0_attn_w_up",
    "L0_attn_wo", "L0_ffn_W_router", "L0_ffn_W_gate", "L0_ffn_W_up",
    "L0_ffn_W_down", "L0_ffn_sA_gate", "L0_ffn_sB_gate", "L0_ffn_sA_up",
    "L0_ffn_sB_up", "L0_ffn_sA_down", "L0_ffn_sB_down", "L0_ffn_A_gate",
    "L0_ffn_B_gate", "L0_ffn_A_up", "L0_ffn_B_up", "L0_ffn_A_down",
    "L0_ffn_B_down", "L0_ffn_expert_bias", "L1_attn_Wq", "L1_attn_Wk",
    "L1_attn_Wv", "L1_attn_Wo", "L1_attn_bo", "L1_ffn_gate_w",
    "L1_ffn_w_gate", "L1_ffn_w_up", "L1_ffn_w_down", "L1_ffn_sw_gate",
    "L1_ffn_sw_up", "L1_ffn_sw_down",
]


def kernel(**inputs):
    import concourse.bacc as bacc
    from concourse.bass_utils import run_bass_kernel_spmd

    nc = bacc.Bacc("TRN2", target_bir_lowering=False, num_devices=1)
    arrays, io = {}, {}
    for name in _INS + ["rope"]:
        a = rope_tables() if name == "rope" else np.ascontiguousarray(inputs[name])
        arrays[f"in_{name}_dram"] = a
        io[name] = nc.dram_tensor(f"in_{name}_dram", a.shape, mybir.dt.from_np(a.dtype), kind="ExternalInput").ap()
    out = nc.dram_tensor("out_0_dram", (BATCH, T, D), F32, kind="ExternalOutput").ap()
    program(nc, io, out)
    return run_bass_kernel_spmd(nc, [arrays], core_ids=[0]).results[0]["out_0_dram"]
```
